# Optimizing a Trainium2 kernel written in Bass

```python
import numpy as np
import jax
import jax.numpy as jnp

def _softmax(x, axis=-1):
    return jax.nn.softmax(x, axis=axis)

def _gelu(x):
    return jax.nn.gelu(x, approximate=True)

def _silu(x):
    return jax.nn.silu(x)

def _sigmoid(x):
    return jax.nn.sigmoid(x)

def _layernorm(x, axis=-1, eps=1e-05):
    m = jnp.mean(x, axis=axis, keepdims=True)
    v = jnp.var(x, axis=axis, keepdims=True)
    return (x - m) / jnp.sqrt(v + eps)

def _scatter_add(tgt, idx, src, axis=0):
    return tgt.at[idx].add(src)

def _segment_sum(src, seg, n):
    return jax.ops.segment_sum(src, seg, n)
kernel_name = 'mk_early_fusion_embed_d1_tok_img768_r4_bfd53d'

def setup_inputs(seed: int=0):
    np.random.seed(seed)
    _w = jnp.asarray

    def _rec_inputs():
        import jax
        import jax.numpy as jnp
        _rk = jax.random.key(seed)
        x = -0.000137204 + 0.999937 * jax.random.normal(jax.random.fold_in(_rk, 1), (8, 3, 84, 84), jnp.float32)
        x_txt = jax.random.randint(jax.random.fold_in(_rk, 51), (8, 128), 0, 8000, jnp.int32)
        return (x, x_txt)
    x, x_txt = _rec_inputs()

    def _L0_tok_setup():
        import jax, jax.numpy as jnp
        import numpy as np
        B, C, H, W_IMG = (128, 3, 224, 224)
        N_PATCH, EMBED = (256, 192)
        GRID = 32
        key = jax.random.key(seed)
        k1, k2, k3, k4 = jax.random.split(key, 4)
        x = jax.random.normal(k1, (B, C, H, W_IMG), dtype=jnp.float32)
        curve = jax.random.randint(k2, (N_PATCH, 2), 0, GRID, dtype=jnp.int32)
        proj_w = jax.random.normal(k3, (EMBED, C), dtype=jnp.float32) * 0.02
        proj_b = jax.random.normal(k4, (EMBED,), dtype=jnp.float32) * 0.02
        return {'x': x, 'curve': curve, 'proj_w': proj_w, 'proj_b': proj_b}
    _L0_tok_all = _L0_tok_setup()
    _L0_tok_in = {k: v for k, v in _L0_tok_all.items() if k in ('curve', 'proj_w', 'proj_b')}
    del _L0_tok_all

    def _L0_txt_setup():
        import jax, jax.numpy as jnp
        import numpy as np
        N_QUBITS = 6
        N_LAYERS = 3
        DIM = 1 << N_QUBITS
        VOCAB = 8000
        EMBED = 192
        B, S = (16, 1024)

        def _cnot_perm(control, target):
            idx = np.arange(DIM)
            cbit = idx >> N_QUBITS - 1 - control & 1
            flipped = idx ^ 1 << N_QUBITS - 1 - target
            return np.where(cbit == 1, flipped, idx)
        _idx = np.arange(DIM)
        Z_SIGNS = np.stack([1.0 - 2.0 * (_idx >> N_QUBITS - 1 - q & 1) for q in range(N_QUBITS)], axis=1).astype(np.float32)

        def _apply_ry(state, theta, q):
            T = state.shape[0]
            left, right = (1 << q, 1 << N_QUBITS - 1 - q)
            s = state.reshape(T, left, 2, right)
            c = jnp.cos(theta * 0.5)[:, None, None]
            sn = jnp.sin(theta * 0.5)[:, None, None]
            a0, a1 = (s[:, :, 0, :], s[:, :, 1, :])
            out = jnp.stack([c * a0 - sn * a1, sn * a0 + c * a1], axis=2)
            return out.reshape(T, DIM)

        def _apply_rz(state, theta, q):
            T = state.shape[0]
            left, right = (1 << q, 1 << N_QUBITS - 1 - q)
            s = state.reshape(T, left, 2, right)
            ph = jnp.exp(1j * (theta * 0.5)).astype(state.dtype)[:, None, None]
            out = jnp.stack([jnp.conj(ph) * s[:, :, 0, :], ph * s[:, :, 1, :]], axis=2)
            return out.reshape(T, DIM)

        def _circuit_expvals(params):
            T = params.shape[0]
            state = jnp.zeros((T, DIM), dtype=jnp.complex64).at[:, 0].set(1.0)
            for layer in range(N_LAYERS):
                for q in range(N_QUBITS):
                    state = _apply_ry(state, params[:, layer, q, 0], q)
                    state = _apply_rz(state, params[:, layer, q, 1], q)
                if layer < N_LAYERS - 1:
                    for q in range(N_QUBITS - 1):
                        state = state[:, _cnot_perm(q, q + 1)]
                    if N_QUBITS > 2:
                        state = state[:, _cnot_perm(N_QUBITS - 1, 0)]
            probs = state.real ** 2 + state.imag ** 2
            return probs @ jnp.asarray(Z_SIGNS)
        key = jax.random.key(seed)
        k1, k2, k3, k4 = jax.random.split(key, 4)
        token_ids = jax.random.randint(k1, (B, S), 0, VOCAB)
        quantum_params = jax.random.normal(k2, (VOCAB, N_LAYERS, N_QUBITS, 2), dtype=jnp.float32) * 0.1
        post_w = jax.random.normal(k3, (EMBED, N_QUBITS), dtype=jnp.float32) / np.sqrt(N_QUBITS)
        post_b = jax.random.normal(k4, (EMBED,), dtype=jnp.float32) * 0.01
        return {'token_ids': token_ids, 'quantum_params': quantum_params, 'post_w': post_w, 'post_b': post_b}
    _L0_txt_all = _L0_txt_setup()
    _L0_txt_in = {k: v for k, v in _L0_txt_all.items() if k in ('quantum_params', 'post_w', 'post_b')}
    del _L0_txt_all

    def _L0_attn_setup():
        import jax, jax.numpy as jnp
        import numpy as np
        B, N, C = (32, 256, 192)
        H = 12
        E = C // H
        SCALE = E ** (-0.5)
        EPS = 1e-06
        key = jax.random.key(seed)
        k1, k2, k3 = jax.random.split(key, 3)
        x = jax.random.normal(k1, (B, N, C), dtype=jnp.float32)
        qkv_w = jax.random.normal(k2, (3 * C, C), dtype=jnp.float32) * C ** (-0.5)
        proj_w = jax.random.normal(k3, (C, C), dtype=jnp.float32) * C ** (-0.5)
        proj_b = jnp.zeros((C,), dtype=jnp.float32)
        return {'x': x, 'qkv_w': qkv_w, 'proj_w': proj_w, 'proj_b': proj_b}
    _L0_attn_all = _L0_attn_setup()
    _L0_attn_in = {k: v for k, v in _L0_attn_all.items() if k in ('qkv_w', 'proj_w', 'proj_b')}
    del _L0_attn_all

    def _L0_ffn_setup():
        import jax, jax.numpy as jnp
        import numpy as np
        D_MODEL = 192
        D_FF = 768
        NUM_EXPERTS = 8
        EXPERT_CAPACITY = 256
        key = jax.random.key(seed)
        k0, k1, k2, k3 = jax.random.split(key, 4)
        hidden_states = jax.random.normal(k0, (2, 256, D_MODEL), dtype=jnp.float32)
        router_w = jax.random.normal(k1, (D_MODEL, NUM_EXPERTS), dtype=jnp.float32) * D_MODEL ** (-0.5)
        wi = jax.random.normal(k2, (NUM_EXPERTS, D_MODEL, D_FF), dtype=jnp.float32) * D_MODEL ** (-0.5)
        wo = jax.random.normal(k3, (NUM_EXPERTS, D_FF, D_MODEL), dtype=jnp.float32) * D_FF ** (-0.5)
        return {'hidden_states': hidden_states, 'router_w': router_w, 'wi': wi, 'wo': wo}
    _L0_ffn_all = _L0_ffn_setup()
    _L0_ffn_in = {k: v for k, v in _L0_ffn_all.items() if k in ('router_w', 'wi', 'wo')}
    del _L0_ffn_all
    return {'x': x, 'x_txt': x_txt, 'L0_tok_curve': _L0_tok_in['curve'], 'L0_tok_proj_w': _L0_tok_in['proj_w'], 'L0_tok_proj_b': _L0_tok_in['proj_b'], 'L0_txt_quantum_params': _L0_txt_in['quantum_params'], 'L0_txt_post_w': _L0_txt_in['post_w'], 'L0_txt_post_b': _L0_txt_in['post_b'], 'L0_attn_qkv_w': _L0_attn_in['qkv_w'], 'L0_attn_proj_w': _L0_attn_in['proj_w'], 'L0_attn_proj_b': _L0_attn_in['proj_b'], 'L0_ffn_router_w': _L0_ffn_in['router_w'], 'L0_ffn_wi': _L0_ffn_in['wi'], 'L0_ffn_wo': _L0_ffn_in['wo']}

def reference(x, x_txt, L0_tok_curve, L0_tok_proj_w, L0_tok_proj_b, L0_txt_quantum_params, L0_txt_post_w, L0_txt_post_b, L0_attn_qkv_w, L0_attn_proj_w, L0_attn_proj_b, L0_ffn_router_w, L0_ffn_wi, L0_ffn_wo):
    import jax
    import jax.numpy as jnp

    def _L0_tok_ref(x, curve, proj_w, proj_b):
        import jax, jax.numpy as jnp
        import numpy as np
        B, C, H, W_IMG = (128, 3, 224, 224)
        N_PATCH, EMBED = (256, 192)
        GRID = 32
        gathered = x[:, :, curve[:, 1], curve[:, 0]]
        return jnp.einsum('bcn,ec->bne', gathered, proj_w) + proj_b

    def _L0_txt_ref(token_ids, quantum_params, post_w, post_b):
        import jax, jax.numpy as jnp
        import numpy as np
        N_QUBITS = 6
        N_LAYERS = 3
        DIM = 1 << N_QUBITS
        VOCAB = 8000
        EMBED = 192
        B, S = (16, 1024)

        def _cnot_perm(control, target):
            idx = np.arange(DIM)
            cbit = idx >> N_QUBITS - 1 - control & 1
            flipped = idx ^ 1 << N_QUBITS - 1 - target
            return np.where(cbit == 1, flipped, idx)
        _idx = np.arange(DIM)
        Z_SIGNS = np.stack([1.0 - 2.0 * (_idx >> N_QUBITS - 1 - q & 1) for q in range(N_QUBITS)], axis=1).astype(np.float32)

        def _apply_ry(state, theta, q):
            T = state.shape[0]
            left, right = (1 << q, 1 << N_QUBITS - 1 - q)
            s = state.reshape(T, left, 2, right)
            c = jnp.cos(theta * 0.5)[:, None, None]
            sn = jnp.sin(theta * 0.5)[:, None, None]
            a0, a1 = (s[:, :, 0, :], s[:, :, 1, :])
            out = jnp.stack([c * a0 - sn * a1, sn * a0 + c * a1], axis=2)
            return out.reshape(T, DIM)

        def _apply_rz(state, theta, q):
            T = state.shape[0]
            left, right = (1 << q, 1 << N_QUBITS - 1 - q)
            s = state.reshape(T, left, 2, right)
            ph = jnp.exp(1j * (theta * 0.5)).astype(state.dtype)[:, None, None]
            out = jnp.stack([jnp.conj(ph) * s[:, :, 0, :], ph * s[:, :, 1, :]], axis=2)
            return out.reshape(T, DIM)

        def _circuit_expvals(params):
            T = params.shape[0]
            state = jnp.zeros((T, DIM), dtype=jnp.complex64).at[:, 0].set(1.0)
            for layer in range(N_LAYERS):
                for q in range(N_QUBITS):
                    state = _apply_ry(state, params[:, layer, q, 0], q)
                    state = _apply_rz(state, params[:, layer, q, 1], q)
                if layer < N_LAYERS - 1:
                    for q in range(N_QUBITS - 1):
                        state = state[:, _cnot_perm(q, q + 1)]
                    if N_QUBITS > 2:
                        state = state[:, _cnot_perm(N_QUBITS - 1, 0)]
            probs = state.real ** 2 + state.imag ** 2
            return probs @ jnp.asarray(Z_SIGNS)
        b, s = token_ids.shape
        params = quantum_params[token_ids.reshape(-1)]
        ev = _circuit_expvals(params)
        emb = ev @ post_w.T + post_b
        return emb.reshape(b, s, -1)

    def _L0_attn_ref(x, qkv_w, proj_w, proj_b):
        import jax, jax.numpy as jnp
        import numpy as np
        B, N, C = (32, 256, 192)
        H = 12
        E = C // H
        SCALE = E ** (-0.5)
        EPS = 1e-06
        b, n, c = x.shape
        qkv = jnp.einsum('bnc,dc->bnd', x, qkv_w).reshape(b, n, 3, H, E)
        q = qkv[:, :, 0]
        k = qkv[:, :, 1]
        v = qkv[:, :, 2]
        q_ = jax.nn.relu(q) + SCALE
        k_ = jax.nn.relu(k) + SCALE
        kv = jnp.einsum('bnhe,bnhd->bhed', k_, v)
        k_sum = jnp.sum(k_, axis=1)
        z = 1.0 / (jnp.einsum('bnhe,bhe->bnh', q_, k_sum) + EPS)
        out = jnp.einsum('bnhe,bhed->bnhd', q_, kv) * z[..., None]
        out = out.reshape(b, n, c)
        return jnp.einsum('bnc,dc->bnd', out, proj_w) + proj_b

    def _L0_ffn_ref(hidden_states, router_w, wi, wo):
        import jax, jax.numpy as jnp
        import numpy as np
        D_MODEL = 192
        D_FF = 768
        NUM_EXPERTS = 8
        EXPERT_CAPACITY = 256
        B, S, d = hidden_states.shape
        E = router_w.shape[1]
        x = hidden_states.reshape(-1, d)
        logits = x.astype(jnp.float32) @ router_w.astype(jnp.float32)
        probs = jax.nn.softmax(logits, axis=-1).astype(x.dtype)
        p = jnp.max(probs, axis=-1)
        e_idx = jnp.argmax(probs, axis=-1)
        mask = jax.nn.one_hot(e_idx, E, dtype=x.dtype)
        token_priority = jnp.cumsum(mask[:, None, :], axis=-2)[:, 0, :]
        mask = mask * (token_priority <= EXPERT_CAPACITY).astype(x.dtype)
        combine = mask * p[:, None]

        def body(acc, ew):
            Wi_e, Wo_e, w_e = ew
            h = jax.nn.relu(x @ Wi_e) @ Wo_e
            return (acc + w_e[:, None] * h, None)
        out, _ = jax.lax.scan(body, jnp.zeros_like(x), (wi, wo, combine.T))
        return out.reshape(B, S, d)
    h = _L0_tok_ref(x, L0_tok_curve, L0_tok_proj_w, L0_tok_proj_b)
    h = jnp.concatenate([h, _L0_txt_ref(x_txt, L0_txt_quantum_params, L0_txt_post_w, L0_txt_post_b)], axis=1)
    h = h + _L0_attn_ref(_layernorm(h, axis=-1), L0_attn_qkv_w, L0_attn_proj_w, L0_attn_proj_b)
    h = h + _L0_ffn_ref(_layernorm(h, axis=-1), L0_ffn_router_w, L0_ffn_wi, L0_ffn_wo)
    return h

_drawn_inputs = setup_inputs


def setup_inputs(seed=0):
    import zlib

    import numpy as np

    out = dict(_drawn_inputs(seed))
    spreads = {'L0_attn_proj_b': (0.0, 0.1)}
    factors = {'L0_txt_quantum_params': 3.712, 'L0_txt_post_b': 6.15}
    for name, (base, spread) in spreads.items():
        noise = np.random.default_rng([zlib.crc32(name.encode()), seed]).standard_normal(out[name].shape)
        drawn = base * np.exp(spread * noise) if base else spread * noise
        out[name] = jnp.asarray(drawn.astype(out[name].dtype))
    for name, factor in factors.items():
        out[name] = (out[name] * factor).astype(out[name].dtype)
    return out
```

```python
from contextlib import ExitStack

import numpy as np

import concourse.bass as bass
from concourse import mybir

F32 = mybir.dt.float32
F32R = mybir.dt.float32r
BF16 = mybir.dt.bfloat16
I32 = mybir.dt.int32
U32 = mybir.dt.uint32
ALU = mybir.AluOpType
ACT = mybir.ActivationFunctionType
AX = mybir.AxisListType

P = 128
B = 8
NIMG, NTXT = 256, 128
NT = 3
TILES = B * NT
TOKENS = TILES * P
D = 192
G2 = 96
HD = 16
FF = 768
FC = FF // P
E = 8
BLK = 256
ST = BLK // P
NBLK = 20
LAST_MIN = (TILES * P // BLK - 1) // 2
NTILE = NBLK * ST
NQ = 6
LAYERS = 3
NPAR = LAYERS * NQ * 2
IMG = 84
CH = 3
VOCAB = 8000
NF = 11
NG = 12
ONE_IMG, ONE_TXT = 3, 10
RA = 3 * NG
RB0 = 64
RB = 3 * NF
RT = RB0 + RB
DL = D + E
C_D, C_RS, C_NM = D, D + E, D + E + 1
RW = D + E + 2
OUT_OF_BOUNDS = 1 << 20
LN_EPS = 1e-5
DEN_EPS = 1e-6
SCALE = HD ** -0.5
PI = 3.1415925
MAGIC = 1.5 * 2.0 ** 23
TWO_PI_HI = 6.28125
TWO_PI_LO = 2 * np.pi - 6.28125
W_COLS = FF + FF + FC * D

PAULI = {"X": (1, 0), "Z": (0, 1), "Y": (1, 1)}


def ap(base, offset, dims):
    return bass.AP(tensor=base.tensor, offset=base.offset + offset, ap=[list(base.ap[0])] + [list(d) for d in dims])


def x5_terms():
    terms = []
    for s1 in "XZY":
        for s5 in "XYZ":
            for s0 in "ZXY":
                (f0, g0), (f1, g1), (f5, g5) = PAULI[s0], PAULI[s1], PAULI[s5]
                x0, z0, x1, z1, w = f0 ^ f5, g1 ^ g5, f0 ^ f1 ^ f5, g0 ^ g1 ^ g5, g0 ^ g5
                ys = [s0, s1, s5].count("Y")
                xz = x0 * z0 + x1 * z1 + f1 * w + f5 * w
                sign = 1 if (ys - xz) % 4 == 0 else -1
                terms.append((x0 * 8 + z0 * 4 + x1 * 2 + z1, f1 * 4 + f5 * 2 + w, sign))
    return terms


def affine_runs(seq):
    out, i = [], 0
    while i < len(seq):
        best, dims = 1, [[1, 1]]
        j = i + 1
        if j < len(seq):
            step = seq[j] - seq[i]
            while j + 1 < len(seq) and seq[j + 1] - seq[j] == step:
                j += 1
            best, dims = j - i + 1, [[step, j - i + 1]]
        for a in (2, 3, 6, 9):
            for b in (2, 3, 4, 9):
                if a * b > best and i + a * b <= len(seq):
                    s1, s2 = seq[i + 1] - seq[i], seq[i + a] - seq[i]
                    if all(seq[i + q * a + r] == seq[i] + q * s2 + r * s1 for q in range(b) for r in range(a)):
                        best, dims = a * b, [[s2, b], [s1, a]]
        out.append((i, best, dims))
        i += best
    return out


class Chain:

    def __init__(self, engine, sem):
        self.engine, self.sem, self.n = engine, sem, 0

    def step(self, ins):
        self.n += 1
        ins.then_inc(self.sem, 1)
        return self.n

    def wait(self, n=None):
        self.engine.wait_ge(self.sem, self.n if n is None else n)

    def link(self, ins):
        self.step(ins)
        self.wait()


def fusion_kernel(nc, pixels, curve, txt_ids, qparams, wf, qkv_wT, proj_w, proj_wT, proj_b, router_w, wi, wo, out):
    out_rows = out.rearrange("b n d -> (b n) d")
    rows = nc.dram_tensor("rows", (TOKENS, RW), F32, kind="Internal").ap()
    ctx = ExitStack()
    with ctx:
        def sb(name, shape, dt=F32):
            return ctx.enter_context(nc.sbuf_tensor(name, shape, dt))

        def sem(name):
            return ctx.enter_context(nc.semaphore(name))

        bank = [ctx.enter_context(nc.psum_tensor(f"bank{i}", [P, 512], F32)) for i in range(8)]

        ident = sb("ident", [P, P])
        tri = sb("tri", [P, P], BF16)
        ones_bf = sb("ones_bf", [P, P], BF16)
        ones_mean = sb("ones_mean", [G2, P])
        head_mask = sb("head_mask", [G2, G2])
        lo_rows = sb("lo_rows", [P, 2])
        hi_coef = sb("hi_coef", [P, 2])
        ksum_sel = sb("ksum_sel", [NG, G2])
        const_row = sb("const_row", [1, 3 * D])
        one_hot_row = sb("one_hot_row", [1, RA])
        half_pi = sb("half_pi", [P, 1])
        eps_tile = sb("eps_tile", [P, 1])
        expert_key = sb("expert_key", [P, NT, E])
        term_sign = sb("term_sign", [P, 27])
        iota_lane = sb("iota_lane", [P, P])
        iota_p = sb("iota_p", [P, 1])
        iota_t = sb("iota_t", [P, TILES])
        iota_blk = sb("iota_blk", [1, NBLK, E])

        wfs = sb("wfs", [G2, 2, NF])
        wf_c = sb("wf_c", [G2, 2, 3, NG])
        wf_b = sb("wf_b", [G2, 2, 3, NF])
        wq_in = sb("wq_in", [G2, 2, 3 * D])
        pw = sb("pw", [G2, 2, D])
        pr = sb("pr", [G2, 2, DL])
        ir = sb("ir", [G2, 2, DL])
        pb = sb("pb", [G2, 2])
        wa = sb("wa", [RA, 2 * D], F32R)
        wa_lo = sb("wa_lo", [RA, 2 * D])
        vw = sb("vw", [NG, D])
        wb = sb("wb", [RT, DL], F32R)
        wb_lo = sb("wb_lo", [RT, DL])
        outer = sb("outer", [G2, 2, 16 + 49])
        quad = sb("quad", [P, 16 + 49])

        ids = sb("ids", [P, B], I32)
        crv = sb("crv", [P, 2, 2], I32)
        pix_id = sb("pix_id", [P, 2], I32)
        prm = sb("prm", [P, B, NPAR])
        kk = sb("kk", [P, B, NPAR])
        sn = sb("sn", [P, B, NPAR])
        cs = sb("cs", [P, B, NPAR])
        fz = sb("fz", [P, B, NQ, 4])
        fn = sb("fn", [P, B, NQ, 4])
        ns = sb("ns", [P, B, NQ])
        tr = sb("tr", [P, B, NQ, 8])
        base = sb("base", [P, B, 12])
        vs = sb("vs", [P, 4, B, 24])
        tmp = [sb(f"tmp{i}", [P, B, 24]) for i in range(2)]
        zs = sb("zs", [P, B, 4])
        ezt = sb("ezt", [P, 4, B, 4])
        w5 = sb("w5", [P, B, 12])
        ez = sb("ez", [P, NQ, B])
        co = sb("co", [P, B, NQ, 3])
        gx = sb("gx", [P, B, 5, 9])
        cx = sb("cx", [P, B, 5, 9])
        zp = sb("zp", [P, B, NQ])
        qv = sb("qv", [P, B, NQ])
        rv = sb("rv", [P, B, NQ])
        xt = sb("xt", [P, B, 8])
        z345 = sb("z345", [P, B, 2])
        p01 = sb("p01", [P, B, 16])
        d25 = sb("d25", [P, B, 8])
        gp = sb("gp", [P, B, 27])
        gd = sb("gd", [P, B, 27])
        c27 = sb("c27", [P, B, 27])
        ex = sb("ex", [P, B, NQ])

        pixg = sb("pixg", [P, 2, B * CH])
        gt = sb("gt", [P, B, NT, NF])
        gs = sb("gs", [P, B, NT, NG])
        sa = sb("sa", [P, B, NT, RT])
        vq = sb("vq", [P, B * 49])
        var = sb("var", [P, B, NT])
        rstd = sb("rstd", [P, B, NT])
        newt = sb("newt", [P, B, NT])

        gtt = [sb(f"gtt{i}", [RT, NT * P], F32R) for i in range(2)]
        qt = [sb(f"qt{i}", [G2 + 1, 2, NT * P]) for i in range(2)]
        kt = [sb(f"kt{i}", [P, NT, D]) for i in range(2)]
        kg = [sb(f"kg{i}", [NG, D]) for i in range(2)]
        kvm = [sb(f"kvm{i}", [G2, 2, G2]) for i in range(2)]
        dm = [sb(f"dm{i}", [G2 + 1, 2, NQ]) for i in range(2)]
        mb = [sb(f"mb{i}", [G2, 2, DL]) for i in range(2)]
        zr = [sb(f"zr{i}", [P, NT, 2, NQ]) for i in range(2)]
        zx = sb("zx", [P, NT, D])
        zt = [sb(f"zt{i}", [G2, 2, NT * P]) for i in range(2)]
        row = [sb(f"row{i}", [P, NT, RW]) for i in range(2)]
        st6 = sb("st6", [P, NT, 6])
        mv = sb("mv", [P, NT, 2])
        std = [sb(f"std{i}", [P, NT]) for i in range(2)]
        mx = sb("mx", [P, NT])
        ohf = sb("ohf", [P, NT, E])
        oh = sb("oh", [P, NT, E], BF16)
        before = sb("before", [P, NT + 1, E], BF16)
        key = sb("key", [P, NT])
        rank = sb("rank", [P, NT])
        cnt = sb("cnt", [P, E])
        cnt_i = sb("cnt_i", [P, E], I32)
        blk_end = sb("blk_end", [P, E])
        first_tile = sb("first_tile", [P, E])
        r_i = sb("r_i", [P, NT], I32)
        lo_i = sb("lo_i", [P, NT], I32)
        hi_i = sb("hi_i", [P, NT], I32)
        lo_f = sb("lo_f", [P, TILES])
        tile_f = sb("tile_f", [P, TILES])
        lane_f = sb("lane_f", [P, NTILE])
        fill_f = sb("fill_f", [P, NTILE])
        cnt_j = sb("cnt_j", [P, E], I32)
        ones_e = sb("ones_e", [P, E])
        hi_f = sb("hi_f", [P, TILES])
        oh_all = sb("oh_all", [P, TILES, E], BF16)
        oh_lo = sb("oh_lo", [P, TILES, P], BF16)
        oh_hi = sb("oh_hi", [P, TILES, 3, NTILE], BF16)
        tl = sb("tl", [P, TILES, E])
        gidf = sb("gidf", [P, NTILE])
        sidf = sb("sidf", [P, NTILE])
        gid = sb("gid", [P, NTILE], I32)
        sid = sb("sid", [P, NTILE], I32)
        be = sb("be", [1, NBLK, E])
        bef = sb("bef", [1, NBLK])
        blk_expert = sb("blk_expert", [1, NBLK], I32)
        n_last = sb("n_last", [1, 1], I32)
        last_pair = sb("last_pair", [1, 1], I32)
        raw = [sb(f"raw{i}", [P, W_COLS]) for i in range(2)]
        wh = [sb(f"wh{i}", [P, W_COLS], F32R) for i in range(2)]
        wl = [sb(f"wl{i}", [P, W_COLS], F32R) for i in range(2)]
        gr = [sb(f"gr{i}", [P, ST], I32) for i in range(2)]
        sr = [sb(f"sr{i}", [P, ST], I32) for i in range(2)]
        hs = [sb(f"hs{i}", [P, ST, RW]) for i in range(2)]
        xn = [sb(f"xn{i}", [P, ST, 256]) for i in range(2)]
        xh = [sb(f"xh{i}", [P, 2 * BLK], F32R) for i in range(2)]
        xl = [sb(f"xl{i}", [P, BLK], F32R) for i in range(2)]
        hh = [sb(f"hh{i}", [P, FC, BLK], F32R) for i in range(2)]
        hl = [sb(f"hl{i}", [P, FC, BLK], F32R) for i in range(2)]
        ed = [sb(f"ed{i}", [P, ST, E]) for i in range(2)]
        sume = [sb(f"sume{i}", [P, ST]) for i in range(2)]
        prob = [sb(f"prob{i}", [P, ST]) for i in range(2)]
        flat = sa[:, :, :, :].rearrange("p b t j -> p (b t j)")
        res, yr = ([flat[:, (2 * k + i) * ST * D:(2 * k + i + 1) * ST * D].rearrange("p (s d) -> p s d", s=ST)
                    for i in range(2)] for k in range(2))

        s_small = sem("s_small")
        s_wload = sem("s_wload")
        s_pixid = sem("s_pixid")
        s_pix = [sem(f"s_pix{n}") for n in range(2)]
        s_prm = sem("s_prm")
        s_const = sem("s_const")
        s_constv = sem("s_constv")
        s_pool = sem("s_pool")
        s_dve = sem("s_dve")
        s_act = sem("s_act")
        s_red = sem("s_red")
        s_abs = sem("s_abs")
        s_trig = sem("s_trig")
        s_bloch = sem("s_bloch")
        s_ex = sem("s_ex")
        s_wmean = sem("s_wmean")
        s_wcent = sem("s_wcent")
        s_wprod = sem("s_wprod")
        s_wready = sem("s_wready")
        s_var = sem("s_var")
        s_sd = sem("s_sd")
        s_sa = sem("s_sa")
        s_t = sem("s_t")
        s_gtt = sem("s_gtt")
        s_q = sem("s_q")
        s_qt = sem("s_qt")
        s_k = sem("s_k")
        s_kt = sem("s_kt")
        s_kg = sem("s_kg")
        s_kgc = sem("s_kgc")
        s_kv = sem("s_kv")
        s_kvc = sem("s_kvc")
        s_m = sem("s_m")
        s_mc = sem("s_mc")
        s_den = sem("s_den")
        s_z = sem("s_z")
        s_zx = sem("s_zx")
        s_zt = sem("s_zt")
        s_qz = sem("s_qz")
        s_h = sem("s_h")
        s_bn = sem("s_bn")
        s_hc = sem("s_hc")
        s_v2 = sem("s_v2")
        s_sd2 = sem("s_sd2")
        s_oh = sem("s_oh")
        s_rk = sem("s_rk")
        s_slot = sem("s_slot")
        s_lo = sem("s_lo")
        s_ohlo = sem("s_ohlo")
        s_rows = [sem(f"s_rows{i}") for i in range(2)]
        s_cnt = sem("s_cnt")
        s_ohhi = sem("s_ohhi")
        s_inv = sem("s_inv")
        s_tab = sem("s_tab")
        s_raw = [sem(f"s_raw{i}") for i in range(2)]
        s_wh = sem("s_wh")
        s_wl = sem("s_wl")
        s_gidx = sem("s_gidx")
        s_issue = sem("s_issue")
        s_sidx = sem("s_sidx")
        s_hs = [sem(f"s_hs{i}") for i in range(2)]
        s_res = sem("s_res")
        s_xn = sem("s_xn")
        s_x = sem("s_x")
        s_xh = sem("s_xh")
        s_xl = sem("s_xl")
        s_u = sem("s_u")
        s_hh = sem("s_hh")
        s_hl = sem("s_hl")
        s_y = sem("s_y")
        s_exp = sem("s_exp")
        s_pr = sem("s_pr")
        s_yr = sem("s_yr")
        s_fin = [sem(f"s_fin{i}") for i in range(2)]

        def pairs(engine, body, last):
            for r in range(2):
                body(0, r, first=True)
            with engine.Fori(1, last) as j:
                for r in range(2):
                    body(j, r)
            for r in range(2):
                body(last, r, tail=True)

        block_ = ctx.enter_context(nc.Block())

        K0, K1, MM, Q0, Q1, D0, D1, HB = bank
        HT = (HB, D0, D1)
        PP, YY, UU = bank[0], bank[7], bank[1:7]

        @block_.sync
        def _(sp):
            sp.dma_start(crv[:, :, :], curve.rearrange("(n p) c -> p n c", p=P)).then_inc(s_small, 16)
            sp.dma_start(ids[:, :], txt_ids).then_inc(s_small, 16)
            sp.dma_start(wfs[:, :, :], wf.rearrange("(g p) j -> p g j", g=2)).then_inc(s_wload, 16)
            sp.dma_start(ir[:, :, D:DL], router_w.rearrange("(g p) e -> p g e", g=2)).then_inc(s_wload, 16)
            sp.dma_start(pb[:, :], proj_b).then_inc(s_wload, 16)
            sp.dma_start(wq_in[:, :, :], qkv_wT.rearrange("(g p) d -> p g d", g=2)).then_inc(s_wload, 16)
            sp.dma_start(pw[:, :, :], proj_w.rearrange("(g p) d -> p g d", g=2)).then_inc(s_wload, 16)
            sp.dma_start(pr[:, :, 0:D], proj_wT.rearrange("(g p) d -> p g d", g=2)).then_inc(s_wload, 16)

            def load_weights(e, r):
                sp.dma_start(raw[r][:, 0:FF], wi[bass.ds(e, 1), 0:P, :]).then_inc(s_raw[r], 16)
                sp.dma_start(raw[r][0:64, FF:2 * FF], wi[bass.ds(e, 1), P:D, :]).then_inc(s_raw[r], 16)
                sp.dma_start(raw[r][64:P, FF:2 * FF], wi[bass.ds(e, 1), P:D, :]).then_inc(s_raw[r], 16)
                sp.dma_start(raw[r][:, 2 * FF:W_COLS].rearrange("p (c d) -> p c d", c=FC),
                             wo[bass.ds(e, 1), :, :].rearrange("o (c p) d -> (o p) c d", p=P))\
                  .then_inc(s_raw[r], 16)

            for b in range(B):
                sp.wait_ge(s_slot, b + 1)
                sp.dma_start(rows[b * NT * P:(b + 1) * NT * P, :].rearrange("(t p) d -> p t d", p=P),
                             row[b % 2][:, :, :]).then_inc(s_rows[b % 2], 16)

            def block(j, r, first=False):
                if not first:
                    sp.wait_ge(s_wh, 2 * (2 * j + r) - 2)
                    sp.wait_ge(s_wl, 2 * (2 * j + r) - 2)
                e = sp.value_load(blk_expert[0:1, bass.ds(2 * j + r, 1)], min_val=0, max_val=E - 1)
                load_weights(e, r)

            sp.wait_ge(s_tab, 1)
            end = sp.value_load(last_pair[0:1, 0:1], min_val=0, max_val=NBLK // 2 - 1 - LAST_MIN) + LAST_MIN
            for r in range(2):
                block(0, r, True)
            with sp.Fori(1, end + 1) as j:
                for r in range(2):
                    block(j, r)

        @block_.gpsimd
        def _(pool):
            ch = Chain(pool, s_pool)
            g = nc.gpsimd
            pool.wait_ge(s_small, 32)
            for b in range(B):
                g.indirect_dma_start(out=prm[:, b, :], out_offset=None, in_=qparams,
                                     in_offset=bass.IndirectOffsetOnAxis(ap=ids[:, b:b + 1].bitcast(U32), axis=0),
                                     bounds_check=VOCAB - 1, oob_is_err=False).then_inc(s_prm, 16)
            pool.wait_ge(s_pixid, 1)
            for n in range(2):
                g.indirect_dma_start(out=pixg[:, n, :], out_offset=None, in_=pixels,
                                     in_offset=bass.IndirectOffsetOnAxis(ap=pix_id[:, n:n + 1].bitcast(U32), axis=0),
                                     bounds_check=IMG * IMG - 1, oob_is_err=False).then_inc(s_pix[n], 16)
            g.memset(ones_mean[:, :], 1.0 / D).then_inc(s_const, 1)
            ch.step(g.memset(ident[:, :], 0.0))
            ch.step(g.memset(head_mask[:, :], 1.0))
            ch.step(g.memset(lo_rows[:, :], 1.0))
            ch.step(g.memset(ksum_sel[:, :], 1.0))
            ch.step(g.memset(tri[:, :], 1.0))
            ch.step(g.memset(one_hot_row[:, :], 0.0))
            ch.step(g.memset(const_row[:, :], 0.0))
            ch.step(g.memset(ir[:, :, 0:D], 0.0))
            ch.wait()
            g.memset(const_row[:, 0:2 * D], SCALE).then_inc(s_const, 1)
            g.memset(ap(one_hot_row[:, :], NF, [[NG, 3]]), 1.0).then_inc(s_const, 1)
            g.affine_select(out=ident[:, :], in_=ident[:, :], compare_op=ALU.not_equal, fill=1.0, base=0,
                            pattern=[[-1, P]], channel_multiplier=1).then_inc(s_const, 1)
            g.affine_select(out=ir[:, :, 0:D], in_=ir[:, :, 0:D], compare_op=ALU.not_equal, fill=1.0, base=0,
                            pattern=[[G2, 2], [-1, D]], channel_multiplier=1).then_inc(s_const, 1)
            g.affine_select(out=tri[:, :], in_=tri[:, :], compare_op=ALU.is_ge, fill=0.0, base=0,
                            pattern=[[1, P]], channel_multiplier=-1).then_inc(s_const, 1)
            hm = head_mask[:, :].rearrange("p (h d) -> p h d", d=HD)
            ch.link(g.affine_select(out=hm, in_=hm, compare_op=ALU.is_ge, fill=0.0, base=0,
                                    pattern=[[-HD, NQ], [0, HD]], channel_multiplier=1))
            g.affine_select(out=hm, in_=hm, compare_op=ALU.is_ge, fill=0.0, base=HD - 1,
                            pattern=[[HD, NQ], [0, HD]], channel_multiplier=-1).then_inc(s_const, 1)
            g.affine_select(out=ksum_sel[:, :], in_=ksum_sel[:, :], compare_op=ALU.is_ge, fill=0.0, base=-NF,
                            pattern=[[0, G2]], channel_multiplier=1).then_inc(s_const, 1)
            for j, first in enumerate((2 * NG, RB0 + 2 * NF)):
                g.affine_select(out=lo_rows[:, j:j + 1], in_=lo_rows[:, j:j + 1], compare_op=ALU.is_ge, fill=0.0,
                                base=-first, pattern=[[0, 1]], channel_multiplier=1).then_inc(s_const, 1)
            g.iota(iota_lane[:, :], pattern=[[1, P]], base=0, channel_multiplier=0,
                   allow_small_or_imprecise_dtypes=True).then_inc(s_const, 1)
            g.iota(iota_p[:, :], pattern=[[0, 1]], base=0, channel_multiplier=1,
                   allow_small_or_imprecise_dtypes=True).then_inc(s_const, 1)
            g.iota(iota_t[:, :], pattern=[[1, TILES]], base=0, channel_multiplier=0,
                   allow_small_or_imprecise_dtypes=True).then_inc(s_const, 1)
            g.iota(iota_blk[:, :, :], pattern=[[1, NBLK], [0, E]], base=0, channel_multiplier=0,
                   allow_small_or_imprecise_dtypes=True).then_inc(s_const, 1)
            g.iota(expert_key[:, :, :], pattern=[[0, NT], [-1, E]], base=E, channel_multiplier=0,
                   allow_small_or_imprecise_dtypes=True).then_inc(s_const, 1)

            pool.wait_ge(s_trig, 2)
            pool.wait_ge(s_bloch, 1)

            def th(a, layer):
                return a[:, :, :].rearrange("p t (l q r) -> p t l q r", l=LAYERS, r=2)[:, :, layer, :, 0]

            def ph(a, layer):
                return a[:, :, :].rearrange("p t (l q r) -> p t l q r", l=LAYERS, r=2)[:, :, layer, :, 1]

            def mul(o, a, b_):
                return g.tensor_tensor(o, a, b_, ALU.mult)

            def F(j, c, n=1):
                v = fz[:, :, j:j + n, c]
                return v

            def N(j, n=1):
                return fn[:, :, j:j + n, 3]

            ch.step(mul(co[:, :, :, 0], ph(cs, 1), th(cs, 1)))
            ch.step(mul(co[:, :, :, 1], ph(cs, 1), th(sn, 1)))
            ch.step(g.tensor_scalar(co[:, :, :, 2], ph(sn, 1), -1.0, None, ALU.mult))
            ch.step(g.tensor_copy(zp[:, :, 1:2], F(0, 1)))
            ch.step(g.tensor_copy(qv[:, :, 1:4], F(3, 2, 3)))
            ch.step(mul(qv[:, :, 4:5], F(0, 2), F(1, 2)))
            ch.step(mul(xt[:, :, 0:1], N(0), F(1, 3)))
            ch.step(mul(z345[:, :, 0:1], F(3, 1), F(4, 1)))
            ch.step(mul(xt[:, :, 1:2], F(2, 1), F(3, 1)))
            for i in range(2, 5):
                ch.wait()
                ch.step(mul(zp[:, :, i:i + 1], zp[:, :, i - 1:i], F(i - 1, 1)))
            ch.step(mul(z345[:, :, 1:2], z345[:, :, 0:1], F(5, 1)))
            ch.step(mul(rv[:, :, 4:5], xt[:, :, 0:1], xt[:, :, 1:2]))
            ch.wait()
            ch.step(mul(rv[:, :, 1:4], zp[:, :, 1:4], F(3, 2, 3)))
            X4, Y4, Z4, N4 = F(1, 2, 4), F(1, 3, 4), F(1, 1, 4), N(1, 4)
            X5, Y5, Z5, N5 = F(2, 2, 4), F(2, 3, 4), F(2, 1, 4), N(2, 4)
            ch.step(mul(gx[:, :, 1:5, 0], X4, qv[:, :, 1:5]))
            ch.step(mul(gx[:, :, 1:5, 1], zp[:, :, 1:5], N4))
            ch.step(mul(gx[:, :, 1:5, 2], Y4, Z5))
            ch.step(mul(gx[:, :, 1:5, 3], Z4, X5))
            ch.step(g.tensor_copy(gx[:, :, 1:5, 4], Z5))
            ch.step(mul(gx[:, :, 1:5, 5], Y5, qv[:, :, 1:5]))
            ch.step(mul(gx[:, :, 1:5, 7], X4, Y5))
            ch.wait()
            ch.step(mul(gx[:, :, 1:5, 1], gx[:, :, 1:5, 1], Y5))
            ch.step(mul(gx[:, :, 1:5, 2], gx[:, :, 1:5, 2], rv[:, :, 1:5]))
            ch.step(mul(gx[:, :, 1:5, 3], gx[:, :, 1:5, 3], rv[:, :, 1:5]))
            ch.step(mul(gx[:, :, 1:5, 6], Y4, rv[:, :, 1:5]))
            ch.step(mul(gx[:, :, 1:5, 8], gx[:, :, 1:5, 0], Z5))
            ch.wait()
            ch.step(g.tensor_scalar(gx[:, :, 1:5, 8], gx[:, :, 1:5, 8], -1.0, None, ALU.mult))
            zz = z345[:, :, 1:2]
            ch.step(mul(xt[:, :, 2:3], F(2, 1), zz))
            ch.step(mul(xt[:, :, 3:4], F(2, 3), zz))
            ch.step(mul(xt[:, :, 4:5], F(0, 3), F(1, 1)))
            ch.step(mul(xt[:, :, 5:6], F(0, 1), F(1, 2)))
            ch.step(mul(xt[:, :, 6:7], F(0, 2), F(1, 1)))
            ch.step(mul(xt[:, :, 7:8], F(0, 3), F(1, 2)))
            ch.wait()
            ch.step(mul(gx[:, :, 0:1, 0], F(0, 2), F(2, 2)))
            ch.step(mul(gx[:, :, 0:1, 1], N(0), F(1, 3)))
            ch.step(mul(gx[:, :, 0:1, 2], xt[:, :, 4:5], F(2, 2)))
            ch.step(mul(gx[:, :, 0:1, 3], N(1), xt[:, :, 3:4]))
            ch.step(mul(gx[:, :, 0:1, 4], F(0, 1), xt[:, :, 2:3]))
            ch.step(mul(gx[:, :, 0:1, 5], xt[:, :, 5:6], xt[:, :, 3:4]))
            ch.step(mul(gx[:, :, 0:1, 6], xt[:, :, 6:7], xt[:, :, 3:4]))
            ch.step(mul(gx[:, :, 0:1, 7], xt[:, :, 7:8], xt[:, :, 2:3]))
            ch.step(mul(gx[:, :, 0:1, 8], F(0, 3), xt[:, :, 3:4]))
            for s in range(3):
                ch.step(mul(cx[:, :, :, 3 * s:3 * s + 3],
                            co[:, :, 0:5, s:s + 1].to_broadcast([P, B, 5, 3]), co[:, :, 1:6, :]))
            ch.wait()
            g.tensor_tensor(gx[:, :, :, :], gx[:, :, :, :], cx[:, :, :, :], ALU.mult).then_inc(s_ex, 1)
            for c in range(4):
                ch.step(mul(p01[:, :, 4 * c:4 * c + 4], fz[:, :, 0, c:c + 1].to_broadcast([P, B, 4]), fz[:, :, 1, :]))
            for f1 in range(2):
                ch.step(mul(d25[:, :, 4 * f1:4 * f1 + 4].rearrange("p t (f w) -> p t f w", w=2),
                            ap(fz[:, :, 2, 2 * f1:2 * f1 + 2], 0, [[4 * NQ, B], [0, 2], [1, 2]]),
                            fz[:, :, 5, :].rearrange("p t (f w) -> p t f w", w=2)))
            ch.wait()
            ch.link(mul(ap(d25[:, :, :], 1, [[8, B], [2, 4]]), ap(d25[:, :, :], 1, [[8, B], [2, 4]]),
                        z345[:, :, 0:1].to_broadcast([P, B, 4])))
            terms = x5_terms()
            for i5, c5 in enumerate((0, 2, 1)):
                ch.step(mul(ap(c27[:, :, :], 3 * i5, [[27, B], [9, 3], [1, 1]]),
                            ap(co[:, :, :, :], 3, [[18, B], [1, 3], [1, 1]]),
                            ap(co[:, :, :, :], 15 + c5, [[18, B], [0, 3], [1, 1]])))
            ch.wait()
            for i0, c0 in ((2, 2), (1, 0), (0, 1)):
                ch.step(mul(ap(c27[:, :, :], i0, [[27, B], [3, 9]]), ap(c27[:, :, :], 0, [[27, B], [3, 9]]),
                            ap(co[:, :, :, :], c0, [[18, B], [0, 9]])))
                ch.wait()
            for dst, src, width, which in ((gp, p01, 16, 0), (gd, d25, 8, 1)):
                seq = [t[which] for t in terms]
                for i, n, dims in affine_runs(seq):
                    o = [[27, B]] + ([[dims[1][1], dims[0][1]], [1, dims[1][1]]] if len(dims) == 2 else [[1, n]])
                    ch.step(g.tensor_copy(ap(dst[:, :, :], i, o), ap(src[:, :, :], seq[i], [[width, B]] + dims)))
            ch.link(mul(c27[:, :, :], c27[:, :, :], ap(term_sign[:, :], 0, [[0, B], [1, 27]])))
            ch.link(mul(gp[:, :, :], gp[:, :, :], gd[:, :, :]))
            mul(gp[:, :, :], gp[:, :, :], c27[:, :, :]).then_inc(s_ex, 1)

            for b in range(B):
                pool.wait_ge(s_lo, b + 1)
                for t in range(NT):
                    n = b * NT + t
                    g.tensor_scalar(oh_lo[:, n, :], iota_lane[:, :], lo_f[:, n:n + 1], None, ALU.is_equal)\
                     .then_inc(s_ohlo, 1)

            def gather(j, r, first=False):
                b = 2 * j + r
                if not first:
                    pool.wait_ge(s_xn, 4 * b - 4)
                    pool.wait_ge(s_exp, 2 * b - 2)
                    pool.wait_ge(s_res, b - 1)
                g.tensor_copy(gr[r][:, :], gid[:, bass.ds(ST * b, ST)]).then_inc(s_gidx, 1)
                pool.wait_ge(s_gidx, b + 1)
                pool.sem_inc(s_issue, 1)
                for s_ in range(ST):
                    g.indirect_dma_start(out=hs[r][:, s_, :], out_offset=None, in_=rows,
                                         in_offset=bass.IndirectOffsetOnAxis(
                                             ap=gr[r][:, s_:s_ + 1].bitcast(U32), axis=0),
                                         bounds_check=TOKENS - 1, oob_is_err=False).then_inc(s_hs[r], 16)

            def scatter(j, r, first=False):
                b = 2 * j + r
                if not first:
                    pool.wait_ge(s_fin[r], 16 * ST * j)
                g.tensor_copy(sr[r][:, :], sid[:, bass.ds(ST * b, ST)]).then_inc(s_sidx, 1)
                pool.wait_ge(s_sidx, b + 1)
                pool.wait_ge(s_yr, ST * b + ST)
                pool.sem_inc(s_issue, 1)
                for s_ in range(ST):
                    g.indirect_dma_start(out=out_rows,
                                         out_offset=bass.IndirectOffsetOnAxis(
                                             ap=sr[r][:, s_:s_ + 1].bitcast(U32), axis=0),
                                         in_=yr[r][:, s_, :], in_offset=None, bounds_check=TOKENS - 1,
                                         oob_is_err=False).then_inc(s_fin[r], 16)

            def block(j, r, first=False, tail=False):
                if not tail:
                    gather(j + 1, r)
                scatter(j, r, first)

            pool.wait_ge(s_tab, 1)
            for r in range(2):
                pool.wait_ge(s_rows[r], 16 * B // 2)
            last = pool.value_load(last_pair[0:1, 0:1], min_val=0, max_val=NBLK // 2 - 1 - LAST_MIN) + LAST_MIN
            gather(0, 0, True)
            gather(0, 1, True)
            pairs(pool, block, last)
            for r in range(2):
                pool.wait_ge(s_fin[r], 16 * ST * (last + 1))

        @block_.scalar
        def _(act):
            a = nc.scalar
            ch = Chain(act, s_act)
            act.wait_ge(s_constv, 2)
            act.wait_ge(s_red, 1)
            ch.step(a.activation(kk[:, :, :], prm[:, :, :], ACT.Abs))
            a.activation(sn[:, :, :], prm[:, :, :], ACT.Sin).then_inc(s_trig, 1)
            ch.wait()
            a.activation(cs[:, :, :], kk[:, :, :], ACT.Sin, bias=half_pi[:, :], scale=-1.0).then_inc(s_trig, 1)
            act.wait_ge(s_var, 1)
            a.activation(rstd[:, :, :], var[:, :, :], ACT.Sqrt, bias=eps_tile[:, :]).then_inc(s_sd, 1)

            def front(b):
                r = b % 2
                act.wait_ge(s_t, b + 1)
                if b >= 2:
                    act.wait_ge(s_h, NT * (b - 1))
                a.activation(gtt[r][:, :], K0[0:RT, 0:NT * P], ACT.Copy).then_inc(s_gtt, 1)

            def h2(b):
                r = b % 2
                for t in range(NT):
                    n = b * NT + t
                    act.wait_ge(s_h, n + 1)
                    if t == 0 and b >= 2:
                        act.wait_ge(s_rows[r], 16 * (b // 2))
                    a.activation(row[r][:, t, 0:DL], HT[t][:, 0:DL], ACT.Copy).then_inc(s_hc, 1)
                act.wait_ge(s_v2, b + 1)
                a.activation(std[r][:, :], mv[:, :, 1], ACT.Sqrt, bias=eps_tile[:, :]).then_inc(s_sd2, 1)

            def m_copy(b):
                r = b % 2
                act.wait_ge(s_m, b + 1)
                a.activation(mb[r][:, :, :], MM[0:G2, 0:2 * DL].rearrange("p (g d) -> p g d", g=2), ACT.Copy)\
                 .then_inc(s_mc, 1)

            front(0)
            for b in range(B):
                if b + 1 < B:
                    front(b + 1)
                m_copy(b)
                act.wait_ge(s_z, b + 1)
                if b:
                    act.wait_ge(s_zt, 2 * b)
                a.activation(zx[:, :, :].rearrange("p t (k j) -> p (t k) j", j=HD),
                             ap(zr[b % 2][:, :, :, :], 0, [[1, NT * 2 * NQ], [0, HD]]), ACT.Copy).then_inc(s_zx, 1)
                h2(b)

            def prepare(j, r, b, opening=False):
                act.wait_ge(s_hs[r], 16 * ST * (j + 1))
                if not opening:
                    act.wait_ge(s_exp, ST * b - ST)
                    act.wait_ge(s_pr, b - 1)
                    act.wait_ge(s_yr, ST * b - ST)
                for s_ in range(ST):
                    a.activation(ed[r][:, s_, :], hs[r][:, s_, C_D:C_D + E], ACT.Exp,
                                 accum_out=sume[r][:, s_:s_ + 1]).then_inc(s_exp, 1)
                a.activation(res[r][:, :, :], hs[r][:, :, 0:D], ACT.Copy).then_inc(s_res, 1)

            def split(j, r, b, opening=False):
                act.wait_ge(s_x, b + 1)
                a.activation(xh[r][:, :], PP[:, :], ACT.Copy).then_inc(s_xh, 1)
                act.wait_ge(s_raw[r], 64 * (j + 1))
                if not opening:
                    act.wait_ge(s_y, b - 1)
                a.activation(wh[r][:, 0:2 * FF], raw[r][:, 0:2 * FF], ACT.Copy).then_inc(s_wh, 1)

            def block(j, r, first=False, tail=False):
                b = 2 * j + r
                opening = first and r == 0
                nxt = (j, 1) if r == 0 else (j + 1, 0)
                if not (tail and r == 1):
                    prepare(*nxt, b + 1, opening)
                for c in range(FC // 2):
                    act.wait_ge(s_u, 3 * b + c + 1)
                    if c == 0 and not first:
                        act.wait_ge(s_y, b - 1)
                    a.activation(hh[r][:, 2 * c:2 * c + 2, :],
                                 UU[3 * r + c][:, :].rearrange("p (c t) -> p c t", c=2), ACT.Relu).then_inc(s_hh, 1)
                    if c == 0:
                        a.activation(wh[r][:, 2 * FF:W_COLS], raw[r][:, 2 * FF:W_COLS], ACT.Copy).then_inc(s_wh, 1)
                if not (tail and r == 1):
                    split(*nxt, b + 1, opening)

            act.wait_ge(s_tab, 1)
            last = act.value_load(last_pair[0:1, 0:1], min_val=0, max_val=NBLK // 2 - 1 - LAST_MIN) + LAST_MIN
            prepare(0, 0, 0, True)
            split(0, 0, 0, True)
            pairs(act, block, last)

        @block_.vector
        def _(v):
            ch = Chain(v, s_dve)
            d = nc.vector

            def mul(o, a, b_):
                return d.tensor_tensor(o, a, b_, ALU.mult)

            d.memset(half_pi[:, :], float(np.pi / 2)).then_inc(s_constv, 1)
            d.memset(eps_tile[:, :], LN_EPS).then_inc(s_constv, 1)
            ch.step(d.memset(ones_bf[:, :], 1.0))
            ch.step(d.memset(ones_e[:, :], 1.0))
            ch.step(d.memset(fz[:, :, :, 0], 1.0))
            ch.step(d.memset(fn[:, :, :, 0], 1.0))
            ch.step(d.memset(before[:, 0, :], 0.0))
            ch.step(d.memset(gt[:, :, :, :], 0.0))
            ch.step(d.memset(sa[:, :, :, RA:RB0], 0.0))
            ch.step(d.memset(gs[:, :, :, NF], 1.0))
            ch.step(d.memset(wf_c[:, :, :, NF], 0.0))
            ch.step(d.memset(zs[:, :, 3], 1.0))
            ch.step(d.memset(term_sign[:, :], 1.0))
            for i in range(2):
                ch.step(d.memset(qt[i][G2:G2 + 1, :, :], 1.0))
                ch.step(d.memset(dm[i][G2:G2 + 1, :, :], DEN_EPS))
            ch.wait()
            ch.step(d.memset(gt[:, :, 0:2, ONE_IMG], 1.0))
            ch.step(d.memset(gt[:, :, 2, ONE_TXT], 1.0))
            for i, (_, _, sign) in enumerate(x5_terms()):
                if sign < 0:
                    ch.step(d.memset(term_sign[:, i:i + 1], -1.0))
            v.wait_ge(s_small, 32)
            d.scalar_tensor_tensor(pix_id[:, :], crv[:, :, 1], float(IMG), crv[:, :, 0], ALU.mult, ALU.add)\
             .then_inc(s_pixid, 1)

            v.wait_ge(s_wload, 96)
            v.wait_ge(s_wmean, 1)
            mean_w = bank[0][0:G2, 0:NF + E]
            for gi in range(2):
                for c in range(3):
                    ch.step(d.tensor_tensor(wf_c[:, gi, c, 0:NF], wfs[:, gi, :], mean_w[:, 0:NF], ALU.subtract))
                    ch.step(d.tensor_copy(wf_b[:, gi, c, :], wfs[:, gi, :]))
                ch.step(d.tensor_tensor(ir[:, gi, D:DL], ir[:, gi, D:DL], mean_w[:, NF:NF + E], ALU.subtract))
            ch.wait()
            for gi in range(2):
                for c in range(3):
                    for col in (ONE_IMG, ONE_TXT):
                        ch.step(d.tensor_tensor(wf_b[:, gi, c, col:col + 1], wf_b[:, gi, c, col:col + 1],
                                                pb[:, gi:gi + 1], ALU.add))
                for o, first, n in ((0, 0, 4), (16, 4, 7)):
                    w_ = wf_c[:, gi, 0, first:first + n]
                    ch.step(mul(outer[:, gi, o:o + n * n].rearrange("p (j k) -> p j k", j=n),
                                ap(w_, 0, [[1, n], [0, n]]), ap(w_, 0, [[0, n], [1, n]])))
            ch.wait()
            v.sem_inc(s_wcent, 1)
            v.wait_ge(s_wprod, 1)
            ch.step(d.tensor_copy(quad[:, :], bank[1][:, 0:65]))
            ch.step(d.tensor_copy(vw[:, :], bank[3][0:NG, 0:D]))
            ch.step(d.tensor_copy(pr[:, :, D:DL], bank[1][0:G2, 128:128 + 2 * E].rearrange("p (g e) -> p g e", g=2)))
            ch.step(d.tensor_scalar(hi_coef[:, :], lo_rows[:, :], -2.0, 1.0, ALU.mult, ALU.add))
            ch.step(d.tensor_copy(wa[:, :], bank[2][0:RA, 0:2 * D]))
            ch.step(d.tensor_copy(wb[RB0:RT, :], bank[4][RB0:RT, 0:DL]))
            ch.step(d.tensor_scalar(wa_lo[:, :], bank[2][0:RA, 0:2 * D], lo_rows[0:RA, 0:1], None, ALU.mult))
            ch.step(d.tensor_scalar(wb_lo[RB0:RT, :], bank[4][RB0:RT, 0:DL], lo_rows[RB0:RT, 1:2], None, ALU.mult))
            ch.wait()
            d.scalar_tensor_tensor(wa[:, :], wa[:, :].bitcast(F32), hi_coef[0:RA, 0:1], wa_lo[:, :],
                                   ALU.mult, ALU.add).then_inc(s_wready, 1)
            d.scalar_tensor_tensor(wb[RB0:RT, :], wb[RB0:RT, :].bitcast(F32), hi_coef[RB0:RT, 1:2], wb_lo[RB0:RT, :],
                                   ALU.mult, ALU.add).then_inc(s_wready, 1)

            v.wait_ge(s_prm, 16 * B)
            ch.link(d.tensor_scalar(kk[:, :, :], prm[:, :, :], float(1 / (2 * np.pi)), MAGIC, ALU.mult, ALU.add))
            ch.link(d.tensor_scalar(kk[:, :, :], kk[:, :, :], -MAGIC, None, ALU.add))
            ch.link(d.scalar_tensor_tensor(prm[:, :, :], kk[:, :, :], -TWO_PI_HI, prm[:, :, :], ALU.mult, ALU.add))
            ch.link(d.scalar_tensor_tensor(prm[:, :, :], kk[:, :, :], -float(TWO_PI_LO), prm[:, :, :],
                                           ALU.mult, ALU.add))
            d.tensor_scalar(prm[:, :, :], prm[:, :, :], PI, -PI, ALU.min, ALU.max).then_inc(s_red, 1)

            for n in range(2):
                v.wait_ge(s_pix[n], 16)
                ch.step(d.tensor_copy(gt[:, :, n, 0:CH], pixg[:, n, :].rearrange("p (b c) -> p b c", c=CH)))
            ch.wait()
            for n in range(2):
                f = gt[:, :, n, 0:4]
                q4 = ap(vq[:, :], 0, [[16, B], [4, 4], [1, 4]])
                ch.link(mul(q4, ap(f, 0, [[NT * NF, B], [1, 4], [0, 4]]), ap(f, 0, [[NT * NF, B], [0, 4], [1, 4]])))
                q1 = ap(vq[:, :], 0, [[16, B], [1, 16]])
                ch.link(mul(q1, q1, ap(quad[:, :], 0, [[0, B], [1, 16]])))
                ch.link(d.tensor_reduce(out=var[:, :, n], in_=q1, axis=AX.X, op=ALU.add))

            def th(a, layer):
                return a[:, :, :].rearrange("p t (l q r) -> p t l q r", l=LAYERS, r=2)[:, :, layer, :, 0]

            def ph(a, layer):
                return a[:, :, :].rearrange("p t (l q r) -> p t l q r", l=LAYERS, r=2)[:, :, layer, :, 1]

            v.wait_ge(s_trig, 2)
            ch.step(d.tensor_copy(fz[:, :, :, 1], th(cs, 0)))
            ch.step(mul(fz[:, :, :, 2], th(sn, 0), ph(cs, 0)))
            ch.step(mul(fz[:, :, :, 3], th(sn, 0), ph(sn, 0)))
            ch.wait()
            ch.step(d.tensor_copy(fn[:, :, :, 1:3], fz[:, :, :, 1:3]))
            ch.step(d.tensor_scalar(fn[:, :, :, 3], fz[:, :, :, 3], -1.0, None, ALU.mult))
            ch.step(d.tensor_scalar(ns[:, :, :], th(sn, 1), -1.0, None, ALU.mult))
            ch.wait()
            v.sem_inc(s_bloch, 1)

            c1 = th(cs, 1)
            ch.step(mul(tr[:, :, :, 0:4], fn[:, :, :, :], ap(c1, 0, [[NPAR, B], [2, NQ], [0, 4]])))
            ch.step(mul(tr[:, :, :, 4:6], fz[:, :, :, 2:4], ap(ns[:, :, :], 0, [[NQ, B], [1, NQ], [0, 2]])))
            ch.step(mul(tr[:, :, :, 6:8], fz[:, :, :, 0:2], ap(ns[:, :, :], 0, [[NQ, B], [1, NQ], [0, 2]])))
            f0, n0 = fz[:, :, 0, :], fn[:, :, 0, :]
            cc = ap(c1, 0, [[NPAR, B], [0, 2]])
            s0 = ns[:, :, 0:1].to_broadcast([P, B, 2])
            ch.step(mul(base[:, :, 0:2], ap(f0, 1, [[4 * NQ, B], [-1, 2]]), cc))
            ch.step(mul(base[:, :, 2:4], f0[:, :, 2:4], s0))
            ch.step(d.tensor_copy(base[:, :, 4:6], f0[:, :, 0:2]))
            ch.step(mul(base[:, :, 6:8], ap(n0, 3, [[4 * NQ, B], [-1, 2]]), cc))
            ch.step(mul(base[:, :, 8:10], f0[:, :, 0:2], s0))
            ch.step(d.tensor_copy(base[:, :, 10:12], f0[:, :, 2:4]))
            ch.wait()
            for f in range(2):
                for fp in range(2):
                    o, st_ = (4 * fp + 2 * f, 1) if f else (4 * fp + 1, -1)
                    ch.step(mul(ap(vs[:, 0, :, :], o, [[24, B], [8, 3], [st_, 2]]),
                                ap(base[:, :, :], 2 * fp, [[12, B], [4, 3], [1, 2]]),
                                ap(tr[:, :, 1, :], 4 * f + 2 * fp, [[8 * NQ, B], [0, 3], [1, 2]])))
            ch.wait()
            for k in range(2, 5):
                for f in range(2):
                    ch.step(mul(ap(tmp[f][:, :, :], 0, [[24, B], [4, 6], [1, 4]]),
                                ap(vs[:, k - 2, :, :], 0, [[24, B], [4, 6], [1, 4]]),
                                ap(tr[:, :, k, :], 4 * f, [[8 * NQ, B], [0, 6], [1, 4]])))
                ch.wait()
                for f in range(2):
                    o, st_ = (2, 1) if f else (1, -1)
                    ch.step(d.tensor_tensor(ap(vs[:, k - 1, :, :], o, [[4, 6 * B], [st_, 2]]),
                                            ap(tmp[f][:, :, :], 0, [[4, 6 * B], [1, 2]]),
                                            ap(tmp[f][:, :, :], 2, [[4, 6 * B], [1, 2]]), ALU.add))
                ch.wait()
            ch.step(d.tensor_copy(zs[:, :, 2:3], fz[:, :, 5, 1:2]))
            ch.link(mul(zs[:, :, 1:2], fz[:, :, 4, 1:2], fz[:, :, 5, 1:2]))
            ch.step(mul(zs[:, :, 0:1], fz[:, :, 3, 1:2], zs[:, :, 1:2]))
            for a_ in range(2):
                o = 4 if a_ else 1
                c_o = 0 if a_ else 1
                ch.step(mul(ap(ezt[:, :, :, :], 2 * a_, [[4 * B, 4], [4, B], [1, 2]]),
                            ap(vs[:, :, :, :], o, [[24 * B, 4], [24, B], [2, 2]]),
                            ap(fn[:, :, 2, :], c_o, [[4, 4], [4 * NQ, B], [2, 2]])))
            for a_, vo, vstep, to, tstep in ((0, 0, 13, 0, 5), (1, 5, 11, 1, 3), (2, 9, 11, 1, 3)):
                ch.step(mul(ap(w5[:, :, :], 4 * a_, [[12, B], [2, 2], [1, 2]]),
                            ap(vs[:, 3, :, :], vo, [[24, B], [vstep, 2], [2, 2]]),
                            ap(tr[:, :, 5, :], to, [[8 * NQ, B], [tstep, 2], [2, 2]])))
            ch.wait()
            ch.step(mul(ap(ezt[:, :, :, :], 0, [[4 * B, 4], [4, B], [1, 2]]),
                        ap(ezt[:, :, :, :], 0, [[4 * B, 4], [4, B], [1, 2]]),
                        ap(zs[:, :, :], 0, [[1, 4], [4, B], [0, 2]])))
            ch.step(d.tensor_reduce(out=ez[:, 0, :], in_=w5[:, :, 8:12], axis=AX.X, op=ALU.add))
            ch.step(d.tensor_reduce(out=ez[:, 5, :], in_=w5[:, :, 0:8], axis=AX.X, op=ALU.add))
            ch.wait()
            ch.step(d.tensor_reduce(out=ez[:, 1:5, :], in_=ezt[:, :, :, :], axis=AX.X, op=ALU.add))
            v.wait_ge(s_ex, 2)
            ch.step(d.tensor_reduce(out=ex[:, :, 0:5], in_=gx[:, :, :, :], axis=AX.X, op=ALU.add))
            ch.step(d.tensor_reduce(out=ex[:, :, 5:6], in_=gp[:, :, :], axis=AX.X, op=ALU.add))
            ch.wait()
            ch.step(mul(ex[:, :, :], ex[:, :, :], th(sn, 2)))
            ch.step(mul(ns[:, :, :], ez[:, :, :].rearrange("p q t -> p t q"), th(cs, 2)))
            ch.wait()
            ch.link(d.tensor_tensor(gt[:, :, 2, 4:4 + NQ], ns[:, :, :], ex[:, :, :], ALU.subtract))

            f = gt[:, :, 2, 4:11]
            ch.link(mul(ap(vq[:, :], 0, [[49, B], [7, 7], [1, 7]]),
                        ap(f, 0, [[NT * NF, B], [1, 7], [0, 7]]), ap(f, 0, [[NT * NF, B], [0, 7], [1, 7]])))
            q1 = ap(vq[:, :], 0, [[49, B], [1, 49]])
            ch.link(mul(q1, q1, ap(quad[:, :], 16, [[0, B], [1, 49]])))
            d.tensor_reduce(out=var[:, :, 2], in_=q1, axis=AX.X, op=ALU.add).then_inc(s_var, 1)
            for t in range(NT):
                g_ = gt[:, :, t, :]
                hi = sa[:, :, t, RB0:RB0 + NF]
                ch.link(d.tensor_copy(hi.bitcast(F32R), g_))
                ch.step(d.tensor_tensor(sa[:, :, t, RB0 + NF:RB0 + 2 * NF], g_, hi, ALU.subtract))
                ch.step(d.tensor_copy(sa[:, :, t, RB0 + 2 * NF:RT], hi))
            v.wait_ge(s_sd, 1)
            ch.step(d.tensor_scalar(var[:, :, :], var[:, :, :], LN_EPS, -0.5, ALU.add, ALU.mult))
            ch.link(d.reciprocal(rstd[:, :, :], rstd[:, :, :]))
            ch.link(mul(newt[:, :, :], rstd[:, :, :], rstd[:, :, :]))
            ch.link(mul(newt[:, :, :], newt[:, :, :], var[:, :, :]))
            ch.link(d.tensor_scalar(newt[:, :, :], newt[:, :, :], 1.5, None, ALU.add))
            ch.link(mul(rstd[:, :, :], rstd[:, :, :], newt[:, :, :]))
            ch.link(mul(gs[:, :, :, 0:NF].rearrange("p b t j -> p (b t) j"),
                        gt[:, :, :, :].rearrange("p b t j -> p (b t) j"),
                        ap(rstd[:, :, :], 0, [[1, TILES], [0, NF]])))
            sat = sa[:, :, :, :].rearrange("p b t j -> p (b t) j")
            gst = gs[:, :, :, :].rearrange("p b t j -> p (b t) j")
            ch.link(d.tensor_copy(sat[:, :, 0:NG].bitcast(F32R), gst))
            ch.step(d.tensor_tensor(sat[:, :, NG:2 * NG], gst, sat[:, :, 0:NG], ALU.subtract))
            ch.step(d.tensor_copy(sat[:, :, 2 * NG:RA], sat[:, :, 0:NG]))
            ch.wait()
            v.sem_inc(s_sa, 1)
            v.wait_ge(s_const, 14)

            def front(b):
                r = b % 2
                for h in range(2):
                    v.wait_ge(s_q, 2 * b + h + 1)
                    d.tensor_scalar(qt[r][0:G2, h, :], (Q0, Q1)[h][0:G2, 0:NT * P], SCALE, None, ALU.max)\
                     .then_inc(s_qt, 1)
                v.wait_ge(s_k, 2 * b + 1)
                if b >= 2:
                    v.wait_ge(s_kg, b - 1)
                d.tensor_scalar(kt[r][:, 0:2, :], K0[:, 0:2 * D].rearrange("p (t d) -> p t d", t=2), SCALE, None,
                                ALU.max).then_inc(s_kt, 1)
                v.wait_ge(s_k, 2 * b + 2)
                d.tensor_scalar(kt[r][:, 2, :], K1[:, 0:D], SCALE, None, ALU.max).then_inc(s_kt, 1)
                v.wait_ge(s_kg, b + 1)
                if b >= 2:
                    v.wait_ge(s_kv, b - 1)
                d.tensor_copy(kg[r][:, :], K1[0:NG, 256:256 + D]).then_inc(s_kgc, 1)
                v.wait_ge(s_kv, b + 1)
                if b >= 2:
                    v.wait_ge(s_den, b - 1)
                    v.wait_ge(s_m, b - 1)
                mul(kvm[r][:, :, :], MM[0:G2, 0:2 * G2].rearrange("p (k d) -> p k d", k=2),
                    ap(head_mask[:, :], 0, [[0, 2], [1, G2]])).then_inc(s_kvc, 1)
                mul(dm[r][0:G2, :, :], MM[0:G2, 2 * G2:2 * G2 + 2 * NQ].rearrange("p (k d) -> p k d", k=2),
                    ap(head_mask[:, :], 0, [[0, 2], [HD, NQ]])).then_inc(s_kvc, 1)

            def back(b):
                r = b % 2
                v.wait_ge(s_den, b + 1)
                if b >= 2:
                    v.wait_ge(s_zt, 2 * (b - 1))
                d.reciprocal(zr[r][:, :, :, :].rearrange("p t g h -> p (t g h)"), HB[:, 0:NT * 2 * NQ])\
                 .then_inc(s_z, 1)
                for h in range(2):
                    v.wait_ge(s_zt, 2 * b + h + 1)
                    if b >= 2 and h == 0:
                        v.wait_ge(s_h, NT * (b - 1))
                    mul(zt[r][:, h, :], qt[r][0:G2, h, :], (D0, D1)[h][0:G2, 0:NT * P]).then_inc(s_qz, 1)
                for t in range(NT):
                    n = b * NT + t
                    v.wait_ge(s_hc, n + 1)
                    d.bn_stats(st6[:, t, :], row[r][:, t, 0:D]).then_inc(s_bn, 1)
                v.wait_ge(s_bn, NT * (b + 1))
                for t in range(NT):
                    ch.step(d.bn_aggr(mv[:, t, :], st6[:, t, :]))
                ch.wait()
                v.sem_inc(s_v2, 1)

            def route(b):
                r = b % 2
                rw_ = row[r]
                v.wait_ge(s_hc, NT * (b + 1))
                lg = rw_[:, :, D:DL]
                ch.step(d.tensor_reduce(out=mx[:, :], in_=lg, axis=AX.X, op=ALU.max))
                v.wait_ge(s_sd2, b + 1)
                ch.step(d.reciprocal(rw_[:, :, C_RS], std[r][:, :]))
                ch.wait()
                mxb = ap(mx[:, :], 0, [[1, NT], [0, E]])
                ch.link(d.tensor_tensor(ohf[:, :, :], lg, mxb, ALU.is_ge))
                ch.step(mul(ohf[:, :, :], ohf[:, :, :], expert_key[:, :, :]))
                ch.step(d.tensor_tensor(lg, lg, mxb, ALU.subtract))
                ch.wait()
                ch.step(mul(lg, lg, ap(rw_[:, :, C_RS:C_RS + 1], 0, [[RW, NT], [0, E]])))
                ch.link(d.tensor_reduce(out=key[:, :], in_=ohf[:, :, :], axis=AX.X, op=ALU.max))
                ch.link(d.tensor_tensor(ohf[:, :, :], expert_key[:, :, :], ap(key[:, :], 0, [[1, NT], [0, E]]),
                                        ALU.is_equal))
                if b:
                    v.wait_ge(s_rk, b)
                    ch.step(d.tensor_copy(before[:, 0, :], before[:, NT, :]))
                ch.step(d.tensor_copy(oh[:, :, :], ohf[:, :, :]))
                for t in range(NT):
                    ch.wait()
                    ch.step(d.tensor_tensor(before[:, t + 1, :], before[:, t, :], oh[:, t, :], ALU.add))
                ch.wait()
                v.sem_inc(s_oh, 1)
                ch.step(d.scalar_tensor_tensor(rw_[:, :, C_NM], mv[:, :, 0], -1.0, rw_[:, :, C_RS],
                                               ALU.mult, ALU.mult))
                ch.step(d.tensor_copy(oh_all[:, b * NT:(b + 1) * NT, :], oh[:, :, :]))
                v.wait_ge(s_rk, b + 1)
                cum = HB[:, 256:256 + NT * E].rearrange("p (t e) -> p t e", e=E)
                ch.link(mul(ohf[:, :, :], cum, ohf[:, :, :]))
                ch.link(d.tensor_reduce(out=rank[:, :], in_=ohf[:, :, :], axis=AX.X, op=ALU.add))
                ch.link(d.tensor_scalar(r_i[:, :], rank[:, :], -1.0, None, ALU.add))
                v.sem_inc(s_slot, 1)
                ch.step(d.tensor_scalar(lo_i[:, :], r_i[:, :], P - 1, None, ALU.bitwise_and))
                ch.step(d.tensor_scalar(hi_i[:, :], r_i[:, :], 7, None, ALU.arith_shift_right))
                ch.wait()
                ch.step(d.tensor_copy(hi_f[:, b * NT:(b + 1) * NT], hi_i[:, :]))
                d.tensor_copy(lo_f[:, b * NT:(b + 1) * NT], lo_i[:, :]).then_inc(s_lo, 1)

            def tables():
                v.wait_ge(s_cnt, 1)
                ch.link(d.tensor_scalar(cnt_i[:, :], HB[:, 384:384 + E], float(BLK - 1), None, ALU.add))
                ch.link(d.tensor_scalar(cnt_j[:, :], cnt_i[:, :], 8, None, ALU.arith_shift_right))
                ch.link(d.tensor_copy(cnt[:, :], cnt_j[:, :]))
                ch.link(d.tensor_tensor_scan(blk_end[:, :], ones_e[:, :], cnt[:, :], 0.0, ALU.mult, ALU.add))
                ch.step(d.tensor_tensor(be[:, :, :], iota_blk[:, :, :], ap(blk_end[0:1, :], 0, [[0, NBLK], [1, E]]),
                                        ALU.is_ge))
                ch.step(d.tensor_scalar(n_last[:, :], blk_end[0:1, E - 1:E], -1.0 - 2 * LAST_MIN, None, ALU.add))
                ch.link(d.tensor_tensor(first_tile[:, :], blk_end[:, :], cnt[:, :], ALU.subtract))
                ch.link(d.tensor_scalar(first_tile[:, :], first_tile[:, :], float(ST), None, ALU.mult))
                ch.link(mul(tl[:, :, :], oh_all[:, :, :], ap(first_tile[:, :], 0, [[0, TILES], [1, E]])))
                ch.link(d.tensor_reduce(out=tile_f[:, :], in_=tl[:, :, :], axis=AX.X, op=ALU.add))
                ch.link(d.tensor_tensor(tile_f[:, :], tile_f[:, :], hi_f[:, :], ALU.add))
                ch.link(d.tensor_tensor(oh_hi[:, :, 0, :], ap(iota_lane[:, :], 0, [[0, TILES], [1, NTILE]]),
                                        ap(tile_f[:, :], 0, [[1, TILES], [0, NTILE]]), ALU.is_equal))
                ch.step(d.tensor_scalar(oh_hi[:, :, 1, :], oh_hi[:, :, 0, :], iota_p[:, :], None, ALU.mult))
                ch.step(mul(oh_hi[:, :, 2, :], oh_hi[:, :, 0, :], ap(iota_t[:, :], 0, [[1, TILES], [0, NTILE]])))
                ch.wait()
                v.sem_inc(s_ohhi, 1)
                ch.link(d.tensor_reduce(out=bef[:, :], in_=be[:, :, :], axis=AX.X, op=ALU.add))
                ch.step(d.tensor_scalar(blk_expert[:, :], bef[:, :], float(E - 1), None, ALU.min))
                ch.step(d.tensor_scalar(last_pair[:, :], n_last[:, :], 1, None, ALU.arith_shift_right))
                v.wait_ge(s_inv, 1)
                filled, lane, tile = (Q0[:, k * NTILE:(k + 1) * NTILE] for k in range(3))
                ch.step(d.tensor_copy(lane_f[:, :], lane))
                ch.link(d.tensor_copy(fill_f[:, :], filled))
                ch.link(d.scalar_tensor_tensor(gidf[:, :], tile, float(P), lane_f[:, :], ALU.mult, ALU.add))
                ch.link(d.scalar_tensor_tensor(sidf[:, :], fill_f[:, :], -float(OUT_OF_BOUNDS), gidf[:, :],
                                               ALU.mult, ALU.add))
                ch.step(d.tensor_scalar(sid[:, :], sidf[:, :], float(OUT_OF_BOUNDS), None, ALU.add))
                ch.step(d.tensor_copy(gid[:, :], gidf[:, :]))
                ch.wait()
                v.sem_inc(s_tab, 1)

            front(0)
            for b in range(B):
                if b + 1 < B:
                    front(b + 1)
                back(b)
                route(b)
            tables()

            def prepare(j, r, b, opening=False):
                v.wait_ge(s_hs[r], 16 * ST * (j + 1))
                if not opening:
                    v.wait_ge(s_x, b - 1)
                for s_ in range(ST):
                    h_ = hs[r][:, s_, :]
                    rs, nm = h_[:, C_RS:C_RS + 1], h_[:, C_NM:C_NM + 1]
                    d.tensor_scalar(xn[r][:, s_, 0:P], h_[:, 0:P], rs, nm, ALU.mult, ALU.add).then_inc(s_xn, 1)
                    d.tensor_scalar(xn[r][:, s_, P:256].rearrange("p (a j) -> p a j", a=2),
                                    ap(h_, P, [[0, 2], [1, 64]]), rs, nm, ALU.mult, ALU.add).then_inc(s_xn, 1)
                v.wait_ge(s_exp, ST * b + ST)
                d.reciprocal(prob[r][:, :], sume[r][:, :]).then_inc(s_pr, 1)

            def split(j, r, b, opening=False):
                v.wait_ge(s_xh, b + 1)
                d.tensor_tensor(xl[r][:, :], PP[:, 0:BLK], xh[r][:, 0:BLK].bitcast(F32), ALU.subtract)\
                 .then_inc(s_xl, 1)
                d.tensor_tensor(xh[r][64:P, BLK:2 * BLK], PP[64:P, BLK:2 * BLK],
                                xh[r][64:P, BLK:2 * BLK].bitcast(F32), ALU.subtract).then_inc(s_xl, 1)
                v.wait_ge(s_wh, 2 * b + 1)
                if not opening:
                    v.wait_ge(s_y, b - 1)
                d.tensor_tensor(wl[r][:, 0:2 * FF], raw[r][:, 0:2 * FF], wh[r][:, 0:2 * FF].bitcast(F32),
                                ALU.subtract).then_inc(s_wl, 1)

            def block(j, r, first=False, tail=False):
                b = 2 * j + r
                opening = first and r == 0
                nxt = (j, 1) if r == 0 else (j + 1, 0)
                if not (tail and r == 1):
                    prepare(*nxt, b + 1, opening)
                for c in range(FC // 2):
                    v.wait_ge(s_hh, 3 * b + c + 1)
                    d.scalar_tensor_tensor(hl[r][:, 2 * c:2 * c + 2, :],
                                           UU[3 * r + c][:, :].rearrange("p (c t) -> p c t", c=2), 0.0,
                                           hh[r][:, 2 * c:2 * c + 2, :].bitcast(F32), ALU.max, ALU.subtract)\
                     .then_inc(s_hl, 1)
                    if c == 0:
                        v.wait_ge(s_wh, 2 * b + 2)
                        d.tensor_tensor(wl[r][:, 2 * FF:W_COLS], raw[r][:, 2 * FF:W_COLS],
                                        wh[r][:, 2 * FF:W_COLS].bitcast(F32), ALU.subtract).then_inc(s_wl, 1)
                if not (tail and r == 1):
                    split(*nxt, b + 1, opening)
                v.wait_ge(s_y, b + 1)
                v.wait_ge(s_res, b + 1)
                v.wait_ge(s_pr, b + 1)
                if not first:
                    v.wait_ge(s_fin[r], 16 * ST * j)
                for s_ in range(ST):
                    d.scalar_tensor_tensor(yr[r][:, s_, :], YY[:, s_ * 256:s_ * 256 + D], prob[r][:, s_:s_ + 1],
                                           res[r][:, s_, :], ALU.mult, ALU.add).then_inc(s_yr, 1)

            last = v.value_load(last_pair[0:1, 0:1], min_val=0, max_val=NBLK // 2 - 1 - LAST_MIN) + LAST_MIN
            prepare(0, 0, 0, True)
            split(0, 0, 0, True)
            pairs(v, block, last)

        @block_.tensor
        def _(pe):
            t_ = nc.tensor

            def mm(o, l, r_, start=True, stop=True):
                return t_.matmul(o, l, r_, start=start, stop=stop)

            pe.wait_ge(s_const, 14)
            pe.wait_ge(s_wload, 96)
            for gi in range(2):
                last = mm(bank[0][:, 0:NF], ones_mean[:, :], wfs[:, gi, :], gi == 0, gi == 1)
            for gi in range(2):
                last = mm(bank[0][:, NF:NF + E], ones_mean[:, :], ir[:, gi, D:DL], gi == 0, gi == 1)
            last.then_inc(s_wmean, 1)
            pe.wait_ge(s_wcent, 1)
            for gi in range(2):
                mm(bank[1][:, 0:65], ones_mean[:, :], outer[:, gi, :], gi == 0, gi == 1)
            for gi in range(2):
                for k in range(2):
                    mm(bank[1][0:G2, 128 + E * gi:128 + E * gi + E], pw[:, k, gi * G2:(gi + 1) * G2], ir[:, k, D:DL],
                       k == 0, k == 1)
            for o, lo, hi, copies in ((bank[2], 0, 2 * D, 3), (bank[3], 2 * D, 3 * D, 1)):
                rows = copies * NG
                for k in range(2):
                    mm(o[0:rows, 0:hi - lo], wf_c[:, k, 0:copies, :].rearrange("p c j -> p (c j)"),
                       wq_in[:, k, lo:hi], k == 0, False)
                mm(o[0:rows, 0:hi - lo], one_hot_row[:, 0:rows], const_row[:, lo:hi], False, True)
            for k in range(2):
                last = mm(bank[4][RB0:RT, 0:DL], wf_b[:, k, :, :].rearrange("p c j -> p (c j)"), ir[:, k, :],
                          k == 0, k == 1)
            last.then_inc(s_wprod, 1)
            pe.wait_ge(s_wready, 2)
            pe.wait_ge(s_sa, 1)

            def transpose(b):
                for t in range(NT):
                    last = t_.transpose(K0[0:RT, t * P:(t + 1) * P], sa[:, b, t, :], ident[:, :])
                last.then_inc(s_t, 1)

            def front(b):
                r = b % 2
                pe.wait_ge(s_gtt, b + 1)
                g_ = gtt[r]
                if b:
                    pe.wait_ge(s_qt, 2 * b)
                for h in range(2):
                    mm((Q0, Q1)[h][0:G2, 0:NT * P], wa[:, h * G2:(h + 1) * G2], g_[0:RA, :]).then_inc(s_q, 1)
                for t in range(2):
                    last = mm(K0[:, t * D:(t + 1) * D], g_[0:RA, t * P:(t + 1) * P], wa[:, D:2 * D])
                last.then_inc(s_k, 1)
                if b:
                    pe.wait_ge(s_kgc, b)
                mm(K1[:, 0:D], g_[0:RA, 2 * P:3 * P], wa[:, D:2 * D]).then_inc(s_k, 1)
                pe.wait_ge(s_kt, 2 * b + 1)
                if b + 1 < B:
                    transpose(b + 1)
                pe.wait_ge(s_kt, 2 * b + 2)
                for t in range(NT):
                    last = mm(K1[0:NG, 256:256 + D], gs[:, b, t, :], kt[r][:, t, :], t == 0, t == NT - 1)
                last.then_inc(s_kg, 1)
                pe.wait_ge(s_kgc, b + 1)
                if b >= 2:
                    pe.wait_ge(s_mc, b - 1)
                for h in range(2):
                    s_ = slice(h * G2, (h + 1) * G2)
                    mm(MM[0:G2, h * G2:(h + 1) * G2], vw[:, s_], kg[r][:, s_])
                    last = mm(MM[0:G2, 2 * G2 + h * NQ:2 * G2 + (h + 1) * NQ], kg[r][:, s_], ksum_sel[:, 0:NQ])
                last.then_inc(s_kv, 1)

            def back(b):
                r = b % 2
                pe.wait_ge(s_kvc, 2 * min(b + 2, B))
                for h in range(2):
                    last = mm(MM[0:G2, h * DL:(h + 1) * DL], kvm[r][:, h, :], pr[:, h, :])
                last.then_inc(s_m, 1)
                pe.wait_ge(s_qt, 2 * b + 2)
                if b:
                    pe.wait_ge(s_hc, NT * b)
                    pe.wait_ge(s_slot, b)
                for t in range(NT):
                    for h in range(2):
                        o = (2 * t + h) * NQ
                        last = mm(HB[:, o:o + NQ], qt[r][:, h, t * P:(t + 1) * P], dm[r][:, h, :])
                last.then_inc(s_den, 1)
                pe.wait_ge(s_zx, b + 1)
                for h in range(2):
                    for t in range(NT):
                        last = t_.transpose((D0, D1)[h][0:G2, t * P:(t + 1) * P],
                                            zx[:, t, h * G2:(h + 1) * G2], ident[:, :])
                    last.then_inc(s_zt, 1)
                pe.wait_ge(s_mc, b + 1)
                pe.wait_ge(s_qz, 2 * (b + 1))
                for t in range(NT):
                    s_ = slice(t * P, (t + 1) * P)
                    o = HT[t][:, 0:DL]
                    mm(o, gtt[r][RB0:RT, s_], wb[RB0:RT, :], True, False)
                    mm(o, zt[r][:, 0, s_], mb[r][:, 0, :], False, False)
                    mm(o, zt[r][:, 1, s_], mb[r][:, 1, :], False, True).then_inc(s_h, 1)

            def ranks(b):
                pe.wait_ge(s_oh, b + 1)
                pe.wait_ge(s_hc, NT * b + 1)
                o = HB[:, 256:256 + NT * E]
                mm(o, tri[:, :], oh[:, :, :].rearrange("p t e -> p (t e)"), True, False)
                mm(o, ones_bf[:, :], before[:, 0:NT, :].rearrange("p t e -> p (t e)"), False, True).then_inc(s_rk, 1)

            transpose(0)
            front(0)
            for b in range(B):
                if b + 1 < B:
                    front(b + 1)
                back(b)
                ranks(b)
            pe.wait_ge(s_slot, B)
            mm(HB[:, 384:384 + E], ones_bf[:, :], before[:, NT, :]).then_inc(s_cnt, 1)
            pe.wait_ge(s_ohhi, 1)
            pe.wait_ge(s_ohlo, TILES)
            for n in range(TILES):
                last = mm(Q0[:, 0:3 * NTILE], oh_lo[:, n, :], oh_hi[:, n, :, :].rearrange("p k s -> p (k s)"),
                          n == 0, n == TILES - 1)
            last.then_inc(s_inv, 1)

            def transpose_slots(r, b):
                pe.wait_ge(s_xn, 2 * ST * b + 2 * ST)
                for k in range(2):
                    for s_ in range(ST):
                        last = t_.transpose(PP[:, k * BLK + s_ * P:k * BLK + (s_ + 1) * P],
                                            xn[r][:, s_, k * P:(k + 1) * P], ident[:, :])
                last.then_inc(s_x, 1)

            def block(j, r, first=False, tail=False):
                b = 2 * j + r
                pe.wait_ge(s_xl, 2 * b + 2)
                pe.wait_ge(s_wh, 2 * b + 1)
                pe.wait_ge(s_wl, 2 * b + 1)
                for c in range(FC):
                    if c % 2 == 0 and not first:
                        pe.wait_ge(s_hl, 3 * b - 5 + c // 2)
                    o = UU[3 * r + c // 2][:, (c % 2) * BLK:(c % 2 + 1) * BLK]
                    s1, s2 = slice(c * P, (c + 1) * P), slice(FF + c * P, FF + (c + 1) * P)
                    mm(o, wh[r][:, s1], xh[r][:, 0:BLK], True, False)
                    mm(o, wh[r][:, s1], xl[r][:, :], False, False)
                    mm(o, wl[r][:, s1], xh[r][:, 0:BLK], False, False)
                    mm(o, wh[r][:, s2], xh[r][:, BLK:2 * BLK], False, False)
                    last = mm(o, wl[r][:, s2], xh[r][:, BLK:2 * BLK], False, True)
                    if c % 2:
                        last.then_inc(s_u, 1)
                if not (tail and r == 1):
                    transpose_slots(1 - r, b + 1)
                pe.wait_ge(s_wl, 2 * b + 2)
                if not (first and r == 0):
                    pe.wait_ge(s_yr, ST * b)
                for s_ in range(ST):
                    o = YY[:, s_ * 256:s_ * 256 + D]
                    t0 = slice(s_ * P, (s_ + 1) * P)
                    for c in range(FC):
                        if s_ == 0 and c % 2 == 0:
                            pe.wait_ge(s_hl, 3 * b + c // 2 + 1)
                        w_ = slice(2 * FF + c * D, 2 * FF + (c + 1) * D)
                        mm(o, hh[r][:, c, t0], wh[r][:, w_], c == 0, False)
                        mm(o, hh[r][:, c, t0], wl[r][:, w_], False, False)
                        last = mm(o, hl[r][:, c, t0], wh[r][:, w_], False, c == FC - 1)
                last.then_inc(s_y, 1)

            pe.wait_ge(s_tab, 1)
            last_ = pe.value_load(last_pair[0:1, 0:1], min_val=0, max_val=NBLK // 2 - 1 - LAST_MIN) + LAST_MIN
            transpose_slots(0, 0)
            pairs(pe, block, last_)


_OUT = (B, NT * P, D)


def kernel(x, x_txt, L0_tok_curve, L0_tok_proj_w, L0_tok_proj_b, L0_txt_quantum_params, L0_txt_post_w,
           L0_txt_post_b, L0_attn_qkv_w, L0_attn_proj_w, L0_attn_proj_b, L0_ffn_router_w, L0_ffn_wi, L0_ffn_wo):
    import concourse.bacc as bacc
    from concourse.bass_utils import run_bass_kernel_spmd

    nc = bacc.Bacc("TRN2", target_bir_lowering=False, num_devices=1)
    x = np.asarray(x)
    layout = {
        "pixels": x.transpose(2, 3, 0, 1).reshape(IMG * IMG, B * CH),
        "curve": np.asarray(L0_tok_curve),
        "txt_ids": np.asarray(x_txt).T,
        "qparams": np.asarray(L0_txt_quantum_params).reshape(VOCAB, NPAR),
        "wf": np.concatenate([np.asarray(L0_tok_proj_w), np.asarray(L0_tok_proj_b)[:, None],
                              np.asarray(L0_txt_post_w), np.asarray(L0_txt_post_b)[:, None]], axis=1),
        "qkv_wT": np.asarray(L0_attn_qkv_w).T,
        "proj_w": np.asarray(L0_attn_proj_w),
        "proj_wT": np.asarray(L0_attn_proj_w).T,
        "proj_b": np.asarray(L0_attn_proj_b).reshape(2, G2).T,
        "router_w": np.asarray(L0_ffn_router_w),
        "wi": np.asarray(L0_ffn_wi),
        "wo": np.asarray(L0_ffn_wo),
    }
    arrays, args = {}, []
    for name, a in layout.items():
        a = np.ascontiguousarray(a)
        arrays[f"{name}_dram"] = a
        args.append(nc.dram_tensor(f"{name}_dram", a.shape, mybir.dt.from_np(a.dtype), kind="ExternalInput").ap())
    args.append(nc.dram_tensor("out_dram", _OUT, F32, kind="ExternalOutput").ap())
    fusion_kernel(nc, *args)
    r = run_bass_kernel_spmd(nc, [arrays], core_ids=[0])
    return r.results[0]["out_dram"]
```

```python
from contextlib import ExitStack

import numpy as np

import concourse.bass as bass
from concourse import mybir

F32 = mybir.dt.float32
F32R = mybir.dt.float32r
BF16 = mybir.dt.bfloat16
I32 = mybir.dt.int32
U32 = mybir.dt.uint32
ALU = mybir.AluOpType
ACT = mybir.ActivationFunctionType
AX = mybir.AxisListType

P = 128
B = 8
NIMG, NTXT = 256, 128
NT = 3
TILES = B * NT
TOKENS = TILES * P
D = 192
G2 = 96
HD = 16
FF = 768
FC = FF // P
E = 8
POOL_TILES = TILES - 8
RANK_BATCH = B // 2 + 1
TG = TILES // 2
BLK = 256
ST = BLK // P
NBLK = 20
CUM0, CNT0 = NT * P, NT * P + TG * E
LAST_MIN = (TILES * P // BLK - 1) // 2
NTILE = NBLK * ST
NQ = 6
LAYERS = 3
NPAR = LAYERS * NQ * 2
IMG = 84
CH = 3
VOCAB = 8000
NF = 11
NG = 12
ONE_IMG, ONE_TXT = 3, 10
RA = 3 * NG
RB0 = 64
RB = 3 * NF
RT = RB0 + RB
DL = D + E
C_D, C_RS, C_NM = D, D + E, D + E + 1
RW = D + E + 2
OUT_OF_BOUNDS = 1 << 20
LN_EPS = 1e-5
DEN_EPS = 1e-6
SCALE = HD ** -0.5
PI = 3.1415925
MAGIC = 1.5 * 2.0 ** 23
TWO_PI_HI = 6.28125
TWO_PI_LO = 2 * np.pi - 6.28125
W_COLS = FF + FF + FC * D

PAULI = {"X": (1, 0), "Z": (0, 1), "Y": (1, 1)}


def ap(base, offset, dims):
    return bass.AP(tensor=base.tensor, offset=base.offset + offset, ap=[list(base.ap[0])] + [list(d) for d in dims])


def x5_terms():
    terms = []
    for s1 in "XZY":
        for s5 in "XYZ":
            for s0 in "ZXY":
                (f0, g0), (f1, g1), (f5, g5) = PAULI[s0], PAULI[s1], PAULI[s5]
                x0, z0, x1, z1, w = f0 ^ f5, g1 ^ g5, f0 ^ f1 ^ f5, g0 ^ g1 ^ g5, g0 ^ g5
                ys = [s0, s1, s5].count("Y")
                xz = x0 * z0 + x1 * z1 + f1 * w + f5 * w
                sign = 1 if (ys - xz) % 4 == 0 else -1
                terms.append((x0 * 8 + z0 * 4 + x1 * 2 + z1, f1 * 4 + f5 * 2 + w, sign))
    return terms


def affine_runs(seq):
    out, i = [], 0
    while i < len(seq):
        best, dims = 1, [[1, 1]]
        j = i + 1
        if j < len(seq):
            step = seq[j] - seq[i]
            while j + 1 < len(seq) and seq[j + 1] - seq[j] == step:
                j += 1
            best, dims = j - i + 1, [[step, j - i + 1]]
        for a in (2, 3, 6, 9):
            for b in (2, 3, 4, 9):
                if a * b > best and i + a * b <= len(seq):
                    s1, s2 = seq[i + 1] - seq[i], seq[i + a] - seq[i]
                    if all(seq[i + q * a + r] == seq[i] + q * s2 + r * s1 for q in range(b) for r in range(a)):
                        best, dims = a * b, [[s2, b], [s1, a]]
        out.append((i, best, dims))
        i += best
    return out


class Chain:

    def __init__(self, engine, sem):
        self.engine, self.sem, self.n = engine, sem, 0

    def step(self, ins):
        self.n += 1
        ins.then_inc(self.sem, 1)
        return self.n

    def wait(self, n=None):
        self.engine.wait_ge(self.sem, self.n if n is None else n)

    def link(self, ins):
        self.step(ins)
        self.wait()


def fusion_kernel(nc, pixels, curve, txt_ids, qparams, wf, qkv_wT, proj_w, proj_wT, proj_b, router_w, wi, wo, out):
    out_rows = out.rearrange("b n d -> (b n) d")
    rows = nc.dram_tensor("rows", (TOKENS, RW), F32, kind="Internal").ap()
    ctx = ExitStack()
    with ctx:
        def sb(name, shape, dt=F32):
            return ctx.enter_context(nc.sbuf_tensor(name, shape, dt))

        def sem(name):
            return ctx.enter_context(nc.semaphore(name))

        bank = [ctx.enter_context(nc.psum_tensor(f"bank{i}", [P, 512], F32)) for i in range(8)]

        ident = sb("ident", [P, P])
        tri = sb("tri", [P, P], BF16)
        ones_bf = sb("ones_bf", [P, P], BF16)
        ones_mean = sb("ones_mean", [G2, P])
        head_mask = sb("head_mask", [G2, G2])
        lo_rows = sb("lo_rows", [P, 2])
        hi_coef = sb("hi_coef", [P, 2])
        ksum_sel = sb("ksum_sel", [NG, G2])
        const_row = sb("const_row", [1, 3 * D])
        one_hot_row = sb("one_hot_row", [1, RA])
        half_pi = sb("half_pi", [P, 1])
        eps_tile = sb("eps_tile", [P, 1])
        expert_key = sb("expert_key", [P, TG, E])
        term_sign = sb("term_sign", [P, 27])
        iota_lane = sb("iota_lane", [P, P])
        iota_p = sb("iota_p", [P, 1])
        iota_t = sb("iota_t", [P, TILES])
        iota_blk = sb("iota_blk", [1, NBLK, E])

        wfs = sb("wfs", [G2, 2, NF])
        wf_c = sb("wf_c", [G2, 2, 3, NG])
        wf_b = sb("wf_b", [G2, 2, 3, NF])
        wq_in = sb("wq_in", [G2, 2, 3 * D])
        pw = sb("pw", [G2, 2, D])
        pr = sb("pr", [G2, 2, DL])
        ir = sb("ir", [G2, 2, DL])
        pb = sb("pb", [G2, 2])
        wa = sb("wa", [RA, 2 * D], F32R)
        wa_lo = sb("wa_lo", [RA, 2 * D])
        vw = sb("vw", [NG, D])
        wb = sb("wb", [RT, DL], F32R)
        wb_lo = sb("wb_lo", [RT, DL])
        outer = sb("outer", [G2, 2, 16 + 49])
        quad = sb("quad", [P, 16 + 49])

        ids = sb("ids", [P, B], I32)
        crv = sb("crv", [P, 2, 2], I32)
        pix_id = sb("pix_id", [P, 2], I32)
        prm = sb("prm", [P, B, NPAR])
        kk = sb("kk", [P, B, NPAR])
        sn = sb("sn", [P, B, NPAR])
        cs = sb("cs", [P, B, NPAR])
        fz = sb("fz", [P, B, NQ, 4])
        fn = sb("fn", [P, B, NQ, 4])
        ns = sb("ns", [P, B, NQ])
        tr = sb("tr", [P, B, NQ, 8])
        base = sb("base", [P, B, 12])
        vs = sb("vs", [P, 4, B, 24])
        tmp = [sb(f"tmp{i}", [P, B, 24]) for i in range(2)]
        zs = sb("zs", [P, B, 4])
        ezt = sb("ezt", [P, 4, B, 4])
        w5 = sb("w5", [P, B, 12])
        ez = sb("ez", [P, NQ, B])
        co = sb("co", [P, B, NQ, 3])
        gx = sb("gx", [P, B, 5, 9])
        cx = sb("cx", [P, B, 5, 9])
        zp = sb("zp", [P, B, NQ])
        qv = sb("qv", [P, B, NQ])
        rv = sb("rv", [P, B, NQ])
        xt = sb("xt", [P, B, 8])
        z345 = sb("z345", [P, B, 2])
        p01 = sb("p01", [P, B, 16])
        d25 = sb("d25", [P, B, 8])
        gp = sb("gp", [P, B, 27])
        gd = sb("gd", [P, B, 27])
        c27 = sb("c27", [P, B, 27])
        ex = sb("ex", [P, B, NQ])

        pixg = sb("pixg", [P, 2, B * CH])
        gt = sb("gt", [P, B, NT, NF])
        gs = sb("gs", [P, B, NT, NG])
        sa = sb("sa", [P, B, NT, RT])
        vq = sb("vq", [P, B * 49])
        var = sb("var", [P, B, NT])
        rstd = sb("rstd", [P, B, NT])
        newt = sb("newt", [P, B, NT])

        qt = [sb(f"qt{i}", [G2 + 1, 2, NT * P]) for i in range(2)]
        kt = [sb(f"kt{i}", [P, NT, D]) for i in range(2)]
        kg = [sb(f"kg{i}", [NG, D]) for i in range(2)]
        kvm = [sb(f"kvm{i}", [G2, 2, G2]) for i in range(2)]
        dm = [sb(f"dm{i}", [G2 + 1, 2, NQ]) for i in range(2)]
        mb = [sb(f"mb{i}", [G2, 2, DL]) for i in range(2)]
        zr = [sb(f"zr{i}", [P, NT, 2, NQ]) for i in range(2)]
        zx = sb("zx", [P, NT, D])
        zt = [sb(f"zt{i}", [G2, 2, NT * P]) for i in range(2)]
        row = [sb(f"row{i}", [P, NT, RW]) for i in range(2)]
        dl = sb("dl", [P, NT, E])
        st6 = sb("st6", [P, NT, 6])
        mv = sb("mv", [P, NT, 2])
        std = [sb(f"std{i}", [P, NT]) for i in range(2)]
        mx = sb("mx", [P, NT])
        ge = sb("ge", [P, TILES, E])
        ohf = sb("ohf", [P, TG, E])
        key = sb("key", [P, TG])
        rank = sb("rank", [P, TG])
        carry = sb("carry", [P, E])
        carry_bf = sb("carry_bf", [P, E], BF16)
        earlier = sb("earlier", [P, E, TG])
        keep = sb("keep", [P, E, TG])
        before = sb("before", [P, E, TG], BF16)
        cnt = sb("cnt", [P, E])
        cnt_i = sb("cnt_i", [P, E], I32)
        blk_end = sb("blk_end", [P, E])
        first_tile = sb("first_tile", [P, E])
        r_i = sb("r_i", [P, TG], I32)
        lo_i = sb("lo_i", [P, TG], I32)
        hi_i = sb("hi_i", [P, TG], I32)
        lo_f = sb("lo_f", [P, TILES])
        tile_f = sb("tile_f", [P, TILES])
        lane_f = sb("lane_f", [P, NTILE])
        fill_f = sb("fill_f", [P, NTILE])
        cnt_j = sb("cnt_j", [P, E], I32)
        ones_e = sb("ones_e", [P, E])
        hi_f = sb("hi_f", [P, TILES])
        oh_all = sb("oh_all", [P, TILES, E], BF16)
        oh_lo = sb("oh_lo", [P, TILES, P], BF16)
        oh_hi = sb("oh_hi", [P, TILES, 3, NTILE], BF16)
        tl = sb("tl", [P, TILES, E])
        gidf = sb("gidf", [P, NTILE])
        sidf = sb("sidf", [P, NTILE])
        gid = sb("gid", [P, NTILE], I32)
        sid = sb("sid", [P, NTILE], I32)
        be = sb("be", [1, NBLK, E])
        bef = sb("bef", [1, NBLK])
        blk_expert = sb("blk_expert", [1, NBLK], I32)
        n_last = sb("n_last", [1, 1], I32)
        mark_act, mark_dve = sb("mark_act", [P, 4]), sb("mark_dve", [P, 4])
        fresh = sb("fresh", [1, NBLK], I32)
        last_pair = sb("last_pair", [1, 1], I32)
        raw = [sb(f"raw{i}", [P, W_COLS]) for i in range(2)]
        wh = [sb(f"wh{i}", [P, W_COLS], F32R) for i in range(2)]
        wl = [sb(f"wl{i}", [P, W_COLS], F32R) for i in range(2)]
        gtt = [wh[0][0:RT, i * NT * P:(i + 1) * NT * P] for i in range(3)]
        gr = [sb(f"gr{i}", [P, ST], I32) for i in range(2)]
        sr = [sb(f"sr{i}", [P, ST], I32) for i in range(2)]
        hs = [sb(f"hs{i}", [P, ST, RW]) for i in range(2)]
        xn = [sb(f"xn{i}", [P, ST, 256]) for i in range(2)]
        xh = [sb(f"xh{i}", [P, 2 * BLK], F32R) for i in range(2)]
        xl = [sb(f"xl{i}", [P, BLK], F32R) for i in range(2)]
        hh = [sb(f"hh{i}", [P, FC, BLK], F32R) for i in range(2)]
        hl = [sb(f"hl{i}", [P, FC, BLK], F32R) for i in range(2)]
        ed = [sb(f"ed{i}", [P, ST, E]) for i in range(2)]
        sume = [sb(f"sume{i}", [P, ST]) for i in range(2)]
        prob = [sb(f"prob{i}", [P, ST]) for i in range(2)]
        flat = sa[:, :, :, :].rearrange("p b t j -> p (b t j)")
        res, yr = ([flat[:, (2 * k + i) * ST * D:(2 * k + i + 1) * ST * D].rearrange("p (s d) -> p s d", s=ST)
                    for i in range(2)] for k in range(2))

        s_small = sem("s_small")
        s_wload = sem("s_wload")
        s_pixid = sem("s_pixid")
        s_pix = [sem(f"s_pix{n}") for n in range(2)]
        s_prm = sem("s_prm")
        s_const = sem("s_const")
        s_constv = sem("s_constv")
        s_pool = sem("s_pool")
        s_dve = sem("s_dve")
        s_act = sem("s_act")
        s_red = sem("s_red")
        s_abs = sem("s_abs")
        s_trig = sem("s_trig")
        s_bloch = sem("s_bloch")
        s_co = sem("s_co")
        s_ex = sem("s_ex")
        s_wmean = sem("s_wmean")
        s_wcent = sem("s_wcent")
        s_wprod = sem("s_wprod")
        s_wready = sem("s_wready")
        s_var = sem("s_var")
        s_sd = sem("s_sd")
        s_sa = sem("s_sa")
        s_t = sem("s_t")
        s_gtt = sem("s_gtt")
        s_q = sem("s_q")
        s_qt = sem("s_qt")
        s_k = sem("s_k")
        s_kt = sem("s_kt")
        s_kg = sem("s_kg")
        s_kgc = sem("s_kgc")
        s_kv = sem("s_kv")
        s_kvc = sem("s_kvc")
        s_m = sem("s_m")
        s_mc = sem("s_mc")
        s_den = sem("s_den")
        s_z = sem("s_z")
        s_zx = sem("s_zx")
        s_zt = sem("s_zt")
        s_qz = sem("s_qz")
        s_h = sem("s_h")
        s_bn = sem("s_bn")
        s_hc = sem("s_hc")
        s_v2 = sem("s_v2")
        s_sd2 = sem("s_sd2")
        s_oh = sem("s_oh")
        s_rk = sem("s_rk")
        s_done = sem("s_done")
        s_ranked = sem("s_ranked")
        s_lo = sem("s_lo")
        s_ohlo = sem("s_ohlo")
        s_ohlo_v = sem("s_ohlo_v")
        s_rows = [sem(f"s_rows{i}") for i in range(2)]
        s_ohhi = sem("s_ohhi")
        s_inv = sem("s_inv")
        s_tab = sem("s_tab")
        s_raw = [sem(f"s_raw{i}") for i in range(2)]
        s_load = sem("s_load")
        s_wh = sem("s_wh")
        s_wl = sem("s_wl")
        s_gidx = sem("s_gidx")
        s_issue = sem("s_issue")
        s_sidx = sem("s_sidx")
        s_hs = [sem(f"s_hs{i}") for i in range(2)]
        s_res = sem("s_res")
        s_xn = sem("s_xn")
        s_x = sem("s_x")
        s_xh = sem("s_xh")
        s_xl = sem("s_xl")
        s_u = sem("s_u")
        s_hh = sem("s_hh")
        s_hl = sem("s_hl")
        s_y = sem("s_y")
        s_exp = sem("s_exp")
        s_pr = sem("s_pr")
        s_yr = sem("s_yr")
        s_fin = [sem(f"s_fin{i}") for i in range(2)]

        def pairs(engine, body, last):
            for r in range(2):
                body(0, r, first=True)
            with engine.Fori(1, last) as j:
                for r in range(2):
                    body(j, r)
            for r in range(2):
                body(last, r, tail=True)

        def is_fresh(engine, b):
            return engine.value_load(fresh[0:1, bass.ds(b, 1)], min_val=0, max_val=1)

        def where_fresh(engine, b, r, part, opening, split, mark, done):
            if opening:
                split()
                return
            with engine.If(is_fresh(engine, b)):
                split()
            with engine.Else():
                mark(part, r).then_inc(done, 1)

        block_ = ctx.enter_context(nc.Block())

        K0, K1, MM, Q0, Q1, D0, D1, HB = bank
        HT = (HB, D0, D1)
        PP, YY, UU = bank[0], bank[7], bank[1:7]

        @block_.sync
        def _(sp):
            sp.dma_start(crv[:, :, :], curve.rearrange("(n p) c -> p n c", p=P)).then_inc(s_small, 16)
            sp.dma_start(ids[:, :], txt_ids).then_inc(s_small, 16)
            sp.dma_start(wfs[:, :, :], wf.rearrange("(g p) j -> p g j", g=2)).then_inc(s_wload, 16)
            sp.dma_start(ir[:, :, D:DL], router_w.rearrange("(g p) e -> p g e", g=2)).then_inc(s_wload, 16)
            sp.dma_start(pb[:, :], proj_b).then_inc(s_wload, 16)
            sp.dma_start(wq_in[:, :, :], qkv_wT.rearrange("(g p) d -> p g d", g=2)).then_inc(s_wload, 16)
            sp.dma_start(pw[:, :, :], proj_w.rearrange("(g p) d -> p g d", g=2)).then_inc(s_wload, 16)
            sp.dma_start(pr[:, :, 0:D], proj_wT.rearrange("(g p) d -> p g d", g=2)).then_inc(s_wload, 16)

            def load_weights(e, r):
                sp.dma_start(raw[r][:, 0:FF], wi[bass.ds(e, 1), 0:P, :]).then_inc(s_raw[r], 16)
                sp.dma_start(raw[r][0:64, FF:2 * FF], wi[bass.ds(e, 1), P:D, :]).then_inc(s_raw[r], 16)
                sp.dma_start(raw[r][64:P, FF:2 * FF], wi[bass.ds(e, 1), P:D, :]).then_inc(s_raw[r], 16)
                sp.dma_start(raw[r][:, 2 * FF:W_COLS].rearrange("p (c d) -> p c d", c=FC),
                             wo[bass.ds(e, 1), :, :].rearrange("o (c p) d -> (o p) c d", p=P))\
                  .then_inc(s_raw[r], 16)

            for b in range(B):
                sp.wait_ge(s_done, b + 1)
                sp.dma_start(rows[b * NT * P:(b + 1) * NT * P, :].rearrange("(t p) d -> p t d", p=P),
                             row[b % 2][:, :, :]).then_inc(s_rows[b % 2], 16)

            def block(j, r, first=False):
                b = 2 * j + r
                e = sp.value_load(blk_expert[0:1, bass.ds(b, 1)], min_val=0, max_val=E - 1)
                if first:
                    load_weights(e, r)
                    return
                sp.wait_ge(s_wh, 2 * b - 2)
                sp.sem_inc(s_load, 1)
                sp.wait_ge(s_wl, 2 * b - 2)
                sp.sem_inc(s_load, 1)
                with sp.If(is_fresh(sp, b)):
                    load_weights(e, r)
                with sp.Else():
                    sp.sem_inc(s_raw[r], 64)

            sp.wait_ge(s_tab, 1)
            end = sp.value_load(last_pair[0:1, 0:1], min_val=0, max_val=NBLK // 2 - 1 - LAST_MIN) + LAST_MIN
            for r in range(2):
                block(0, r, True)
            with sp.Fori(1, end + 1) as j:
                for r in range(2):
                    block(j, r)

        @block_.gpsimd
        def _(pool):
            ch = Chain(pool, s_pool)
            g = nc.gpsimd
            g.memset(ones_mean[:, :], 1.0 / D).then_inc(s_const, 1)
            ch.step(g.memset(ident[:, :], 0.0))
            ch.step(g.memset(head_mask[:, :], 1.0))
            ch.step(g.memset(lo_rows[:, :], 1.0))
            ch.step(g.memset(ksum_sel[:, :], 1.0))
            ch.step(g.memset(tri[:, :], 1.0))
            ch.step(g.memset(one_hot_row[:, :], 0.0))
            ch.step(g.memset(const_row[:, :], 0.0))
            ch.step(g.memset(ir[:, :, 0:D], 0.0))
            ch.wait()
            g.memset(const_row[:, 0:2 * D], SCALE).then_inc(s_const, 1)
            g.memset(ap(one_hot_row[:, :], NF, [[NG, 3]]), 1.0).then_inc(s_const, 1)
            pool.wait_ge(s_small, 32)
            for b in range(B):
                g.indirect_dma_start(out=prm[:, b, :], out_offset=None, in_=qparams,
                                     in_offset=bass.IndirectOffsetOnAxis(ap=ids[:, b:b + 1].bitcast(U32), axis=0),
                                     bounds_check=VOCAB - 1, oob_is_err=False).then_inc(s_prm, 16)
            pool.wait_ge(s_pixid, 1)
            for n in range(2):
                g.indirect_dma_start(out=pixg[:, n, :], out_offset=None, in_=pixels,
                                     in_offset=bass.IndirectOffsetOnAxis(ap=pix_id[:, n:n + 1].bitcast(U32), axis=0),
                                     bounds_check=IMG * IMG - 1, oob_is_err=False).then_inc(s_pix[n], 16)
            g.affine_select(out=ident[:, :], in_=ident[:, :], compare_op=ALU.not_equal, fill=1.0, base=0,
                            pattern=[[-1, P]], channel_multiplier=1).then_inc(s_const, 1)
            g.affine_select(out=ir[:, :, 0:D], in_=ir[:, :, 0:D], compare_op=ALU.not_equal, fill=1.0, base=0,
                            pattern=[[G2, 2], [-1, D]], channel_multiplier=1).then_inc(s_const, 1)
            g.affine_select(out=tri[:, :], in_=tri[:, :], compare_op=ALU.is_ge, fill=0.0, base=0,
                            pattern=[[1, P]], channel_multiplier=-1).then_inc(s_const, 1)
            hm = head_mask[:, :].rearrange("p (h d) -> p h d", d=HD)
            ch.link(g.affine_select(out=hm, in_=hm, compare_op=ALU.is_ge, fill=0.0, base=0,
                                    pattern=[[-HD, NQ], [0, HD]], channel_multiplier=1))
            g.affine_select(out=hm, in_=hm, compare_op=ALU.is_ge, fill=0.0, base=HD - 1,
                            pattern=[[HD, NQ], [0, HD]], channel_multiplier=-1).then_inc(s_const, 1)
            g.affine_select(out=ksum_sel[:, :], in_=ksum_sel[:, :], compare_op=ALU.is_ge, fill=0.0, base=-NF,
                            pattern=[[0, G2]], channel_multiplier=1).then_inc(s_const, 1)
            for j, first in enumerate((2 * NG, RB0 + 2 * NF)):
                g.affine_select(out=lo_rows[:, j:j + 1], in_=lo_rows[:, j:j + 1], compare_op=ALU.is_ge, fill=0.0,
                                base=-first, pattern=[[0, 1]], channel_multiplier=1).then_inc(s_const, 1)
            g.iota(iota_lane[:, :], pattern=[[1, P]], base=0, channel_multiplier=0,
                   allow_small_or_imprecise_dtypes=True).then_inc(s_const, 1)
            g.iota(iota_p[:, :], pattern=[[0, 1]], base=0, channel_multiplier=1,
                   allow_small_or_imprecise_dtypes=True).then_inc(s_const, 1)
            g.iota(iota_t[:, :], pattern=[[1, TILES]], base=0, channel_multiplier=0,
                   allow_small_or_imprecise_dtypes=True).then_inc(s_const, 1)
            g.iota(iota_blk[:, :, :], pattern=[[1, NBLK], [0, E]], base=0, channel_multiplier=0,
                   allow_small_or_imprecise_dtypes=True).then_inc(s_const, 1)
            g.iota(expert_key[:, :, :], pattern=[[0, TG], [-1, E]], base=E, channel_multiplier=0,
                   allow_small_or_imprecise_dtypes=True).then_inc(s_const, 1)

            pool.wait_ge(s_trig, 2)
            pool.wait_ge(s_bloch, 1)

            def th(a, layer):
                return a[:, :, :].rearrange("p t (l q r) -> p t l q r", l=LAYERS, r=2)[:, :, layer, :, 0]

            def ph(a, layer):
                return a[:, :, :].rearrange("p t (l q r) -> p t l q r", l=LAYERS, r=2)[:, :, layer, :, 1]

            def mul(o, a, b_):
                return g.tensor_tensor(o, a, b_, ALU.mult)

            def F(j, c, n=1):
                v = fz[:, :, j:j + n, c]
                return v

            def N(j, n=1):
                return fn[:, :, j:j + n, 3]

            ch.step(mul(co[:, :, :, 0], ph(cs, 1), th(cs, 1)))
            ch.step(mul(co[:, :, :, 1], ph(cs, 1), th(sn, 1)))
            ch.step(g.tensor_scalar(co[:, :, :, 2], ph(sn, 1), -1.0, None, ALU.mult))
            ch.step(g.tensor_copy(zp[:, :, 1:2], F(0, 1)))
            ch.step(g.tensor_copy(qv[:, :, 1:4], F(3, 2, 3)))
            ch.step(mul(qv[:, :, 4:5], F(0, 2), F(1, 2)))
            ch.step(mul(xt[:, :, 0:1], N(0), F(1, 3)))
            ch.step(mul(z345[:, :, 0:1], F(3, 1), F(4, 1)))
            ch.step(mul(xt[:, :, 1:2], F(2, 1), F(3, 1)))
            for i in range(2, 5):
                ch.wait()
                ch.step(mul(zp[:, :, i:i + 1], zp[:, :, i - 1:i], F(i - 1, 1)))
            ch.step(mul(z345[:, :, 1:2], z345[:, :, 0:1], F(5, 1)))
            ch.step(mul(rv[:, :, 4:5], xt[:, :, 0:1], xt[:, :, 1:2]))
            ch.wait()
            ch.step(mul(rv[:, :, 1:4], zp[:, :, 1:4], F(3, 2, 3)))
            pool.sem_inc(s_co, 1)
            X4, Y4, Z4, N4 = F(1, 2, 4), F(1, 3, 4), F(1, 1, 4), N(1, 4)
            X5, Y5, Z5, N5 = F(2, 2, 4), F(2, 3, 4), F(2, 1, 4), N(2, 4)
            ch.step(mul(gx[:, :, 1:5, 0], X4, qv[:, :, 1:5]))
            ch.step(mul(gx[:, :, 1:5, 1], zp[:, :, 1:5], N4))
            ch.step(mul(gx[:, :, 1:5, 2], Y4, Z5))
            ch.step(mul(gx[:, :, 1:5, 3], Z4, X5))
            ch.step(g.tensor_copy(gx[:, :, 1:5, 4], Z5))
            ch.step(mul(gx[:, :, 1:5, 5], Y5, qv[:, :, 1:5]))
            ch.step(mul(gx[:, :, 1:5, 7], X4, Y5))
            ch.wait()
            ch.step(mul(gx[:, :, 1:5, 1], gx[:, :, 1:5, 1], Y5))
            ch.step(mul(gx[:, :, 1:5, 2], gx[:, :, 1:5, 2], rv[:, :, 1:5]))
            ch.step(mul(gx[:, :, 1:5, 3], gx[:, :, 1:5, 3], rv[:, :, 1:5]))
            ch.step(mul(gx[:, :, 1:5, 6], Y4, rv[:, :, 1:5]))
            ch.step(mul(gx[:, :, 1:5, 8], gx[:, :, 1:5, 0], Z5))
            ch.wait()
            ch.step(g.tensor_scalar(gx[:, :, 1:5, 8], gx[:, :, 1:5, 8], -1.0, None, ALU.mult))
            zz = z345[:, :, 1:2]
            ch.step(mul(xt[:, :, 2:3], F(2, 1), zz))
            ch.step(mul(xt[:, :, 3:4], F(2, 3), zz))
            ch.step(mul(xt[:, :, 4:5], F(0, 3), F(1, 1)))
            ch.step(mul(xt[:, :, 5:6], F(0, 1), F(1, 2)))
            ch.step(mul(xt[:, :, 6:7], F(0, 2), F(1, 1)))
            ch.step(mul(xt[:, :, 7:8], F(0, 3), F(1, 2)))
            ch.wait()
            ch.step(mul(gx[:, :, 0:1, 0], F(0, 2), F(2, 2)))
            ch.step(mul(gx[:, :, 0:1, 1], N(0), F(1, 3)))
            ch.step(mul(gx[:, :, 0:1, 2], xt[:, :, 4:5], F(2, 2)))
            ch.step(mul(gx[:, :, 0:1, 3], N(1), xt[:, :, 3:4]))
            ch.step(mul(gx[:, :, 0:1, 4], F(0, 1), xt[:, :, 2:3]))
            ch.step(mul(gx[:, :, 0:1, 5], xt[:, :, 5:6], xt[:, :, 3:4]))
            ch.step(mul(gx[:, :, 0:1, 6], xt[:, :, 6:7], xt[:, :, 3:4]))
            ch.step(mul(gx[:, :, 0:1, 7], xt[:, :, 7:8], xt[:, :, 2:3]))
            ch.step(mul(gx[:, :, 0:1, 8], F(0, 3), xt[:, :, 3:4]))
            for s in range(3):
                ch.step(mul(cx[:, :, :, 3 * s:3 * s + 3],
                            co[:, :, 0:5, s:s + 1].to_broadcast([P, B, 5, 3]), co[:, :, 1:6, :]))
            ch.wait()
            g.tensor_tensor(gx[:, :, :, :], gx[:, :, :, :], cx[:, :, :, :], ALU.mult).then_inc(s_ex, 1)
            for k in range(2):
                pool.wait_ge(s_lo, k + 1)
                for n in range(k * TG, TG if k == 0 else POOL_TILES):
                    g.tensor_scalar(oh_lo[:, n, :], iota_lane[:, :], lo_f[:, n:n + 1], None, ALU.is_equal)\
                     .then_inc(s_ohlo, 1)

            def gather(j, r, first=False):
                b = 2 * j + r
                if not first:
                    pool.wait_ge(s_xn, 4 * b - 4)
                    pool.wait_ge(s_exp, 2 * b - 2)
                    pool.wait_ge(s_res, b - 1)
                g.tensor_copy(gr[r][:, :], gid[:, bass.ds(ST * b, ST)]).then_inc(s_gidx, 1)
                pool.wait_ge(s_gidx, b + 1)
                pool.sem_inc(s_issue, 1)
                for s_ in range(ST):
                    g.indirect_dma_start(out=hs[r][:, s_, :], out_offset=None, in_=rows,
                                         in_offset=bass.IndirectOffsetOnAxis(
                                             ap=gr[r][:, s_:s_ + 1].bitcast(U32), axis=0),
                                         bounds_check=TOKENS - 1, oob_is_err=False).then_inc(s_hs[r], 16)

            def scatter(j, r, first=False):
                b = 2 * j + r
                if not first:
                    pool.wait_ge(s_fin[r], 16 * ST * j)
                g.tensor_copy(sr[r][:, :], sid[:, bass.ds(ST * b, ST)]).then_inc(s_sidx, 1)
                pool.wait_ge(s_sidx, b + 1)
                pool.wait_ge(s_yr, ST * b + ST)
                pool.sem_inc(s_issue, 1)
                for s_ in range(ST):
                    g.indirect_dma_start(out=out_rows,
                                         out_offset=bass.IndirectOffsetOnAxis(
                                             ap=sr[r][:, s_:s_ + 1].bitcast(U32), axis=0),
                                         in_=yr[r][:, s_, :], in_offset=None, bounds_check=TOKENS - 1,
                                         oob_is_err=False).then_inc(s_fin[r], 16)

            def block(j, r, first=False, tail=False):
                if not tail:
                    gather(j + 1, r)
                scatter(j, r, first)

            pool.wait_ge(s_tab, 1)
            for r in range(2):
                pool.wait_ge(s_rows[r], 16 * B // 2)
            last = pool.value_load(last_pair[0:1, 0:1], min_val=0, max_val=NBLK // 2 - 1 - LAST_MIN) + LAST_MIN
            gather(0, 0, True)
            gather(0, 1, True)
            pairs(pool, block, last)
            for r in range(2):
                pool.wait_ge(s_fin[r], 16 * ST * (last + 1))

        @block_.scalar
        def _(act):
            a = nc.scalar
            ch = Chain(act, s_act)
            act.wait_ge(s_constv, 2)
            act.wait_ge(s_red, 1)
            a.activation(sn[:, :, :], prm[:, :, :], ACT.Sin).then_inc(s_trig, 1)
            act.wait_ge(s_red, 2)
            a.activation(cs[:, :, :], kk[:, :, :], ACT.Sin, bias=half_pi[:, :], scale=-1.0).then_inc(s_trig, 1)
            act.wait_ge(s_var, 1)
            a.activation(rstd[:, :, :], var[:, :, :], ACT.Sqrt, bias=eps_tile[:, :]).then_inc(s_sd, 1)

            def features(b):
                act.wait_ge(s_t, b + 1)
                if b >= 3:
                    act.wait_ge(s_h, NT * (b - 2))
                a.activation(gtt[b % 3], K0[0:RT, 0:NT * P], ACT.Copy).then_inc(s_gtt, 1)

            def deviation(b):
                act.wait_ge(s_v2, b + 1)
                a.activation(std[b % 2][:, :], mv[:, :, 1], ACT.Sqrt, bias=eps_tile[:, :]).then_inc(s_sd2, 1)

            def h2(b):
                r = b % 2
                for t in range(NT):
                    act.wait_ge(s_h, b * NT + t + 1)
                    if t == 0 and b >= 2:
                        act.wait_ge(s_rows[r], 16 * (b // 2))
                    a.activation(row[r][:, t, 0:DL], HT[t][:, 0:DL], ACT.Copy).then_inc(s_hc, 1)

            def m_copy(b):
                r = b % 2
                act.wait_ge(s_m, b + 1)
                a.activation(mb[r][:, :, :], MM[0:G2, 0:2 * DL].rearrange("p (g d) -> p g d", g=2), ACT.Copy)\
                 .then_inc(s_mc, 1)

            features(0)
            features(1)
            for b in range(B):
                m_copy(b)
                if b:
                    deviation(b - 1)
                act.wait_ge(s_z, b + 1)
                if b:
                    act.wait_ge(s_zt, 2 * b)
                a.activation(zx[:, :, :].rearrange("p t (k j) -> p (t k) j", j=HD),
                             ap(zr[b % 2][:, :, :, :], 0, [[1, NT * 2 * NQ], [0, HD]]), ACT.Copy).then_inc(s_zx, 1)
                if b + 2 < B:
                    features(b + 2)
                h2(b)
            deviation(B - 1)

            def mark(part, r):
                c = 2 * r + part
                return a.activation(mark_act[:, c:c + 1], half_pi[:, :], ACT.Copy)

            def prepare(j, r, b, opening=False):
                act.wait_ge(s_hs[r], 16 * ST * (j + 1))
                if not opening:
                    act.wait_ge(s_exp, ST * b - ST)
                    act.wait_ge(s_pr, b - 1)
                    act.wait_ge(s_yr, ST * b - ST)
                for s_ in range(ST):
                    a.activation(ed[r][:, s_, :], hs[r][:, s_, C_D:C_D + E], ACT.Exp,
                                 accum_out=sume[r][:, s_:s_ + 1]).then_inc(s_exp, 1)
                a.activation(res[r][:, :, :], hs[r][:, :, 0:D], ACT.Copy).then_inc(s_res, 1)

            def split(j, r, b, opening=False):
                act.wait_ge(s_x, b + 1)
                a.activation(xh[r][:, :], PP[:, :], ACT.Copy).then_inc(s_xh, 1)

                def high_up():
                    act.wait_ge(s_raw[r], 64 * (j + 1))
                    if not opening:
                        act.wait_ge(s_y, b - 1)
                    a.activation(wh[r][:, 0:2 * FF], raw[r][:, 0:2 * FF], ACT.Copy).then_inc(s_wh, 1)

                where_fresh(act, b, r, 0, opening, high_up, mark, s_wh)

            def block(j, r, first=False, tail=False):
                b = 2 * j + r
                opening = first and r == 0
                nxt = (j, 1) if r == 0 else (j + 1, 0)
                if not (tail and r == 1):
                    prepare(*nxt, b + 1, opening)
                for c in range(FC // 2):
                    act.wait_ge(s_u, 3 * b + c + 1)
                    if c == 0 and not first:
                        act.wait_ge(s_y, b - 1)
                    a.activation(hh[r][:, 2 * c:2 * c + 2, :],
                                 UU[3 * r + c][:, :].rearrange("p (c t) -> p c t", c=2), ACT.Relu).then_inc(s_hh, 1)
                    if c == 0:
                        def high_down():
                            a.activation(wh[r][:, 2 * FF:W_COLS], raw[r][:, 2 * FF:W_COLS], ACT.Copy)\
                             .then_inc(s_wh, 1)

                        where_fresh(act, b, r, 1, first, high_down, mark, s_wh)
                if not (tail and r == 1):
                    split(*nxt, b + 1, opening)

            act.wait_ge(s_tab, 1)
            last = act.value_load(last_pair[0:1, 0:1], min_val=0, max_val=NBLK // 2 - 1 - LAST_MIN) + LAST_MIN
            prepare(0, 0, 0, True)
            split(0, 0, 0, True)
            pairs(act, block, last)

        @block_.vector
        def _(v):
            ch = Chain(v, s_dve)
            d = nc.vector

            def mul(o, a, b_):
                return d.tensor_tensor(o, a, b_, ALU.mult)

            d.memset(half_pi[:, :], float(np.pi / 2)).then_inc(s_constv, 1)
            d.memset(eps_tile[:, :], LN_EPS).then_inc(s_constv, 1)
            ch.step(d.memset(ones_bf[:, :], 1.0))
            ch.step(d.memset(ones_e[:, :], 1.0))
            ch.step(d.memset(fz[:, :, :, 0], 1.0))
            ch.step(d.memset(fn[:, :, :, 0], 1.0))
            ch.step(d.memset(carry[:, :], 0.0))
            ch.step(d.memset(keep[:, :, 0:1], 0.0))
            ch.step(d.memset(keep[:, :, 1:TG], 1.0))
            ch.step(d.memset(gt[:, :, :, :], 0.0))
            ch.step(d.memset(sa[:, :, :, RA:RB0], 0.0))
            ch.step(d.memset(gs[:, :, :, NF], 1.0))
            ch.step(d.memset(wf_c[:, :, :, NF], 0.0))
            ch.step(d.memset(zs[:, :, 3], 1.0))
            ch.step(d.memset(term_sign[:, :], 1.0))
            for i in range(2):
                ch.step(d.memset(qt[i][G2:G2 + 1, :, :], 1.0))
                ch.step(d.memset(dm[i][G2:G2 + 1, :, :], DEN_EPS))
            ch.wait()
            ch.step(d.memset(gt[:, :, 0:2, ONE_IMG], 1.0))
            ch.step(d.memset(gt[:, :, 2, ONE_TXT], 1.0))
            for i, (_, _, sign) in enumerate(x5_terms()):
                if sign < 0:
                    ch.step(d.memset(term_sign[:, i:i + 1], -1.0))
            v.wait_ge(s_small, 32)
            d.scalar_tensor_tensor(pix_id[:, :], crv[:, :, 1], float(IMG), crv[:, :, 0], ALU.mult, ALU.add)\
             .then_inc(s_pixid, 1)

            v.wait_ge(s_prm, 16 * B)
            ch.link(d.tensor_scalar(kk[:, :, :], prm[:, :, :], float(1 / (2 * np.pi)), MAGIC, ALU.mult, ALU.add))
            ch.link(d.tensor_scalar(kk[:, :, :], kk[:, :, :], -MAGIC, None, ALU.add))
            ch.link(d.scalar_tensor_tensor(prm[:, :, :], kk[:, :, :], -TWO_PI_HI, prm[:, :, :], ALU.mult, ALU.add))
            ch.link(d.scalar_tensor_tensor(prm[:, :, :], kk[:, :, :], -float(TWO_PI_LO), prm[:, :, :],
                                           ALU.mult, ALU.add))
            d.tensor_scalar(prm[:, :, :], prm[:, :, :], PI, -PI, ALU.min, ALU.max).then_inc(s_red, 1)
            v.wait_ge(s_red, 1)
            d.scalar_tensor_tensor(kk[:, :, :], prm[:, :, :], -1.0, prm[:, :, :], ALU.mult, ALU.max)\
             .then_inc(s_red, 1)

            v.wait_ge(s_wload, 96)
            v.wait_ge(s_wmean, 1)
            mean_w = bank[0][0:G2, 0:NF + E]
            for gi in range(2):
                for c in range(3):
                    ch.step(d.tensor_tensor(wf_c[:, gi, c, 0:NF], wfs[:, gi, :], mean_w[:, 0:NF], ALU.subtract))
                    ch.step(d.tensor_copy(wf_b[:, gi, c, :], wfs[:, gi, :]))
                ch.step(d.tensor_tensor(ir[:, gi, D:DL], ir[:, gi, D:DL], mean_w[:, NF:NF + E], ALU.subtract))
            ch.wait()
            for gi in range(2):
                for c in range(3):
                    for col in (ONE_IMG, ONE_TXT):
                        ch.step(d.tensor_tensor(wf_b[:, gi, c, col:col + 1], wf_b[:, gi, c, col:col + 1],
                                                pb[:, gi:gi + 1], ALU.add))
                for o, first, n in ((0, 0, 4), (16, 4, 7)):
                    w_ = wf_c[:, gi, 0, first:first + n]
                    ch.step(mul(outer[:, gi, o:o + n * n].rearrange("p (j k) -> p j k", j=n),
                                ap(w_, 0, [[1, n], [0, n]]), ap(w_, 0, [[0, n], [1, n]])))
            ch.wait()
            v.sem_inc(s_wcent, 1)
            def th(a, layer):
                return a[:, :, :].rearrange("p t (l q r) -> p t l q r", l=LAYERS, r=2)[:, :, layer, :, 0]

            def ph(a, layer):
                return a[:, :, :].rearrange("p t (l q r) -> p t l q r", l=LAYERS, r=2)[:, :, layer, :, 1]

            v.wait_ge(s_trig, 2)
            ch.step(d.tensor_copy(fz[:, :, :, 1], th(cs, 0)))
            ch.step(mul(fz[:, :, :, 2], th(sn, 0), ph(cs, 0)))
            ch.step(mul(fz[:, :, :, 3], th(sn, 0), ph(sn, 0)))
            ch.wait()
            ch.step(d.tensor_copy(fn[:, :, :, 1:3], fz[:, :, :, 1:3]))
            ch.step(d.tensor_scalar(fn[:, :, :, 3], fz[:, :, :, 3], -1.0, None, ALU.mult))
            ch.step(d.tensor_scalar(ns[:, :, :], th(sn, 1), -1.0, None, ALU.mult))
            ch.wait()
            v.sem_inc(s_bloch, 1)

            c1 = th(cs, 1)
            ch.step(mul(tr[:, :, :, 0:4], fn[:, :, :, :], ap(c1, 0, [[NPAR, B], [2, NQ], [0, 4]])))
            ch.step(mul(tr[:, :, :, 4:6], fz[:, :, :, 2:4], ap(ns[:, :, :], 0, [[NQ, B], [1, NQ], [0, 2]])))
            ch.step(mul(tr[:, :, :, 6:8], fz[:, :, :, 0:2], ap(ns[:, :, :], 0, [[NQ, B], [1, NQ], [0, 2]])))
            f0, n0 = fz[:, :, 0, :], fn[:, :, 0, :]
            cc = ap(c1, 0, [[NPAR, B], [0, 2]])
            s0 = ns[:, :, 0:1].to_broadcast([P, B, 2])
            ch.step(mul(base[:, :, 0:2], ap(f0, 1, [[4 * NQ, B], [-1, 2]]), cc))
            ch.step(mul(base[:, :, 2:4], f0[:, :, 2:4], s0))
            ch.step(d.tensor_copy(base[:, :, 4:6], f0[:, :, 0:2]))
            ch.step(mul(base[:, :, 6:8], ap(n0, 3, [[4 * NQ, B], [-1, 2]]), cc))
            ch.step(mul(base[:, :, 8:10], f0[:, :, 0:2], s0))
            ch.step(d.tensor_copy(base[:, :, 10:12], f0[:, :, 2:4]))
            ch.wait()
            for f in range(2):
                for fp in range(2):
                    o, st_ = (4 * fp + 2 * f, 1) if f else (4 * fp + 1, -1)
                    ch.step(mul(ap(vs[:, 0, :, :], o, [[24, B], [8, 3], [st_, 2]]),
                                ap(base[:, :, :], 2 * fp, [[12, B], [4, 3], [1, 2]]),
                                ap(tr[:, :, 1, :], 4 * f + 2 * fp, [[8 * NQ, B], [0, 3], [1, 2]])))
            ch.wait()
            for k in range(2, 5):
                for f in range(2):
                    ch.step(mul(ap(tmp[f][:, :, :], 0, [[24, B], [4, 6], [1, 4]]),
                                ap(vs[:, k - 2, :, :], 0, [[24, B], [4, 6], [1, 4]]),
                                ap(tr[:, :, k, :], 4 * f, [[8 * NQ, B], [0, 6], [1, 4]])))
                ch.wait()
                for f in range(2):
                    o, st_ = (2, 1) if f else (1, -1)
                    ch.step(d.tensor_tensor(ap(vs[:, k - 1, :, :], o, [[4, 6 * B], [st_, 2]]),
                                            ap(tmp[f][:, :, :], 0, [[4, 6 * B], [1, 2]]),
                                            ap(tmp[f][:, :, :], 2, [[4, 6 * B], [1, 2]]), ALU.add))
                ch.wait()
            ch.step(d.tensor_copy(zs[:, :, 2:3], fz[:, :, 5, 1:2]))
            ch.link(mul(zs[:, :, 1:2], fz[:, :, 4, 1:2], fz[:, :, 5, 1:2]))
            ch.step(mul(zs[:, :, 0:1], fz[:, :, 3, 1:2], zs[:, :, 1:2]))
            for a_ in range(2):
                o = 4 if a_ else 1
                c_o = 0 if a_ else 1
                ch.step(mul(ap(ezt[:, :, :, :], 2 * a_, [[4 * B, 4], [4, B], [1, 2]]),
                            ap(vs[:, :, :, :], o, [[24 * B, 4], [24, B], [2, 2]]),
                            ap(fn[:, :, 2, :], c_o, [[4, 4], [4 * NQ, B], [2, 2]])))
            for a_, vo, vstep, to, tstep in ((0, 0, 13, 0, 5), (1, 5, 11, 1, 3), (2, 9, 11, 1, 3)):
                ch.step(mul(ap(w5[:, :, :], 4 * a_, [[12, B], [2, 2], [1, 2]]),
                            ap(vs[:, 3, :, :], vo, [[24, B], [vstep, 2], [2, 2]]),
                            ap(tr[:, :, 5, :], to, [[8 * NQ, B], [tstep, 2], [2, 2]])))
            ch.wait()
            ch.step(mul(ap(ezt[:, :, :, :], 0, [[4 * B, 4], [4, B], [1, 2]]),
                        ap(ezt[:, :, :, :], 0, [[4 * B, 4], [4, B], [1, 2]]),
                        ap(zs[:, :, :], 0, [[1, 4], [4, B], [0, 2]])))
            ch.step(d.tensor_reduce(out=ez[:, 0, :], in_=w5[:, :, 8:12], axis=AX.X, op=ALU.add))
            ch.step(d.tensor_reduce(out=ez[:, 5, :], in_=w5[:, :, 0:8], axis=AX.X, op=ALU.add))
            ch.wait()
            ch.step(d.tensor_reduce(out=ez[:, 1:5, :], in_=ezt[:, :, :, :], axis=AX.X, op=ALU.add))
            v.wait_ge(s_co, 1)
            for c in range(4):
                ch.step(mul(p01[:, :, 4 * c:4 * c + 4], fz[:, :, 0, c:c + 1].to_broadcast([P, B, 4]), fz[:, :, 1, :]))
            for f1 in range(2):
                ch.step(mul(d25[:, :, 4 * f1:4 * f1 + 4].rearrange("p t (f w) -> p t f w", w=2),
                            ap(fz[:, :, 2, 2 * f1:2 * f1 + 2], 0, [[4 * NQ, B], [0, 2], [1, 2]]),
                            fz[:, :, 5, :].rearrange("p t (f w) -> p t f w", w=2)))
            ch.wait()
            ch.link(mul(ap(d25[:, :, :], 1, [[8, B], [2, 4]]), ap(d25[:, :, :], 1, [[8, B], [2, 4]]),
                        z345[:, :, 0:1].to_broadcast([P, B, 4])))
            terms = x5_terms()
            for i5, c5 in enumerate((0, 2, 1)):
                ch.step(mul(ap(c27[:, :, :], 3 * i5, [[27, B], [9, 3], [1, 1]]),
                            ap(co[:, :, :, :], 3, [[18, B], [1, 3], [1, 1]]),
                            ap(co[:, :, :, :], 15 + c5, [[18, B], [0, 3], [1, 1]])))
            ch.wait()
            for i0, c0 in ((2, 2), (1, 0), (0, 1)):
                ch.step(mul(ap(c27[:, :, :], i0, [[27, B], [3, 9]]), ap(c27[:, :, :], 0, [[27, B], [3, 9]]),
                            ap(co[:, :, :, :], c0, [[18, B], [0, 9]])))
                ch.wait()
            for dst, src, width, which in ((gp, p01, 16, 0), (gd, d25, 8, 1)):
                seq = [t[which] for t in terms]
                for i, n, dims in affine_runs(seq):
                    o = [[27, B]] + ([[dims[1][1], dims[0][1]], [1, dims[1][1]]] if len(dims) == 2 else [[1, n]])
                    ch.step(d.tensor_copy(ap(dst[:, :, :], i, o), ap(src[:, :, :], seq[i], [[width, B]] + dims)))
            ch.link(mul(c27[:, :, :], c27[:, :, :], ap(term_sign[:, :], 0, [[0, B], [1, 27]])))
            ch.link(mul(gp[:, :, :], gp[:, :, :], gd[:, :, :]))
            ch.link(mul(gp[:, :, :], gp[:, :, :], c27[:, :, :]))

            v.wait_ge(s_wprod, 1)
            ch.step(d.tensor_copy(quad[:, :], bank[1][:, 0:65]))
            ch.step(d.tensor_copy(vw[:, :], bank[3][0:NG, 0:D]))
            ch.step(d.tensor_copy(pr[:, :, D:DL], bank[1][0:G2, 128:128 + 2 * E].rearrange("p (g e) -> p g e", g=2)))
            ch.step(d.tensor_scalar(hi_coef[:, :], lo_rows[:, :], -2.0, 1.0, ALU.mult, ALU.add))
            ch.step(d.tensor_copy(wa[:, :], bank[2][0:RA, 0:2 * D]))
            ch.step(d.tensor_copy(wb[RB0:RT, :], bank[4][RB0:RT, 0:DL]))
            ch.step(d.tensor_scalar(wa_lo[:, :], bank[2][0:RA, 0:2 * D], lo_rows[0:RA, 0:1], None, ALU.mult))
            ch.step(d.tensor_scalar(wb_lo[RB0:RT, :], bank[4][RB0:RT, 0:DL], lo_rows[RB0:RT, 1:2], None, ALU.mult))
            ch.wait()
            d.scalar_tensor_tensor(wa[:, :], wa[:, :].bitcast(F32), hi_coef[0:RA, 0:1], wa_lo[:, :],
                                   ALU.mult, ALU.add).then_inc(s_wready, 1)
            d.scalar_tensor_tensor(wb[RB0:RT, :], wb[RB0:RT, :].bitcast(F32), hi_coef[RB0:RT, 1:2], wb_lo[RB0:RT, :],
                                   ALU.mult, ALU.add).then_inc(s_wready, 1)

            for n in range(2):
                v.wait_ge(s_pix[n], 16)
                ch.step(d.tensor_copy(gt[:, :, n, 0:CH], pixg[:, n, :].rearrange("p (b c) -> p b c", c=CH)))
            ch.wait()
            for n in range(2):
                f = gt[:, :, n, 0:4]
                q4 = ap(vq[:, :], 0, [[16, B], [4, 4], [1, 4]])
                ch.link(mul(q4, ap(f, 0, [[NT * NF, B], [1, 4], [0, 4]]), ap(f, 0, [[NT * NF, B], [0, 4], [1, 4]])))
                q1 = ap(vq[:, :], 0, [[16, B], [1, 16]])
                ch.link(mul(q1, q1, ap(quad[:, :], 0, [[0, B], [1, 16]])))
                ch.link(d.tensor_reduce(out=var[:, :, n], in_=q1, axis=AX.X, op=ALU.add))

            v.wait_ge(s_ex, 1)
            ch.step(d.tensor_reduce(out=ex[:, :, 0:5], in_=gx[:, :, :, :], axis=AX.X, op=ALU.add))
            ch.step(d.tensor_reduce(out=ex[:, :, 5:6], in_=gp[:, :, :], axis=AX.X, op=ALU.add))
            ch.wait()
            ch.step(mul(ex[:, :, :], ex[:, :, :], th(sn, 2)))
            ch.step(mul(ns[:, :, :], ez[:, :, :].rearrange("p q t -> p t q"), th(cs, 2)))
            ch.wait()
            ch.link(d.tensor_tensor(gt[:, :, 2, 4:4 + NQ], ns[:, :, :], ex[:, :, :], ALU.subtract))

            f = gt[:, :, 2, 4:11]
            ch.link(mul(ap(vq[:, :], 0, [[49, B], [7, 7], [1, 7]]),
                        ap(f, 0, [[NT * NF, B], [1, 7], [0, 7]]), ap(f, 0, [[NT * NF, B], [0, 7], [1, 7]])))
            q1 = ap(vq[:, :], 0, [[49, B], [1, 49]])
            ch.link(mul(q1, q1, ap(quad[:, :], 16, [[0, B], [1, 49]])))
            d.tensor_reduce(out=var[:, :, 2], in_=q1, axis=AX.X, op=ALU.add).then_inc(s_var, 1)
            for t in range(NT):
                g_ = gt[:, :, t, :]
                hi = sa[:, :, t, RB0:RB0 + NF]
                ch.link(d.tensor_copy(hi.bitcast(F32R), g_))
                ch.step(d.tensor_tensor(sa[:, :, t, RB0 + NF:RB0 + 2 * NF], g_, hi, ALU.subtract))
                ch.step(d.tensor_copy(sa[:, :, t, RB0 + 2 * NF:RT], hi))
            v.wait_ge(s_sd, 1)
            ch.step(d.tensor_scalar(var[:, :, :], var[:, :, :], LN_EPS, -0.5, ALU.add, ALU.mult))
            ch.link(d.reciprocal(rstd[:, :, :], rstd[:, :, :]))
            ch.link(mul(newt[:, :, :], rstd[:, :, :], rstd[:, :, :]))
            ch.link(mul(newt[:, :, :], newt[:, :, :], var[:, :, :]))
            ch.link(d.tensor_scalar(newt[:, :, :], newt[:, :, :], 1.5, None, ALU.add))
            ch.link(mul(rstd[:, :, :], rstd[:, :, :], newt[:, :, :]))
            ch.link(mul(gs[:, :, :, 0:NF].rearrange("p b t j -> p (b t) j"),
                        gt[:, :, :, :].rearrange("p b t j -> p (b t) j"),
                        ap(rstd[:, :, :], 0, [[1, TILES], [0, NF]])))
            sat = sa[:, :, :, :].rearrange("p b t j -> p (b t) j")
            gst = gs[:, :, :, :].rearrange("p b t j -> p (b t) j")
            ch.link(d.tensor_copy(sat[:, :, 0:NG].bitcast(F32R), gst))
            ch.step(d.tensor_tensor(sat[:, :, NG:2 * NG], gst, sat[:, :, 0:NG], ALU.subtract))
            ch.step(d.tensor_copy(sat[:, :, 2 * NG:RA], sat[:, :, 0:NG]))
            ch.wait()
            v.sem_inc(s_sa, 1)
            v.wait_ge(s_const, 14)

            def queries_keys(b):
                r = b % 2
                for h in range(2):
                    v.wait_ge(s_q, 2 * b + h + 1)
                    d.tensor_scalar(qt[r][0:G2, h, :], (Q0, Q1)[h][0:G2, 0:NT * P], SCALE, None, ALU.max)\
                     .then_inc(s_qt, 1)
                v.wait_ge(s_k, 2 * b + 1)
                if b >= 2:
                    v.wait_ge(s_kg, b - 1)
                d.tensor_scalar(kt[r][:, 0:2, :], K0[:, 0:2 * D].rearrange("p (t d) -> p t d", t=2), SCALE, None,
                                ALU.max).then_inc(s_kt, 1)
                v.wait_ge(s_k, 2 * b + 2)
                d.tensor_scalar(kt[r][:, 2, :], K1[:, 0:D], SCALE, None, ALU.max).then_inc(s_kt, 1)

            def key_features(b):
                r = b % 2
                v.wait_ge(s_kg, b + 1)
                if b >= 2:
                    v.wait_ge(s_kv, b - 1)
                d.tensor_copy(kg[r][:, :], K1[0:NG, 256:256 + D]).then_inc(s_kgc, 1)

            def key_values(b):
                r = b % 2
                v.wait_ge(s_kv, b + 1)
                if b >= 2:
                    v.wait_ge(s_den, b - 1)
                    v.wait_ge(s_m, b - 1)
                mul(kvm[r][:, :, :], MM[0:G2, 0:2 * G2].rearrange("p (k d) -> p k d", k=2),
                    ap(head_mask[:, :], 0, [[0, 2], [1, G2]])).then_inc(s_kvc, 1)
                mul(dm[r][0:G2, :, :], MM[0:G2, 2 * G2:2 * G2 + 2 * NQ].rearrange("p (k d) -> p k d", k=2),
                    ap(head_mask[:, :], 0, [[0, 2], [HD, NQ]])).then_inc(s_kvc, 1)

            def statistics(b):
                r = b % 2
                v.wait_ge(s_hc, NT * (b + 1))
                for t in range(NT):
                    d.bn_stats(st6[:, t, :], row[r][:, t, 0:D]).then_inc(s_bn, 1)
                v.wait_ge(s_bn, NT * (b + 1))
                for t in range(NT):
                    ch.step(d.bn_aggr(mv[:, t, :], st6[:, t, :]))
                ch.wait()
                v.sem_inc(s_v2, 1)

            def inverse_denominators(b):
                r = b % 2
                v.wait_ge(s_den, b + 1)
                if b >= 2:
                    v.wait_ge(s_zt, 2 * (b - 1))
                d.reciprocal(zr[r][:, :, :, :].rearrange("p t g h -> p (t g h)"), HB[:, 0:NT * 2 * NQ])\
                 .then_inc(s_z, 1)

            def scaled_queries(b):
                r = b % 2
                for h in range(2):
                    v.wait_ge(s_zt, 2 * b + h + 1)
                    if b >= 2 and h == 0:
                        v.wait_ge(s_h, NT * (b - 1))
                    mul(zt[r][:, h, :], qt[r][0:G2, h, :], (D0, D1)[h][0:G2, 0:NT * P]).then_inc(s_qz, 1)

            def finish_rows(b):
                r = b % 2
                rw_ = row[r]
                lg = rw_[:, :, D:DL]
                ch.step(d.tensor_reduce(out=mx[:, :], in_=lg, axis=AX.X, op=ALU.max))
                v.wait_ge(s_sd2, b + 1)
                ch.step(d.reciprocal(rw_[:, :, C_RS], std[r][:, :]))
                ch.wait()
                mxb = ap(mx[:, :], 0, [[1, NT], [0, E]])
                ch.step(d.tensor_tensor(ge[:, b * NT:(b + 1) * NT, :], lg, mxb, ALU.is_ge))
                ch.step(d.tensor_tensor(dl[:, :, :], lg, mxb, ALU.subtract))
                ch.step(d.scalar_tensor_tensor(rw_[:, :, C_NM], mv[:, :, 0], -1.0, rw_[:, :, C_RS],
                                               ALU.mult, ALU.mult))
                ch.wait()
                ch.step(mul(lg, dl[:, :, :], ap(rw_[:, :, C_RS:C_RS + 1], 0, [[RW, NT], [0, E]])))
                ch.wait()
                v.sem_inc(s_done, 1)

            def choose(k):
                tiles = slice(k * TG, (k + 1) * TG)
                ch.link(mul(ohf[:, :, :], ge[:, tiles, :], expert_key[:, :, :]))
                ch.link(d.tensor_reduce(out=key[:, :], in_=ohf[:, :, :], axis=AX.X, op=ALU.max))
                ch.link(d.tensor_tensor(ohf[:, :, :], expert_key[:, :, :], ap(key[:, :], 0, [[1, TG], [0, E]]),
                                        ALU.is_equal))
                ch.step(d.tensor_copy(oh_all[:, tiles, :], ohf[:, :, :]))
                ch.step(d.tensor_copy(earlier[:, :, 0], carry[:, :]))
                ch.step(d.tensor_copy(earlier[:, :, 1:TG], ohf[:, 0:TG - 1, :].rearrange("p t e -> p e t")))
                ch.wait()
                ch.link(d.tensor_tensor_scan(before[:, :, :].rearrange("p e t -> p (e t)"),
                                             keep[:, :, :].rearrange("p e t -> p (e t)"),
                                             earlier[:, :, :].rearrange("p e t -> p (e t)"), 0.0,
                                             ALU.mult, ALU.add))
                ch.link(d.tensor_tensor(carry[:, :], before[:, :, TG - 1], ohf[:, TG - 1, :], ALU.add))
                ch.link(d.tensor_copy(carry_bf[:, :], carry[:, :]))
                v.sem_inc(s_oh, 1)

            def read_ranks(k):
                tiles = slice(k * TG, (k + 1) * TG)
                v.wait_ge(s_rk, k + 1)
                cum = Q0[:, CUM0:CUM0 + TG * E].rearrange("p (t e) -> p t e", e=E)
                ch.link(mul(ohf[:, :, :], cum, ohf[:, :, :]))
                v.sem_inc(s_ranked, 1)
                ch.link(d.tensor_reduce(out=rank[:, :], in_=ohf[:, :, :], axis=AX.X, op=ALU.add))
                ch.link(d.tensor_scalar(r_i[:, :], rank[:, :], -1.0, None, ALU.add))
                ch.step(d.tensor_scalar(lo_i[:, :], r_i[:, :], P - 1, None, ALU.bitwise_and))
                ch.step(d.tensor_scalar(hi_i[:, :], r_i[:, :], 7, None, ALU.arith_shift_right))
                ch.wait()
                ch.step(d.tensor_copy(lo_f[:, tiles], lo_i[:, :]))
                ch.step(d.tensor_copy(hi_f[:, tiles], hi_i[:, :]))
                ch.wait()
                v.sem_inc(s_lo, 1)

            def tables():
                for n in range(POOL_TILES, TILES):
                    d.tensor_scalar(oh_lo[:, n, :], iota_lane[:, :], lo_f[:, n:n + 1], None, ALU.is_equal)\
                     .then_inc(s_ohlo_v, 1)
                ch.link(d.tensor_scalar(cnt_i[:, :], Q0[:, CNT0:CNT0 + E], float(BLK - 1), None, ALU.add))
                ch.link(d.tensor_scalar(cnt_j[:, :], cnt_i[:, :], 8, None, ALU.arith_shift_right))
                ch.link(d.tensor_copy(cnt[:, :], cnt_j[:, :]))
                ch.link(d.tensor_tensor_scan(blk_end[:, :], ones_e[:, :], cnt[:, :], 0.0, ALU.mult, ALU.add))
                ch.step(d.tensor_tensor(be[:, :, :], iota_blk[:, :, :], ap(blk_end[0:1, :], 0, [[0, NBLK], [1, E]]),
                                        ALU.is_ge))
                ch.step(d.tensor_scalar(n_last[:, :], blk_end[0:1, E - 1:E], -1.0 - 2 * LAST_MIN, None, ALU.add))
                ch.link(d.tensor_tensor(first_tile[:, :], blk_end[:, :], cnt[:, :], ALU.subtract))
                ch.link(d.tensor_scalar(first_tile[:, :], first_tile[:, :], float(ST), None, ALU.mult))
                ch.link(mul(tl[:, :, :], oh_all[:, :, :], ap(first_tile[:, :], 0, [[0, TILES], [1, E]])))
                ch.link(d.tensor_reduce(out=tile_f[:, :], in_=tl[:, :, :], axis=AX.X, op=ALU.add))
                ch.link(d.tensor_tensor(tile_f[:, :], tile_f[:, :], hi_f[:, :], ALU.add))
                ch.link(d.tensor_tensor(oh_hi[:, :, 0, :], ap(iota_lane[:, :], 0, [[0, TILES], [1, NTILE]]),
                                        ap(tile_f[:, :], 0, [[1, TILES], [0, NTILE]]), ALU.is_equal))
                ch.step(d.tensor_scalar(oh_hi[:, :, 1, :], oh_hi[:, :, 0, :], iota_p[:, :], None, ALU.mult))
                ch.step(mul(oh_hi[:, :, 2, :], oh_hi[:, :, 0, :], ap(iota_t[:, :], 0, [[1, TILES], [0, NTILE]])))
                ch.wait()
                v.sem_inc(s_ohhi, 1)
                ch.link(d.tensor_reduce(out=bef[:, :], in_=be[:, :, :], axis=AX.X, op=ALU.add))
                ch.step(d.tensor_scalar(blk_expert[:, :], bef[:, :], float(E - 1), None, ALU.min))
                ch.step(d.tensor_tensor(fresh[:, 2:], bef[:, 2:], bef[:, :NBLK - 2], ALU.not_equal))
                ch.step(d.tensor_scalar(last_pair[:, :], n_last[:, :], 1, None, ALU.arith_shift_right))
                v.wait_ge(s_inv, 1)
                filled, lane, tile = (Q0[:, k * NTILE:(k + 1) * NTILE] for k in range(3))
                ch.step(d.tensor_copy(lane_f[:, :], lane))
                ch.link(d.tensor_copy(fill_f[:, :], filled))
                ch.link(d.scalar_tensor_tensor(gidf[:, :], tile, float(P), lane_f[:, :], ALU.mult, ALU.add))
                ch.link(d.scalar_tensor_tensor(sidf[:, :], fill_f[:, :], -float(OUT_OF_BOUNDS), gidf[:, :],
                                               ALU.mult, ALU.add))
                ch.step(d.tensor_scalar(sid[:, :], sidf[:, :], float(OUT_OF_BOUNDS), None, ALU.add))
                ch.step(d.tensor_copy(gid[:, :], gidf[:, :]))
                ch.wait()
                v.sem_inc(s_tab, 1)

            queries_keys(0)
            key_features(0)
            key_values(0)
            for b in range(B):
                if b + 1 < B:
                    queries_keys(b + 1)
                if b:
                    statistics(b - 1)
                inverse_denominators(b)
                if b + 1 < B:
                    key_features(b + 1)
                scaled_queries(b)
                if b + 1 < B:
                    key_values(b + 1)
                if b:
                    finish_rows(b - 1)
                if b == RANK_BATCH - 1:
                    choose(0)
                elif b == RANK_BATCH:
                    read_ranks(0)
            statistics(B - 1)
            finish_rows(B - 1)
            choose(1)
            read_ranks(1)
            tables()

            def mark(part, r):
                c = 2 * r + part
                return d.memset(mark_dve[:, c:c + 1], 0.0)

            def prepare(j, r, b, opening=False):
                v.wait_ge(s_hs[r], 16 * ST * (j + 1))
                if not opening:
                    v.wait_ge(s_x, b - 1)
                for s_ in range(ST):
                    h_ = hs[r][:, s_, :]
                    rs, nm = h_[:, C_RS:C_RS + 1], h_[:, C_NM:C_NM + 1]
                    d.tensor_scalar(xn[r][:, s_, 0:P], h_[:, 0:P], rs, nm, ALU.mult, ALU.add).then_inc(s_xn, 1)
                    d.tensor_scalar(xn[r][:, s_, P:256].rearrange("p (a j) -> p a j", a=2),
                                    ap(h_, P, [[0, 2], [1, 64]]), rs, nm, ALU.mult, ALU.add).then_inc(s_xn, 1)
                v.wait_ge(s_exp, ST * b + ST)
                d.reciprocal(prob[r][:, :], sume[r][:, :]).then_inc(s_pr, 1)

            def split(j, r, b, opening=False):
                v.wait_ge(s_xh, b + 1)
                d.tensor_tensor(xl[r][:, :], PP[:, 0:BLK], xh[r][:, 0:BLK].bitcast(F32), ALU.subtract)\
                 .then_inc(s_xl, 1)
                d.tensor_tensor(xh[r][64:P, BLK:2 * BLK], PP[64:P, BLK:2 * BLK],
                                xh[r][64:P, BLK:2 * BLK].bitcast(F32), ALU.subtract).then_inc(s_xl, 1)

                def low_up():
                    v.wait_ge(s_wh, 2 * b + 1)
                    if not opening:
                        v.wait_ge(s_y, b - 1)
                    d.tensor_tensor(wl[r][:, 0:2 * FF], raw[r][:, 0:2 * FF], wh[r][:, 0:2 * FF].bitcast(F32),
                                    ALU.subtract).then_inc(s_wl, 1)

                where_fresh(v, b, r, 0, opening, low_up, mark, s_wl)

            def block(j, r, first=False, tail=False):
                b = 2 * j + r
                opening = first and r == 0
                nxt = (j, 1) if r == 0 else (j + 1, 0)
                if not (tail and r == 1):
                    prepare(*nxt, b + 1, opening)
                for c in range(FC // 2):
                    v.wait_ge(s_hh, 3 * b + c + 1)
                    d.scalar_tensor_tensor(hl[r][:, 2 * c:2 * c + 2, :],
                                           UU[3 * r + c][:, :].rearrange("p (c t) -> p c t", c=2), 0.0,
                                           hh[r][:, 2 * c:2 * c + 2, :].bitcast(F32), ALU.max, ALU.subtract)\
                     .then_inc(s_hl, 1)
                    if c == 0:
                        def low_down():
                            v.wait_ge(s_wh, 2 * b + 2)
                            d.tensor_tensor(wl[r][:, 2 * FF:W_COLS], raw[r][:, 2 * FF:W_COLS],
                                            wh[r][:, 2 * FF:W_COLS].bitcast(F32), ALU.subtract).then_inc(s_wl, 1)

                        where_fresh(v, b, r, 1, first, low_down, mark, s_wl)
                if not (tail and r == 1):
                    split(*nxt, b + 1, opening)
                v.wait_ge(s_y, b + 1)
                v.wait_ge(s_res, b + 1)
                v.wait_ge(s_pr, b + 1)
                if not first:
                    v.wait_ge(s_fin[r], 16 * ST * j)
                for s_ in range(ST):
                    d.scalar_tensor_tensor(yr[r][:, s_, :], YY[:, s_ * 256:s_ * 256 + D], prob[r][:, s_:s_ + 1],
                                           res[r][:, s_, :], ALU.mult, ALU.add).then_inc(s_yr, 1)

            last = v.value_load(last_pair[0:1, 0:1], min_val=0, max_val=NBLK // 2 - 1 - LAST_MIN) + LAST_MIN
            prepare(0, 0, 0, True)
            split(0, 0, 0, True)
            pairs(v, block, last)

        @block_.tensor
        def _(pe):
            t_ = nc.tensor

            def mm(o, l, r_, start=True, stop=True):
                return t_.matmul(o, l, r_, start=start, stop=stop)

            pe.wait_ge(s_const, 1)
            pe.wait_ge(s_wload, 96)
            for gi in range(2):
                last = mm(bank[0][:, 0:NF], ones_mean[:, :], wfs[:, gi, :], gi == 0, gi == 1)
            for gi in range(2):
                last = mm(bank[0][:, NF:NF + E], ones_mean[:, :], ir[:, gi, D:DL], gi == 0, gi == 1)
            last.then_inc(s_wmean, 1)
            pe.wait_ge(s_wcent, 1)
            pe.wait_ge(s_const, 14)
            for gi in range(2):
                mm(bank[1][:, 0:65], ones_mean[:, :], outer[:, gi, :], gi == 0, gi == 1)
            for gi in range(2):
                for k in range(2):
                    mm(bank[1][0:G2, 128 + E * gi:128 + E * gi + E], pw[:, k, gi * G2:(gi + 1) * G2], ir[:, k, D:DL],
                       k == 0, k == 1)
            for o, lo, hi, copies in ((bank[2], 0, 2 * D, 3), (bank[3], 2 * D, 3 * D, 1)):
                rows = copies * NG
                for k in range(2):
                    mm(o[0:rows, 0:hi - lo], wf_c[:, k, 0:copies, :].rearrange("p c j -> p (c j)"),
                       wq_in[:, k, lo:hi], k == 0, False)
                mm(o[0:rows, 0:hi - lo], one_hot_row[:, 0:rows], const_row[:, lo:hi], False, True)
            for k in range(2):
                last = mm(bank[4][RB0:RT, 0:DL], wf_b[:, k, :, :].rearrange("p c j -> p (c j)"), ir[:, k, :],
                          k == 0, k == 1)
            last.then_inc(s_wprod, 1)
            pe.wait_ge(s_wready, 2)
            pe.wait_ge(s_sa, 1)

            def transpose(b):
                for t in range(NT):
                    last = t_.transpose(K0[0:RT, t * P:(t + 1) * P], sa[:, b, t, :], ident[:, :])
                last.then_inc(s_t, 1)

            def queries_keys(b):
                pe.wait_ge(s_gtt, b + 1)
                g_ = gtt[b % 3]
                if b:
                    pe.wait_ge(s_qt, 2 * b)
                if b == RANK_BATCH + 2:
                    pe.wait_ge(s_ranked, 1)
                for h in range(2):
                    mm((Q0, Q1)[h][0:G2, 0:NT * P], wa[:, h * G2:(h + 1) * G2], g_[0:RA, :]).then_inc(s_q, 1)
                for t in range(2):
                    last = mm(K0[:, t * D:(t + 1) * D], g_[0:RA, t * P:(t + 1) * P], wa[:, D:2 * D])
                last.then_inc(s_k, 1)
                if b:
                    pe.wait_ge(s_kgc, b)
                mm(K1[:, 0:D], g_[0:RA, 2 * P:3 * P], wa[:, D:2 * D]).then_inc(s_k, 1)

            def key_features(b):
                pe.wait_ge(s_kt, 2 * b + 2)
                for t in range(NT):
                    last = mm(K1[0:NG, 256:256 + D], gs[:, b, t, :], kt[b % 2][:, t, :], t == 0, t == NT - 1)
                last.then_inc(s_kg, 1)

            def key_values(b):
                r = b % 2
                pe.wait_ge(s_kgc, b + 1)
                if b:
                    pe.wait_ge(s_mc, b)
                for h in range(2):
                    s_ = slice(h * G2, (h + 1) * G2)
                    mm(MM[0:G2, h * G2:(h + 1) * G2], vw[:, s_], kg[r][:, s_])
                    last = mm(MM[0:G2, 2 * G2 + h * NQ:2 * G2 + (h + 1) * NQ], kg[r][:, s_], ksum_sel[:, 0:NQ])
                last.then_inc(s_kv, 1)

            def products(b):
                r = b % 2
                pe.wait_ge(s_kvc, 2 * b + 2)
                if b >= 2:
                    pe.wait_ge(s_h, NT * (b - 1))
                for h in range(2):
                    last = mm(MM[0:G2, h * DL:(h + 1) * DL], kvm[r][:, h, :], pr[:, h, :])
                last.then_inc(s_m, 1)
                if b:
                    pe.wait_ge(s_hc, NT * b)
                for t in range(NT):
                    for h in range(2):
                        o = (2 * t + h) * NQ
                        last = mm(HB[:, o:o + NQ], qt[r][:, h, t * P:(t + 1) * P], dm[r][:, h, :])
                last.then_inc(s_den, 1)

            def expand(b):
                pe.wait_ge(s_zx, b + 1)
                for h in range(2):
                    for t in range(NT):
                        last = t_.transpose((D0, D1)[h][0:G2, t * P:(t + 1) * P],
                                            zx[:, t, h * G2:(h + 1) * G2], ident[:, :])
                    last.then_inc(s_zt, 1)

            def hidden(b):
                r = b % 2
                pe.wait_ge(s_mc, b + 1)
                pe.wait_ge(s_qz, 2 * (b + 1))
                for t in range(NT):
                    s_ = slice(t * P, (t + 1) * P)
                    o = HT[t][:, 0:DL]
                    mm(o, gtt[b % 3][RB0:RT, s_], wb[RB0:RT, :], True, False)
                    mm(o, zt[r][:, 0, s_], mb[r][:, 0, :], False, False)
                    mm(o, zt[r][:, 1, s_], mb[r][:, 1, :], False, True).then_inc(s_h, 1)

            def ranks(k):
                pe.wait_ge(s_oh, k + 1)
                if k == 1:
                    mm(Q0[:, CNT0:CNT0 + E], ones_bf[:, :], carry_bf[:, :])
                o = Q0[:, CUM0:CUM0 + TG * E]
                mm(o, tri[:, :], oh_all[:, k * TG:(k + 1) * TG, :].rearrange("p t e -> p (t e)"), True, False)
                mm(o.rearrange("p (t e) -> p t e", e=E), ones_bf[:, :], before[:, :, :].rearrange("p e t -> p t e"),
                   False, True).then_inc(s_rk, 1)

            transpose(0)
            queries_keys(0)
            key_features(0)
            transpose(1)
            key_values(0)
            for b in range(B):
                if b + 1 < B:
                    queries_keys(b + 1)
                products(b)
                if b + 1 < B:
                    key_features(b + 1)
                if b + 2 < B:
                    transpose(b + 2)
                expand(b)
                if b + 1 < B:
                    key_values(b + 1)
                if b == RANK_BATCH:
                    ranks(0)
                hidden(b)
            ranks(1)
            pe.wait_ge(s_ohhi, 1)
            pe.wait_ge(s_ohlo, POOL_TILES)
            pe.wait_ge(s_ohlo_v, TILES - POOL_TILES)
            for n in range(TILES):
                last = mm(Q0[:, 0:3 * NTILE], oh_lo[:, n, :], oh_hi[:, n, :, :].rearrange("p k s -> p (k s)"),
                          n == 0, n == TILES - 1)
            last.then_inc(s_inv, 1)

            def transpose_slots(r, b):
                pe.wait_ge(s_xn, 2 * ST * b + 2 * ST)
                for k in range(2):
                    for s_ in range(ST):
                        last = t_.transpose(PP[:, k * BLK + s_ * P:k * BLK + (s_ + 1) * P],
                                            xn[r][:, s_, k * P:(k + 1) * P], ident[:, :])
                last.then_inc(s_x, 1)

            def block(j, r, first=False, tail=False):
                b = 2 * j + r
                pe.wait_ge(s_xl, 2 * b + 2)
                pe.wait_ge(s_wh, 2 * b + 1)
                pe.wait_ge(s_wl, 2 * b + 1)
                for c in range(FC):
                    if c % 2 == 0 and not first:
                        pe.wait_ge(s_hl, 3 * b - 5 + c // 2)
                    o = UU[3 * r + c // 2][:, (c % 2) * BLK:(c % 2 + 1) * BLK]
                    s1, s2 = slice(c * P, (c + 1) * P), slice(FF + c * P, FF + (c + 1) * P)
                    mm(o, wh[r][:, s1], xh[r][:, 0:BLK], True, False)
                    mm(o, wh[r][:, s1], xl[r][:, :], False, False)
                    mm(o, wl[r][:, s1], xh[r][:, 0:BLK], False, False)
                    mm(o, wh[r][:, s2], xh[r][:, BLK:2 * BLK], False, False)
                    last = mm(o, wl[r][:, s2], xh[r][:, BLK:2 * BLK], False, True)
                    if c % 2:
                        last.then_inc(s_u, 1)
                if not (tail and r == 1):
                    transpose_slots(1 - r, b + 1)
                pe.wait_ge(s_wh, 2 * b + 2)
                pe.wait_ge(s_wl, 2 * b + 2)
                if not (first and r == 0):
                    pe.wait_ge(s_yr, ST * b)
                for s_ in range(ST):
                    o = YY[:, s_ * 256:s_ * 256 + D]
                    t0 = slice(s_ * P, (s_ + 1) * P)
                    for c in range(FC):
                        if s_ == 0 and c % 2 == 0:
                            pe.wait_ge(s_hl, 3 * b + c // 2 + 1)
                        w_ = slice(2 * FF + c * D, 2 * FF + (c + 1) * D)
                        mm(o, hh[r][:, c, t0], wh[r][:, w_], c == 0, False)
                        mm(o, hh[r][:, c, t0], wl[r][:, w_], False, False)
                        last = mm(o, hl[r][:, c, t0], wh[r][:, w_], False, c == FC - 1)
                last.then_inc(s_y, 1)

            pe.wait_ge(s_tab, 1)
            last_ = pe.value_load(last_pair[0:1, 0:1], min_val=0, max_val=NBLK // 2 - 1 - LAST_MIN) + LAST_MIN
            transpose_slots(0, 0)
            pairs(pe, block, last_)


_OUT = (B, NT * P, D)


def kernel(x, x_txt, L0_tok_curve, L0_tok_proj_w, L0_tok_proj_b, L0_txt_quantum_params, L0_txt_post_w,
           L0_txt_post_b, L0_attn_qkv_w, L0_attn_proj_w, L0_attn_proj_b, L0_ffn_router_w, L0_ffn_wi, L0_ffn_wo):
    import concourse.bacc as bacc
    from concourse.bass_utils import run_bass_kernel_spmd

    nc = bacc.Bacc("TRN2", target_bir_lowering=False, num_devices=1)
    x = np.asarray(x)
    layout = {
        "pixels": x.transpose(2, 3, 0, 1).reshape(IMG * IMG, B * CH),
        "curve": np.asarray(L0_tok_curve),
        "txt_ids": np.asarray(x_txt).T,
        "qparams": np.asarray(L0_txt_quantum_params).reshape(VOCAB, NPAR),
        "wf": np.concatenate([np.asarray(L0_tok_proj_w), np.asarray(L0_tok_proj_b)[:, None],
                              np.asarray(L0_txt_post_w), np.asarray(L0_txt_post_b)[:, None]], axis=1),
        "qkv_wT": np.asarray(L0_attn_qkv_w).T,
        "proj_w": np.asarray(L0_attn_proj_w),
        "proj_wT": np.asarray(L0_attn_proj_w).T,
        "proj_b": np.asarray(L0_attn_proj_b).reshape(2, G2).T,
        "router_w": np.asarray(L0_ffn_router_w),
        "wi": np.asarray(L0_ffn_wi),
        "wo": np.asarray(L0_ffn_wo),
    }
    arrays, args = {}, []
    for name, a in layout.items():
        a = np.ascontiguousarray(a)
        arrays[f"{name}_dram"] = a
        args.append(nc.dram_tensor(f"{name}_dram", a.shape, mybir.dt.from_np(a.dtype), kind="ExternalInput").ap())
    args.append(nc.dram_tensor("out_dram", _OUT, F32, kind="ExternalOutput").ap())
    fusion_kernel(nc, *args)
    r = run_bass_kernel_spmd(nc, [arrays], core_ids=[0])
    return r.results[0]["out_dram"]
```

```python
from contextlib import ExitStack

import numpy as np

import concourse.bass as bass
from concourse import mybir

F32 = mybir.dt.float32
F32R = mybir.dt.float32r
BF16 = mybir.dt.bfloat16
I32 = mybir.dt.int32
U32 = mybir.dt.uint32
ALU = mybir.AluOpType
ACT = mybir.ActivationFunctionType
AX = mybir.AxisListType

P = 128
B = 8
NIMG, NTXT = 256, 128
NT = 3
TILES = B * NT
TOKENS = TILES * P
D = 192
G2 = 96
HD = 16
FF = 768
FC = FF // P
E = 8
POOL_TILES = TILES - 2
RANK_BATCH = B - 2
TG = TILES // 2
BLK = 256
ST = BLK // P
NBLK = 20
CUM0, CNT0 = NT * P, NT * P + TG * E
LAST_MIN = (TILES * P // BLK - 1) // 2
NTILE = NBLK * ST
NQ = 6
LAYERS = 3
NPAR = LAYERS * NQ * 2
IMG = 84
CH = 3
VOCAB = 8000
NF = 11
NG = 12
ONE_IMG, ONE_TXT = 3, 10
RA = 3 * NG
RB0 = 64
RB = 3 * NF
RT = RB0 + RB
DL = D + E
C_D, C_RS, C_NM = D, D + E, D + E + 1
RW = D + E + 2
OUT_OF_BOUNDS = 1 << 20
LN_EPS = 1e-5
DEN_EPS = 1e-6
SCALE = HD ** -0.5
PI = 3.1415925
MAGIC = 1.5 * 2.0 ** 23
TWO_PI_HI = 6.28125
TWO_PI_LO = 2 * np.pi - 6.28125
W_COLS = FF + FF + FC * D

PAULI = {"X": (1, 0), "Z": (0, 1), "Y": (1, 1)}


def ap(base, offset, dims):
    return bass.AP(tensor=base.tensor, offset=base.offset + offset, ap=[list(base.ap[0])] + [list(d) for d in dims])


def x5_terms():
    terms = []
    for s1 in "XZY":
        for s5 in "XYZ":
            for s0 in "ZXY":
                (f0, g0), (f1, g1), (f5, g5) = PAULI[s0], PAULI[s1], PAULI[s5]
                x0, z0, x1, z1, w = f0 ^ f5, g1 ^ g5, f0 ^ f1 ^ f5, g0 ^ g1 ^ g5, g0 ^ g5
                ys = [s0, s1, s5].count("Y")
                xz = x0 * z0 + x1 * z1 + f1 * w + f5 * w
                sign = 1 if (ys - xz) % 4 == 0 else -1
                terms.append((x0 * 8 + z0 * 4 + x1 * 2 + z1, f1 * 4 + f5 * 2 + w, sign))
    return terms


def term_copies():
    return sum(len(affine_runs([t[which] for t in x5_terms()])) for which in (0, 1))


def affine_runs(seq):
    out, i = [], 0
    while i < len(seq):
        best, dims = 1, [[1, 1]]
        j = i + 1
        if j < len(seq):
            step = seq[j] - seq[i]
            while j + 1 < len(seq) and seq[j + 1] - seq[j] == step:
                j += 1
            best, dims = j - i + 1, [[step, j - i + 1]]
        for a in (2, 3, 6, 9):
            for b in (2, 3, 4, 9):
                if a * b > best and i + a * b <= len(seq):
                    s1, s2 = seq[i + 1] - seq[i], seq[i + a] - seq[i]
                    if all(seq[i + q * a + r] == seq[i] + q * s2 + r * s1 for q in range(b) for r in range(a)):
                        best, dims = a * b, [[s2, b], [s1, a]]
        out.append((i, best, dims))
        i += best
    return out


class Chain:

    def __init__(self, engine, sem):
        self.engine, self.sem, self.n = engine, sem, 0

    def step(self, ins):
        self.n += 1
        ins.then_inc(self.sem, 1)
        return self.n

    def wait(self, n=None):
        self.engine.wait_ge(self.sem, self.n if n is None else n)

    def link(self, ins):
        self.step(ins)
        self.wait()


def fusion_kernel(nc, pixels, curve, txt_ids, qparams, wf, qkv_wT, proj_w, proj_wT, proj_b, router_w, wi, wo, out):
    out_rows = out.rearrange("b n d -> (b n) d")
    rows = nc.dram_tensor("rows", (TOKENS, RW), F32, kind="Internal").ap()
    ctx = ExitStack()
    with ctx:
        def sb(name, shape, dt=F32):
            return ctx.enter_context(nc.sbuf_tensor(name, shape, dt))

        def sem(name):
            return ctx.enter_context(nc.semaphore(name))

        bank = [ctx.enter_context(nc.psum_tensor(f"bank{i}", [P, 512], F32)) for i in range(8)]

        ident = sb("ident", [P, P])
        tri = sb("tri", [P, P], BF16)
        ones_bf = sb("ones_bf", [P, P], BF16)
        ones_mean = sb("ones_mean", [G2, P])
        head_mask = sb("head_mask", [G2, G2])
        lo_rows = sb("lo_rows", [P, 2])
        hi_coef = sb("hi_coef", [P, 2])
        ksum_sel = sb("ksum_sel", [NG, G2])
        const_row = sb("const_row", [1, 3 * D])
        one_hot_row = sb("one_hot_row", [1, RA])
        half_pi = sb("half_pi", [P, 1])
        eps_tile = sb("eps_tile", [P, 1])
        expert_key = sb("expert_key", [P, TG, E])
        term_sign = sb("term_sign", [P, 27])
        iota_lane = sb("iota_lane", [P, P])
        iota_p = sb("iota_p", [P, 1])
        iota_t = sb("iota_t", [P, TILES])
        iota_blk = sb("iota_blk", [1, NBLK, E])

        wfs = sb("wfs", [G2, 2, NF])
        wf_c = sb("wf_c", [G2, 2, 3, NG])
        wf_b = sb("wf_b", [G2, 2, 3, NF])
        wq_in = sb("wq_in", [G2, 2, 3 * D])
        pw = sb("pw", [G2, 2, D])
        pr = sb("pr", [G2, 2, DL])
        ir = sb("ir", [G2, 2, DL])
        pb = sb("pb", [G2, 2])
        wa = sb("wa", [RA, 2 * D], F32R)
        wa_lo = sb("wa_lo", [RA, 2 * D])
        vw = sb("vw", [NG, D])
        wb = sb("wb", [RT, DL], F32R)
        wb_lo = sb("wb_lo", [RT, DL])
        outer = sb("outer", [G2, 2, 16 + 49])
        quad = sb("quad", [P, 16 + 49])

        ids = sb("ids", [P, B], I32)
        crv = sb("crv", [P, 2, 2], I32)
        pix_id = sb("pix_id", [P, 2], I32)
        prm = sb("prm", [P, B, NPAR])
        kk = sb("kk", [P, B, NPAR])
        sn = sb("sn", [P, B, NPAR])
        cs = sb("cs", [P, B, NPAR])
        fz = sb("fz", [P, B, NQ, 4])
        fn = sb("fn", [P, B, NQ, 4])
        ns = sb("ns", [P, B, NQ])
        tr = sb("tr", [P, B, NQ, 8])
        base = sb("base", [P, B, 12])
        vs = sb("vs", [P, 4, B, 24])
        tmp = [sb(f"tmp{i}", [P, B, 24]) for i in range(2)]
        zs = sb("zs", [P, B, 4])
        ezt = sb("ezt", [P, 4, B, 4])
        w5 = sb("w5", [P, B, 12])
        ez = sb("ez", [P, NQ, B])
        co = sb("co", [P, B, NQ, 3])
        gx = sb("gx", [P, B, 5, 9])
        cx = sb("cx", [P, B, 5, 9])
        zp = sb("zp", [P, B, NQ])
        qv = sb("qv", [P, B, NQ])
        rv = sb("rv", [P, B, NQ])
        xt = sb("xt", [P, B, 8])
        z345 = sb("z345", [P, B, 2])
        p01 = sb("p01", [P, B, 16])
        d25 = sb("d25", [P, B, 8])
        gp = sb("gp", [P, B, 27])
        gd = sb("gd", [P, B, 27])
        c27 = sb("c27", [P, B, 27])
        ex = sb("ex", [P, B, NQ])

        pixg = sb("pixg", [P, 2, B * CH])
        gt = sb("gt", [P, B, NT, NF])
        gs = sb("gs", [P, B, NT, NG])
        sa = sb("sa", [P, B, NT, RT])
        vq = sb("vq", [P, B * 49])
        var = sb("var", [P, B, NT])
        rstd = sb("rstd", [P, B, NT])
        newt = sb("newt", [P, B, NT])

        qt = [sb(f"qt{i}", [G2 + 1, 2, NT * P]) for i in range(2)]
        kt = [sb(f"kt{i}", [P, NT, D]) for i in range(2)]
        kg = [sb(f"kg{i}", [NG, D]) for i in range(2)]
        kvm = [sb(f"kvm{i}", [G2, 2, G2]) for i in range(2)]
        dm = [sb(f"dm{i}", [G2 + 1, 2, NQ]) for i in range(2)]
        mb = [sb(f"mb{i}", [G2, 2, DL]) for i in range(2)]
        zr = [sb(f"zr{i}", [P, NT, 2, NQ]) for i in range(2)]
        zx = sb("zx", [P, NT, D])
        zt = [sb(f"zt{i}", [G2, 2, NT * P]) for i in range(2)]
        row = [sb(f"row{i}", [P, NT, RW]) for i in range(2)]
        dl = sb("dl", [P, NT, E])
        st6 = sb("st6", [P, NT, 6])
        mv = sb("mv", [P, NT, 2])
        std = [sb(f"std{i}", [P, NT]) for i in range(2)]
        mx = sb("mx", [P, NT])
        ge = sb("ge", [P, TILES, E])
        ohf = sb("ohf", [P, TG, E])
        key = sb("key", [P, TG])
        rank = sb("rank", [P, TG])
        carry = sb("carry", [P, E])
        carry_bf = sb("carry_bf", [P, E], BF16)
        earlier = sb("earlier", [P, E, TG])
        keep = sb("keep", [P, E, TG])
        before = sb("before", [P, E, TG], BF16)
        cnt = sb("cnt", [P, E])
        cnt_i = sb("cnt_i", [P, E], I32)
        blk_end = sb("blk_end", [P, E])
        first_block = sb("first_block", [P, E])
        first_tile = sb("first_tile", [P, E])
        r_i = sb("r_i", [P, TG], I32)
        lo_i = sb("lo_i", [P, TG], I32)
        hi_i = sb("hi_i", [P, TG], I32)
        lo_f = sb("lo_f", [P, TILES])
        tile_f = sb("tile_f", [P, TILES])
        lane_f = sb("lane_f", [P, NTILE])
        cnt_j = sb("cnt_j", [P, E], I32)
        ones_e = sb("ones_e", [P, E])
        hi_f = sb("hi_f", [P, TILES])
        oh_all = sb("oh_all", [P, TILES, E], BF16)
        oh_lo = sb("oh_lo", [P, TILES, P], BF16)
        in_tile = sb("in_tile", [P, TILES, NTILE], BF16)
        oh_hi = sb("oh_hi", [P, TILES, 2, NTILE], BF16)
        tl = sb("tl", [P, TILES, E])
        gidf = sb("gidf", [P, NTILE])
        sidf = sb("sidf", [P, NTILE])
        gid = sb("gid", [P, NTILE], I32)
        sid = sb("sid", [P, NTILE], I32)
        be = sb("be", [1, NBLK, E])
        bef = sb("bef", [1, NBLK])
        blk_expert = sb("blk_expert", [1, NBLK], I32)
        n_last = sb("n_last", [1, 1], I32)
        first_exp = sb("first_exp", [P, 1])
        mark_act, mark_dve, mark_pool = (sb(n, [P, 4]) for n in ("mark_act", "mark_dve", "mark_pool"))
        other = sb("other", [1, NBLK - 2])
        fresh = sb("fresh", [1, NBLK], I32)
        both = sb("both", [1, 1], I32)
        last_pair = sb("last_pair", [1, 1], I32)
        raw = [sb(f"raw{i}", [P, W_COLS]) for i in range(2)]
        whl = [sb(f"whl{i}", [P, 2, W_COLS], F32R) for i in range(2)]
        wh, wl = ([w_[:, k, :] for w_ in whl] for k in range(2))
        gtt = [wh[0][0:RT, i * NT * P:(i + 1) * NT * P] for i in range(3)]
        gr = [sb(f"gr{i}", [P, ST], I32) for i in range(2)]
        sr = [sb(f"sr{i}", [P, ST], I32) for i in range(2)]
        hs = [sb(f"hs{i}", [P, ST, RW]) for i in range(2)]
        xn = [sb(f"xn{i}", [P, ST, 256]) for i in range(2)]
        xh = [sb(f"xh{i}", [P, 2 * BLK], F32R) for i in range(2)]
        xl = [sb(f"xl{i}", [P, BLK], F32R) for i in range(2)]
        hh = [sb(f"hh{i}", [P, FC, BLK], F32R) for i in range(2)]
        hl = [sb(f"hl{i}", [P, FC, BLK], F32R) for i in range(2)]
        ed = [sb(f"ed{i}", [P, ST, E]) for i in range(2)]
        sume = [sb(f"sume{i}", [P, ST]) for i in range(2)]
        prob = [sb(f"prob{i}", [P, ST]) for i in range(2)]
        flat = sa[:, :, :, :].rearrange("p b t j -> p (b t j)")
        res, yr = ([flat[:, (2 * k + i) * ST * D:(2 * k + i + 1) * ST * D].rearrange("p (s d) -> p s d", s=ST)
                    for i in range(2)] for k in range(2))

        s_ids = sem("s_ids")
        s_small = sem("s_small")
        s_wload = sem("s_wload")
        s_pixid = sem("s_pixid")
        s_pix = [sem(f"s_pix{n}") for n in range(2)]
        s_prm = sem("s_prm")
        s_const = sem("s_const")
        s_constv = sem("s_constv")
        s_pool = sem("s_pool")
        s_dve = sem("s_dve")
        s_act = sem("s_act")
        s_red = sem("s_red")
        s_abs = sem("s_abs")
        s_trig = sem("s_trig")
        s_bloch = sem("s_bloch")
        s_co = sem("s_co")
        s_ex = sem("s_ex")
        s_wmean = sem("s_wmean")
        s_wcent = sem("s_wcent")
        s_wprod = sem("s_wprod")
        s_p01 = sem("s_p01")
        s_terms = sem("s_terms")
        s_wcopy = sem("s_wcopy")
        s_wready = sem("s_wready")
        s_var = sem("s_var")
        s_sd = sem("s_sd")
        s_sa = sem("s_sa")
        s_t = sem("s_t")
        s_gtt = sem("s_gtt")
        s_q = sem("s_q")
        s_qt = sem("s_qt")
        s_k = sem("s_k")
        s_kt = sem("s_kt")
        s_kg = sem("s_kg")
        s_kgc = sem("s_kgc")
        s_kv = sem("s_kv")
        s_kvc = sem("s_kvc")
        s_m = sem("s_m")
        s_mc = sem("s_mc")
        s_den = sem("s_den")
        s_z = sem("s_z")
        s_zx = sem("s_zx")
        s_zt = sem("s_zt")
        s_qz = sem("s_qz")
        s_h = sem("s_h")
        s_bn = sem("s_bn")
        s_hc = sem("s_hc")
        s_v2 = sem("s_v2")
        s_sd2 = sem("s_sd2")
        s_oh = sem("s_oh")
        s_rk = sem("s_rk")
        s_done = sem("s_done")
        s_lo = sem("s_lo")
        s_ohlo = sem("s_ohlo")
        s_ohlo_v = sem("s_ohlo_v")
        s_rows = [sem(f"s_rows{i}") for i in range(2)]
        s_ohhi = sem("s_ohhi")
        s_inv = sem("s_inv")
        s_plan = sem("s_plan")
        s_sid = sem("s_sid")
        s_tab = sem("s_tab")
        s_raw = [sem(f"s_raw{i}") for i in range(2)]
        s_load = sem("s_load")
        s_wh = sem("s_wh")
        s_wl = sem("s_wl")
        s_wd = sem("s_wd")
        s_gidx = sem("s_gidx")
        s_issue = sem("s_issue")
        s_sidx = sem("s_sidx")
        s_hs = [sem(f"s_hs{i}") for i in range(2)]
        s_res = sem("s_res")
        s_xn = sem("s_xn")
        s_xa = sem("s_xa")
        s_x = sem("s_x")
        s_xh = sem("s_xh")
        s_xl = sem("s_xl")
        s_u = sem("s_u")
        s_hh = sem("s_hh")
        s_hl = sem("s_hl")
        s_y = [sem(f"s_y{i}") for i in range(ST)]
        s_exp = sem("s_exp")
        s_pr = sem("s_pr")
        s_yr = sem("s_yr")
        s_fin = [sem(f"s_fin{i}") for i in range(2)]

        def last_blocks(engine):
            last = engine.value_load(last_pair[0:1, 0:1], min_val=0, max_val=NBLK // 2 - 1 - LAST_MIN) + LAST_MIN
            return last, engine.value_load(both[0:1, 0:1], min_val=0, max_val=1)

        def pairs(engine, body, last, two):
            for r in range(2):
                body(0, r, first=True)
            with engine.Fori(1, last) as j:
                for r in range(2):
                    body(j, r)
            body(last, 0, tail=True)
            with engine.If(two):
                body(last, 1, tail=True)

        def is_fresh(engine, b):
            return engine.value_load(fresh[0:1, bass.ds(b, 1)], min_val=0, max_val=1)

        def where_fresh(engine, b, opening, split, keep):
            if opening:
                split()
                return
            with engine.If(is_fresh(engine, b)):
                split()
            with engine.Else():
                keep()

        block_ = ctx.enter_context(nc.Block())

        K0, K1, MM, Q0, Q1, D0, D1, HB = bank
        HT = (HB, D0, D1)
        PP, UU, YY = bank[0], bank[1:4], bank[4:8]

        @block_.sync
        def _(sp):
            sp.dma_start(ids[:, :], txt_ids).then_inc(s_ids, 16)
            sp.dma_start(crv[:, :, :], curve.rearrange("(n p) c -> p n c", p=P)).then_inc(s_small, 16)
            sp.dma_start(wfs[:, :, :], wf.rearrange("(g p) j -> p g j", g=2)).then_inc(s_wload, 16)
            sp.dma_start(ir[:, :, D:DL], router_w.rearrange("(g p) e -> p g e", g=2)).then_inc(s_wload, 16)
            sp.dma_start(pb[:, :], proj_b).then_inc(s_wload, 16)
            sp.dma_start(wq_in[:, :, :], qkv_wT.rearrange("(g p) d -> p g d", g=2)).then_inc(s_wload, 16)
            sp.dma_start(pw[:, :, :], proj_w.rearrange("(g p) d -> p g d", g=2)).then_inc(s_wload, 16)
            sp.dma_start(pr[:, :, 0:D], proj_wT.rearrange("(g p) d -> p g d", g=2)).then_inc(s_wload, 16)

            def load_up(e, r):
                sp.dma_start(raw[r][:, 0:FF], wi[bass.ds(e, 1), 0:P, :]).then_inc(s_raw[r], 16)
                sp.dma_start(raw[r][0:64, FF:2 * FF], wi[bass.ds(e, 1), P:D, :]).then_inc(s_raw[r], 16)
                sp.dma_start(raw[r][64:P, FF:2 * FF], wi[bass.ds(e, 1), P:D, :]).then_inc(s_raw[r], 16)

            def load_down(e, r):
                sp.dma_start(raw[r][:, 2 * FF:W_COLS].rearrange("p (c d) -> p c d", c=FC),
                             wo[bass.ds(e, 1), :, :].rearrange("o (c p) d -> (o p) c d", p=P))\
                  .then_inc(s_raw[r], 16)

            for b in range(B):
                sp.wait_ge(s_done, b + 1)
                sp.dma_start(rows[b * NT * P:(b + 1) * NT * P, :].rearrange("(t p) d -> p t d", p=P),
                             row[b % 2][:, :, :]).then_inc(s_rows[b % 2], 16)

            def block(j, r, first=False):
                b = 2 * j + r
                e = sp.value_load(blk_expert[0:1, bass.ds(b, 1)], min_val=0, max_val=E - 1)
                if first:
                    load_up(e, r)
                    load_down(e, r)
                    return
                sp.wait_ge(s_wl, 2 * b - 2)
                sp.sem_inc(s_load, 1)
                with sp.If(is_fresh(sp, b)):
                    load_up(e, r)
                    sp.wait_ge(s_wd, b - 1)
                    load_down(e, r)
                with sp.Else():
                    sp.wait_ge(s_wd, b - 1)
                    sp.sem_inc(s_raw[r], 64)

            sp.wait_ge(s_plan, 1)
            block(0, 0, True)
            end = sp.value_load(last_pair[0:1, 0:1], min_val=0, max_val=NBLK // 2 - 1 - LAST_MIN) + LAST_MIN
            sp.wait_ge(s_hs[0], 16 * ST)
            block(0, 1, True)
            with sp.Fori(1, end + 1) as j:
                for r in range(2):
                    block(j, r)

        @block_.gpsimd
        def _(pool):
            ch = Chain(pool, s_pool)
            g = nc.gpsimd
            g.memset(ones_mean[:, :], 1.0 / D).then_inc(s_const, 1)
            ch.step(g.memset(ident[:, :], 0.0))
            ch.step(g.memset(head_mask[:, :], 1.0))
            ch.step(g.memset(lo_rows[:, :], 1.0))
            ch.step(g.memset(ksum_sel[:, :], 1.0))
            ch.step(g.memset(tri[:, :], 1.0))
            ch.step(g.memset(one_hot_row[:, :], 0.0))
            ch.step(g.memset(const_row[:, :], 0.0))
            ch.step(g.memset(ir[:, :, 0:D], 0.0))
            ch.wait()
            g.memset(const_row[:, 0:2 * D], SCALE).then_inc(s_const, 1)
            g.memset(ap(one_hot_row[:, :], NF, [[NG, 3]]), 1.0).then_inc(s_const, 1)
            pool.wait_ge(s_ids, 16)
            for b in range(B):
                g.indirect_dma_start(out=prm[:, b, :], out_offset=None, in_=qparams,
                                     in_offset=bass.IndirectOffsetOnAxis(ap=ids[:, b:b + 1].bitcast(U32), axis=0),
                                     bounds_check=VOCAB - 1, oob_is_err=False).then_inc(s_prm, 16)
            pool.wait_ge(s_pixid, 1)
            for n in range(2):
                g.indirect_dma_start(out=pixg[:, n, :], out_offset=None, in_=pixels,
                                     in_offset=bass.IndirectOffsetOnAxis(ap=pix_id[:, n:n + 1].bitcast(U32), axis=0),
                                     bounds_check=IMG * IMG - 1, oob_is_err=False).then_inc(s_pix[n], 16)
            g.affine_select(out=ident[:, :], in_=ident[:, :], compare_op=ALU.not_equal, fill=1.0, base=0,
                            pattern=[[-1, P]], channel_multiplier=1).then_inc(s_const, 1)
            g.affine_select(out=ir[:, :, 0:D], in_=ir[:, :, 0:D], compare_op=ALU.not_equal, fill=1.0, base=0,
                            pattern=[[G2, 2], [-1, D]], channel_multiplier=1).then_inc(s_const, 1)
            g.affine_select(out=tri[:, :], in_=tri[:, :], compare_op=ALU.is_ge, fill=0.0, base=-1,
                            pattern=[[1, P]], channel_multiplier=-1).then_inc(s_const, 1)
            hm = head_mask[:, :].rearrange("p (h d) -> p h d", d=HD)
            ch.link(g.affine_select(out=hm, in_=hm, compare_op=ALU.is_ge, fill=0.0, base=0,
                                    pattern=[[-HD, NQ], [0, HD]], channel_multiplier=1))
            g.affine_select(out=hm, in_=hm, compare_op=ALU.is_ge, fill=0.0, base=HD - 1,
                            pattern=[[HD, NQ], [0, HD]], channel_multiplier=-1).then_inc(s_const, 1)
            g.affine_select(out=ksum_sel[:, :], in_=ksum_sel[:, :], compare_op=ALU.is_ge, fill=0.0, base=-NF,
                            pattern=[[0, G2]], channel_multiplier=1).then_inc(s_const, 1)
            for j, first in enumerate((2 * NG, RB0 + 2 * NF)):
                g.affine_select(out=lo_rows[:, j:j + 1], in_=lo_rows[:, j:j + 1], compare_op=ALU.is_ge, fill=0.0,
                                base=-first, pattern=[[0, 1]], channel_multiplier=1).then_inc(s_const, 1)
            g.iota(iota_lane[:, :], pattern=[[1, P]], base=0, channel_multiplier=0,
                   allow_small_or_imprecise_dtypes=True).then_inc(s_const, 1)
            g.iota(iota_p[:, :], pattern=[[0, 1]], base=1, channel_multiplier=1,
                   allow_small_or_imprecise_dtypes=True).then_inc(s_const, 1)
            g.iota(iota_t[:, :], pattern=[[1, TILES]], base=0, channel_multiplier=0,
                   allow_small_or_imprecise_dtypes=True).then_inc(s_const, 1)
            g.iota(iota_blk[:, :, :], pattern=[[1, NBLK], [0, E]], base=0, channel_multiplier=0,
                   allow_small_or_imprecise_dtypes=True).then_inc(s_const, 1)
            g.iota(expert_key[:, :, :], pattern=[[0, TG], [-1, E]], base=E, channel_multiplier=0,
                   allow_small_or_imprecise_dtypes=True).then_inc(s_const, 1)

            pool.wait_ge(s_trig, 2)
            pool.wait_ge(s_bloch, 1)

            def th(a, layer):
                return a[:, :, :].rearrange("p t (l q r) -> p t l q r", l=LAYERS, r=2)[:, :, layer, :, 0]

            def ph(a, layer):
                return a[:, :, :].rearrange("p t (l q r) -> p t l q r", l=LAYERS, r=2)[:, :, layer, :, 1]

            def mul(o, a, b_):
                return g.tensor_tensor(o, a, b_, ALU.mult)

            def F(j, c, n=1):
                v = fz[:, :, j:j + n, c]
                return v

            def N(j, n=1):
                return fn[:, :, j:j + n, 3]

            ch.step(mul(co[:, :, :, 0], ph(cs, 1), th(cs, 1)))
            ch.step(mul(co[:, :, :, 1], ph(cs, 1), th(sn, 1)))
            ch.step(g.tensor_scalar(co[:, :, :, 2], ph(sn, 1), -1.0, None, ALU.mult))
            ch.step(g.tensor_copy(zp[:, :, 1:2], F(0, 1)))
            ch.step(g.tensor_copy(qv[:, :, 1:4], F(3, 2, 3)))
            ch.step(mul(qv[:, :, 4:5], F(0, 2), F(1, 2)))
            ch.step(mul(xt[:, :, 0:1], N(0), F(1, 3)))
            ch.step(mul(z345[:, :, 0:1], F(3, 1), F(4, 1)))
            ch.step(mul(xt[:, :, 1:2], F(2, 1), F(3, 1)))
            for i in range(2, 5):
                ch.wait()
                ch.step(mul(zp[:, :, i:i + 1], zp[:, :, i - 1:i], F(i - 1, 1)))
            ch.step(mul(z345[:, :, 1:2], z345[:, :, 0:1], F(5, 1)))
            ch.step(mul(rv[:, :, 4:5], xt[:, :, 0:1], xt[:, :, 1:2]))
            ch.wait()
            ch.step(mul(rv[:, :, 1:4], zp[:, :, 1:4], F(3, 2, 3)))
            pool.sem_inc(s_co, 1)
            X4, Y4, Z4, N4 = F(1, 2, 4), F(1, 3, 4), F(1, 1, 4), N(1, 4)
            X5, Y5, Z5, N5 = F(2, 2, 4), F(2, 3, 4), F(2, 1, 4), N(2, 4)
            ch.step(mul(gx[:, :, 1:5, 0], X4, qv[:, :, 1:5]))
            ch.step(mul(gx[:, :, 1:5, 1], zp[:, :, 1:5], N4))
            ch.step(mul(gx[:, :, 1:5, 2], Y4, Z5))
            ch.step(mul(gx[:, :, 1:5, 3], Z4, X5))
            ch.step(g.tensor_copy(gx[:, :, 1:5, 4], Z5))
            ch.step(mul(gx[:, :, 1:5, 5], Y5, qv[:, :, 1:5]))
            ch.step(mul(gx[:, :, 1:5, 7], X4, Y5))
            ch.wait()
            ch.step(mul(gx[:, :, 1:5, 1], gx[:, :, 1:5, 1], Y5))
            ch.step(mul(gx[:, :, 1:5, 2], gx[:, :, 1:5, 2], rv[:, :, 1:5]))
            ch.step(mul(gx[:, :, 1:5, 3], gx[:, :, 1:5, 3], rv[:, :, 1:5]))
            ch.step(mul(gx[:, :, 1:5, 6], Y4, rv[:, :, 1:5]))
            ch.step(mul(gx[:, :, 1:5, 8], gx[:, :, 1:5, 0], Z5))
            ch.wait()
            ch.step(g.tensor_scalar(gx[:, :, 1:5, 8], gx[:, :, 1:5, 8], -1.0, None, ALU.mult))
            zz = z345[:, :, 1:2]
            ch.step(mul(xt[:, :, 2:3], F(2, 1), zz))
            ch.step(mul(xt[:, :, 3:4], F(2, 3), zz))
            ch.step(mul(xt[:, :, 4:5], F(0, 3), F(1, 1)))
            ch.step(mul(xt[:, :, 5:6], F(0, 1), F(1, 2)))
            ch.step(mul(xt[:, :, 6:7], F(0, 2), F(1, 1)))
            ch.step(mul(xt[:, :, 7:8], F(0, 3), F(1, 2)))
            ch.wait()
            ch.step(mul(gx[:, :, 0:1, 0], F(0, 2), F(2, 2)))
            ch.step(mul(gx[:, :, 0:1, 1], N(0), F(1, 3)))
            ch.step(mul(gx[:, :, 0:1, 2], xt[:, :, 4:5], F(2, 2)))
            ch.step(mul(gx[:, :, 0:1, 3], N(1), xt[:, :, 3:4]))
            ch.step(mul(gx[:, :, 0:1, 4], F(0, 1), xt[:, :, 2:3]))
            ch.step(mul(gx[:, :, 0:1, 5], xt[:, :, 5:6], xt[:, :, 3:4]))
            ch.step(mul(gx[:, :, 0:1, 6], xt[:, :, 6:7], xt[:, :, 3:4]))
            ch.step(mul(gx[:, :, 0:1, 7], xt[:, :, 7:8], xt[:, :, 2:3]))
            ch.step(mul(gx[:, :, 0:1, 8], F(0, 3), xt[:, :, 3:4]))
            for s in range(3):
                ch.step(mul(cx[:, :, :, 3 * s:3 * s + 3],
                            co[:, :, 0:5, s:s + 1].to_broadcast([P, B, 5, 3]), co[:, :, 1:6, :]))
            ch.wait()
            g.tensor_tensor(gx[:, :, :, :], gx[:, :, :, :], cx[:, :, :, :], ALU.mult).then_inc(s_ex, 1)
            for k in range(2):
                pool.wait_ge(s_lo, k + 1)
                for n in range(k * TG, TG if k == 0 else POOL_TILES):
                    g.tensor_scalar(oh_lo[:, n, :], iota_lane[:, :], lo_f[:, n:n + 1], None, ALU.is_equal)\
                     .then_inc(s_ohlo, 1)

            def gather(j, r, first=False):
                b = 2 * j + r
                if not first:
                    pool.wait_ge(s_xn, 2 * b - 2)
                    pool.wait_ge(s_xa, 2 * b - 2)
                    pool.wait_ge(s_exp, 2 * b - 2)
                    pool.wait_ge(s_res, b - 1)
                g.tensor_copy(gr[r][:, :], gid[:, bass.ds(ST * b, ST)]).then_inc(s_gidx, 1)
                pool.wait_ge(s_gidx, b + 1)
                pool.sem_inc(s_issue, 1)
                for s_ in range(ST):
                    g.indirect_dma_start(out=hs[r][:, s_, :], out_offset=None, in_=rows,
                                         in_offset=bass.IndirectOffsetOnAxis(
                                             ap=gr[r][:, s_:s_ + 1].bitcast(U32), axis=0),
                                         bounds_check=TOKENS - 1, oob_is_err=False).then_inc(s_hs[r], 16)

            def scatter(j, r, first=False):
                b = 2 * j + r
                if not first:
                    pool.wait_ge(s_fin[r], 16 * ST * j)
                g.tensor_copy(sr[r][:, :], sid[:, bass.ds(ST * b, ST)]).then_inc(s_sidx, 1)
                pool.wait_ge(s_sidx, b + 1)
                for s_ in range(ST):
                    pool.wait_ge(s_yr, 2 * ST * b + 2 * s_ + 2)
                    pool.sem_inc(s_issue, 1)
                    g.indirect_dma_start(out=out_rows,
                                         out_offset=bass.IndirectOffsetOnAxis(
                                             ap=sr[r][:, s_:s_ + 1].bitcast(U32), axis=0),
                                         in_=yr[r][:, s_, :], in_offset=None, bounds_check=TOKENS - 1,
                                         oob_is_err=False).then_inc(s_fin[r], 16)

            def low_down(r, b, opening=False):
                def split():
                    pool.wait_ge(s_wh, 3 * b + 3)
                    if not opening:
                        pool.wait_ge(s_y[ST - 1], b - 1)
                    g.tensor_tensor(wl[r][:, 2 * FF:], raw[r][:, 2 * FF:], wh[r][:, 2 * FF:].bitcast(F32),
                                    ALU.subtract).then_inc(s_wd, 1)

                def keep():
                    g.memset(mark_pool[:, r:r + 1], 0.0).then_inc(s_wd, 1)

                where_fresh(pool, b, opening, split, keep)

            def block(j, r, first=False, tail=False):
                b = 2 * j + r
                if not tail:
                    gather(j + 1, r)
                if not (tail and r == 1):
                    low_down(1 - r, b + 1, first and r == 0)
                scatter(j, r, first)

            pool.wait_ge(s_tab, 1)
            for r in range(2):
                pool.wait_ge(s_rows[r], 16 * B // 2)
            gather(0, 0, True)
            low_down(0, 0, True)
            gather(0, 1, True)
            last, two = last_blocks(pool)
            pool.wait_ge(s_sid, 1)
            pairs(pool, block, last, two)
            pool.wait_ge(s_fin[0], 16 * ST * (last + 1))
            pool.wait_ge(s_fin[1], 16 * ST * (last + two))

        @block_.scalar
        def _(act):
            a = nc.scalar
            ch = Chain(act, s_act)
            act.wait_ge(s_constv, 2)
            act.wait_ge(s_red, 1)
            a.activation(sn[:, :, :], prm[:, :, :], ACT.Sin).then_inc(s_trig, 1)
            act.wait_ge(s_red, 2)
            a.activation(cs[:, :, :], kk[:, :, :], ACT.Sin, bias=half_pi[:, :], scale=-1.0).then_inc(s_trig, 1)
            act.wait_ge(s_wprod, 1)
            a.activation(quad[:, :], bank[1][:, 0:65], ACT.Copy).then_inc(s_wcopy, 1)
            act.wait_ge(s_p01, 1)
            for dst, src, width, which in ((gp, p01, 16, 0), (gd, d25, 8, 1)):
                seq = [t[which] for t in x5_terms()]
                for i, n, dims in affine_runs(seq):
                    o = [[27, B]] + ([[dims[1][1], dims[0][1]], [1, dims[1][1]]] if len(dims) == 2 else [[1, n]])
                    a.activation(ap(dst[:, :, :], i, o), ap(src[:, :, :], seq[i], [[width, B]] + dims), ACT.Copy)\
                     .then_inc(s_terms, 1)
            for o, w_ in ((vw[:, :], bank[3][0:NG, 0:D]),
                          (pr[:, :, D:DL], bank[1][0:G2, 128:128 + 2 * E].rearrange("p (g e) -> p g e", g=2)),
                          (wa[:, :], bank[2][0:RA, 0:2 * D]), (wb[RB0:RT, :], bank[4][RB0:RT, 0:DL])):
                a.activation(o, w_, ACT.Copy).then_inc(s_wcopy, 1)
            a.activation(wa_lo[:, :], bank[2][0:RA, 0:2 * D], ACT.Copy, scale=lo_rows[0:RA, 0:1]).then_inc(s_wcopy, 1)
            a.activation(wb_lo[RB0:RT, :], bank[4][RB0:RT, 0:DL], ACT.Copy, scale=lo_rows[RB0:RT, 1:2])\
             .then_inc(s_wcopy, 1)
            act.wait_ge(s_var, 1)
            a.activation(rstd[:, :, :], var[:, :, :], ACT.Sqrt, bias=eps_tile[:, :]).then_inc(s_sd, 1)

            def features(b):
                act.wait_ge(s_t, b + 1)
                if b >= 3:
                    act.wait_ge(s_h, NT * (b - 2))
                a.activation(gtt[b % 3], K0[0:RT, 0:NT * P], ACT.Copy).then_inc(s_gtt, 1)

            def deviation(b):
                act.wait_ge(s_v2, b + 1)
                a.activation(std[b % 2][:, :], mv[:, :, 1], ACT.Sqrt, bias=eps_tile[:, :]).then_inc(s_sd2, 1)

            def h2(b):
                r = b % 2
                for t in range(NT):
                    act.wait_ge(s_h, b * NT + t + 1)
                    if t == 0 and b >= 2:
                        act.wait_ge(s_rows[r], 16 * (b // 2))
                    a.activation(row[r][:, t, 0:DL], HT[t][:, 0:DL], ACT.Copy).then_inc(s_hc, 1)

            def m_copy(b):
                r = b % 2
                act.wait_ge(s_m, b + 1)
                a.activation(mb[r][:, :, :], MM[0:G2, 0:2 * DL].rearrange("p (g d) -> p g d", g=2), ACT.Copy)\
                 .then_inc(s_mc, 1)

            features(0)
            features(1)
            for b in range(B):
                m_copy(b)
                if b:
                    deviation(b - 1)
                act.wait_ge(s_z, b + 1)
                if b:
                    act.wait_ge(s_zt, 2 * b)
                a.activation(zx[:, :, :].rearrange("p t (k j) -> p (t k) j", j=HD),
                             ap(zr[b % 2][:, :, :, :], 0, [[1, NT * 2 * NQ], [0, HD]]), ACT.Copy).then_inc(s_zx, 1)
                if b + 2 < B:
                    features(b + 2)
                h2(b)
            deviation(B - 1)

            def mark(r, k):
                a.activation(mark_act[:, 2 * r + k:2 * r + k + 1], half_pi[:, :], ACT.Copy).then_inc(s_wh, 2 - k)

            def normalise(j, r, b, opening=False):
                act.wait_ge(s_hs[r], 16 * ST * (j + 1))
                if not opening:
                    act.wait_ge(s_x, b - 1)
                h_ = hs[r][:, ST - 1, :]
                rs, nm = h_[:, C_RS:C_RS + 1], h_[:, C_NM:C_NM + 1]
                a.activation(xn[r][:, ST - 1, 0:P], h_[:, 0:P], ACT.Identity, bias=nm, scale=rs).then_inc(s_xa, 1)
                a.activation(xn[r][:, ST - 1, P:256].rearrange("p (a j) -> p a j", a=2),
                             ap(h_, P, [[0, 2], [1, 64]]), ACT.Identity, bias=nm, scale=rs).then_inc(s_xa, 1)

            def keep_rows(r, b, opening=False):
                if not opening:
                    act.wait_ge(s_exp, ST * b - ST)
                    act.wait_ge(s_pr, b - 1)
                    act.wait_ge(s_yr, 2 * ST * b - 2 * ST)
                for s_ in range(ST):
                    a.activation(ed[r][:, s_, :], hs[r][:, s_, C_D:C_D + E], ACT.Exp,
                                 accum_out=sume[r][:, s_:s_ + 1]).then_inc(s_exp, 1)
                a.activation(res[r][:, :, :], hs[r][:, :, 0:D], ACT.Copy).then_inc(s_res, 1)

            def split_slots(r, b):
                act.wait_ge(s_x, b + 1)
                a.activation(xh[r][:, :], PP[:, :], ACT.Copy).then_inc(s_xh, 1)

            def high_up(j, r, b, opening=False):
                def split():
                    act.wait_ge(s_raw[r], 64 * (j + 1))
                    if not opening:
                        act.wait_ge(s_u, 3 * b - 3)
                    for g_ in range(2):
                        a.activation(wh[r][:, g_ * FF:(g_ + 1) * FF], raw[r][:, g_ * FF:(g_ + 1) * FF], ACT.Copy)\
                         .then_inc(s_wh, 1)

                where_fresh(act, b, opening, split, lambda: mark(r, 0))

            def high_down(r, b, opening=False):
                def split():
                    if not opening:
                        act.wait_ge(s_y[ST - 1], b - 1)
                    a.activation(wh[r][:, 2 * FF:], raw[r][:, 2 * FF:], ACT.Copy).then_inc(s_wh, 1)

                where_fresh(act, b, opening, split, lambda: mark(r, 1))

            def block(j, r, first=False, tail=False):
                b = 2 * j + r
                opening = first and r == 0
                nxt = (j, 1) if r == 0 else (j + 1, 0)
                for c in range(FC // 2):
                    act.wait_ge(s_u, 3 * b + c + 1)
                    if c == 0 and not first:
                        act.wait_ge(s_y[ST - 1], b - 1)
                    a.activation(hh[r][:, 2 * c:2 * c + 2, :],
                                 UU[c][:, :].rearrange("p (c t) -> p c t", c=2), ACT.Relu).then_inc(s_hh, 1)
                    if c == 0 and not (tail and r == 1):
                        normalise(*nxt, b + 1, opening)
                    if c == 2 and not (tail and r == 1):
                        high_up(*nxt, b + 1, opening)
                if not (tail and r == 1):
                    split_slots(1 - r, b + 1)
                    high_down(1 - r, b + 1, opening)
                    keep_rows(1 - r, b + 1, opening)

            a.activation(first_exp[:, :], half_pi[:, :], ACT.Exp)
            high_up(0, 0, 0, True)
            high_down(0, 0, True)
            act.wait_ge(s_tab, 1)
            normalise(0, 0, 0, True)
            split_slots(0, 0)
            keep_rows(0, 0, True)
            last, two = last_blocks(act)
            pairs(act, block, last, two)

        @block_.vector
        def _(v):
            ch = Chain(v, s_dve)
            d = nc.vector

            def mul(o, a, b_):
                return d.tensor_tensor(o, a, b_, ALU.mult)

            d.memset(half_pi[:, :], float(np.pi / 2)).then_inc(s_constv, 1)
            d.memset(eps_tile[:, :], LN_EPS).then_inc(s_constv, 1)
            ch.step(d.memset(ones_bf[:, :], 1.0))
            ch.step(d.memset(ones_e[:, :], 1.0))
            ch.step(d.memset(fz[:, :, :, 0], 1.0))
            ch.step(d.memset(fn[:, :, :, 0], 1.0))
            ch.step(d.memset(carry[:, :], 0.0))
            ch.step(d.memset(keep[:, :, 0:1], 0.0))
            ch.step(d.memset(keep[:, :, 1:TG], 1.0))
            ch.step(d.memset(gt[:, :, :, :], 0.0))
            ch.step(d.memset(sa[:, :, :, RA:RB0], 0.0))
            ch.step(d.memset(gs[:, :, :, NF], 1.0))
            ch.step(d.memset(wf_c[:, :, :, NF], 0.0))
            ch.step(d.memset(zs[:, :, 3], 1.0))
            ch.step(d.memset(term_sign[:, :], 1.0))
            for i in range(2):
                ch.step(d.memset(qt[i][G2:G2 + 1, :, :], 1.0))
                ch.step(d.memset(dm[i][G2:G2 + 1, :, :], DEN_EPS))
            ch.wait()
            ch.step(d.memset(gt[:, :, 0:2, ONE_IMG], 1.0))
            ch.step(d.memset(gt[:, :, 2, ONE_TXT], 1.0))
            for i, (_, _, sign) in enumerate(x5_terms()):
                if sign < 0:
                    ch.step(d.memset(term_sign[:, i:i + 1], -1.0))
            v.wait_ge(s_small, 16)
            d.scalar_tensor_tensor(pix_id[:, :], crv[:, :, 1], float(IMG), crv[:, :, 0], ALU.mult, ALU.add)\
             .then_inc(s_pixid, 1)

            v.wait_ge(s_prm, 16 * B)
            ch.link(d.tensor_scalar(kk[:, :, :], prm[:, :, :], float(1 / (2 * np.pi)), MAGIC, ALU.mult, ALU.add))
            ch.link(d.tensor_scalar(kk[:, :, :], kk[:, :, :], -MAGIC, None, ALU.add))
            ch.link(d.scalar_tensor_tensor(prm[:, :, :], kk[:, :, :], -TWO_PI_HI, prm[:, :, :], ALU.mult, ALU.add))
            ch.link(d.scalar_tensor_tensor(prm[:, :, :], kk[:, :, :], -float(TWO_PI_LO), prm[:, :, :],
                                           ALU.mult, ALU.add))
            d.tensor_scalar(prm[:, :, :], prm[:, :, :], PI, -PI, ALU.min, ALU.max).then_inc(s_red, 1)
            v.wait_ge(s_red, 1)
            d.scalar_tensor_tensor(kk[:, :, :], prm[:, :, :], -1.0, prm[:, :, :], ALU.mult, ALU.max)\
             .then_inc(s_red, 1)

            v.wait_ge(s_wload, 96)
            v.wait_ge(s_wmean, 1)
            mean_w = bank[0][0:G2, 0:NF + E]
            for gi in range(2):
                for c in range(3):
                    ch.step(d.tensor_tensor(wf_c[:, gi, c, 0:NF], wfs[:, gi, :], mean_w[:, 0:NF], ALU.subtract))
                    ch.step(d.tensor_copy(wf_b[:, gi, c, :], wfs[:, gi, :]))
                ch.step(d.tensor_tensor(ir[:, gi, D:DL], ir[:, gi, D:DL], mean_w[:, NF:NF + E], ALU.subtract))
            ch.wait()
            for gi in range(2):
                for c in range(3):
                    for col in (ONE_IMG, ONE_TXT):
                        ch.step(d.tensor_tensor(wf_b[:, gi, c, col:col + 1], wf_b[:, gi, c, col:col + 1],
                                                pb[:, gi:gi + 1], ALU.add))
                for o, first, n in ((0, 0, 4), (16, 4, 7)):
                    w_ = wf_c[:, gi, 0, first:first + n]
                    ch.step(mul(outer[:, gi, o:o + n * n].rearrange("p (j k) -> p j k", j=n),
                                ap(w_, 0, [[1, n], [0, n]]), ap(w_, 0, [[0, n], [1, n]])))
            ch.wait()
            v.sem_inc(s_wcent, 1)
            def th(a, layer):
                return a[:, :, :].rearrange("p t (l q r) -> p t l q r", l=LAYERS, r=2)[:, :, layer, :, 0]

            def ph(a, layer):
                return a[:, :, :].rearrange("p t (l q r) -> p t l q r", l=LAYERS, r=2)[:, :, layer, :, 1]

            v.wait_ge(s_trig, 2)
            ch.step(d.tensor_copy(fz[:, :, :, 1], th(cs, 0)))
            ch.step(mul(fz[:, :, :, 2], th(sn, 0), ph(cs, 0)))
            ch.step(mul(fz[:, :, :, 3], th(sn, 0), ph(sn, 0)))
            ch.wait()
            ch.step(d.tensor_copy(fn[:, :, :, 1:3], fz[:, :, :, 1:3]))
            ch.step(d.tensor_scalar(fn[:, :, :, 3], fz[:, :, :, 3], -1.0, None, ALU.mult))
            ch.step(d.tensor_scalar(ns[:, :, :], th(sn, 1), -1.0, None, ALU.mult))
            ch.wait()
            v.sem_inc(s_bloch, 1)

            c1 = th(cs, 1)
            ch.step(mul(tr[:, :, :, 0:4], fn[:, :, :, :], ap(c1, 0, [[NPAR, B], [2, NQ], [0, 4]])))
            ch.step(mul(tr[:, :, :, 4:6], fz[:, :, :, 2:4], ap(ns[:, :, :], 0, [[NQ, B], [1, NQ], [0, 2]])))
            ch.step(mul(tr[:, :, :, 6:8], fz[:, :, :, 0:2], ap(ns[:, :, :], 0, [[NQ, B], [1, NQ], [0, 2]])))
            f0, n0 = fz[:, :, 0, :], fn[:, :, 0, :]
            cc = ap(c1, 0, [[NPAR, B], [0, 2]])
            s0 = ns[:, :, 0:1].to_broadcast([P, B, 2])
            ch.step(mul(base[:, :, 0:2], ap(f0, 1, [[4 * NQ, B], [-1, 2]]), cc))
            ch.step(mul(base[:, :, 2:4], f0[:, :, 2:4], s0))
            ch.step(d.tensor_copy(base[:, :, 4:6], f0[:, :, 0:2]))
            ch.step(mul(base[:, :, 6:8], ap(n0, 3, [[4 * NQ, B], [-1, 2]]), cc))
            ch.step(mul(base[:, :, 8:10], f0[:, :, 0:2], s0))
            ch.step(d.tensor_copy(base[:, :, 10:12], f0[:, :, 2:4]))
            ch.wait()
            for f in range(2):
                for fp in range(2):
                    o, st_ = (4 * fp + 2 * f, 1) if f else (4 * fp + 1, -1)
                    ch.step(mul(ap(vs[:, 0, :, :], o, [[24, B], [8, 3], [st_, 2]]),
                                ap(base[:, :, :], 2 * fp, [[12, B], [4, 3], [1, 2]]),
                                ap(tr[:, :, 1, :], 4 * f + 2 * fp, [[8 * NQ, B], [0, 3], [1, 2]])))
            ch.wait()
            for k in range(2, 5):
                for f in range(2):
                    ch.step(mul(ap(tmp[f][:, :, :], 0, [[24, B], [4, 6], [1, 4]]),
                                ap(vs[:, k - 2, :, :], 0, [[24, B], [4, 6], [1, 4]]),
                                ap(tr[:, :, k, :], 4 * f, [[8 * NQ, B], [0, 6], [1, 4]])))
                ch.wait()
                for f in range(2):
                    o, st_ = (2, 1) if f else (1, -1)
                    ch.step(d.tensor_tensor(ap(vs[:, k - 1, :, :], o, [[4, 6 * B], [st_, 2]]),
                                            ap(tmp[f][:, :, :], 0, [[4, 6 * B], [1, 2]]),
                                            ap(tmp[f][:, :, :], 2, [[4, 6 * B], [1, 2]]), ALU.add))
                ch.wait()
            ch.step(d.tensor_copy(zs[:, :, 2:3], fz[:, :, 5, 1:2]))
            ch.link(mul(zs[:, :, 1:2], fz[:, :, 4, 1:2], fz[:, :, 5, 1:2]))
            ch.step(mul(zs[:, :, 0:1], fz[:, :, 3, 1:2], zs[:, :, 1:2]))
            for a_ in range(2):
                o = 4 if a_ else 1
                c_o = 0 if a_ else 1
                ch.step(mul(ap(ezt[:, :, :, :], 2 * a_, [[4 * B, 4], [4, B], [1, 2]]),
                            ap(vs[:, :, :, :], o, [[24 * B, 4], [24, B], [2, 2]]),
                            ap(fn[:, :, 2, :], c_o, [[4, 4], [4 * NQ, B], [2, 2]])))
            for a_, vo, vstep, to, tstep in ((0, 0, 13, 0, 5), (1, 5, 11, 1, 3), (2, 9, 11, 1, 3)):
                ch.step(mul(ap(w5[:, :, :], 4 * a_, [[12, B], [2, 2], [1, 2]]),
                            ap(vs[:, 3, :, :], vo, [[24, B], [vstep, 2], [2, 2]]),
                            ap(tr[:, :, 5, :], to, [[8 * NQ, B], [tstep, 2], [2, 2]])))
            ch.wait()
            ch.step(mul(ap(ezt[:, :, :, :], 0, [[4 * B, 4], [4, B], [1, 2]]),
                        ap(ezt[:, :, :, :], 0, [[4 * B, 4], [4, B], [1, 2]]),
                        ap(zs[:, :, :], 0, [[1, 4], [4, B], [0, 2]])))
            ch.step(d.tensor_reduce(out=ez[:, 0, :], in_=w5[:, :, 8:12], axis=AX.X, op=ALU.add))
            ch.step(d.tensor_reduce(out=ez[:, 5, :], in_=w5[:, :, 0:8], axis=AX.X, op=ALU.add))
            ch.wait()
            ch.step(d.tensor_reduce(out=ez[:, 1:5, :], in_=ezt[:, :, :, :], axis=AX.X, op=ALU.add))
            v.wait_ge(s_co, 1)
            for c in range(4):
                ch.step(mul(p01[:, :, 4 * c:4 * c + 4], fz[:, :, 0, c:c + 1].to_broadcast([P, B, 4]), fz[:, :, 1, :]))
            for f1 in range(2):
                ch.step(mul(d25[:, :, 4 * f1:4 * f1 + 4].rearrange("p t (f w) -> p t f w", w=2),
                            ap(fz[:, :, 2, 2 * f1:2 * f1 + 2], 0, [[4 * NQ, B], [0, 2], [1, 2]]),
                            fz[:, :, 5, :].rearrange("p t (f w) -> p t f w", w=2)))
            ch.wait()
            ch.link(mul(ap(d25[:, :, :], 1, [[8, B], [2, 4]]), ap(d25[:, :, :], 1, [[8, B], [2, 4]]),
                        z345[:, :, 0:1].to_broadcast([P, B, 4])))
            v.sem_inc(s_p01, 1)
            for i5, c5 in enumerate((0, 2, 1)):
                ch.step(mul(ap(c27[:, :, :], 3 * i5, [[27, B], [9, 3], [1, 1]]),
                            ap(co[:, :, :, :], 3, [[18, B], [1, 3], [1, 1]]),
                            ap(co[:, :, :, :], 15 + c5, [[18, B], [0, 3], [1, 1]])))
            ch.wait()
            for i0, c0 in ((2, 2), (1, 0), (0, 1)):
                ch.step(mul(ap(c27[:, :, :], i0, [[27, B], [3, 9]]), ap(c27[:, :, :], 0, [[27, B], [3, 9]]),
                            ap(co[:, :, :, :], c0, [[18, B], [0, 9]])))
                ch.wait()
            ch.link(mul(c27[:, :, :], c27[:, :, :], ap(term_sign[:, :], 0, [[0, B], [1, 27]])))

            v.wait_ge(s_wcopy, 1)
            for n in range(2):
                v.wait_ge(s_pix[n], 16)
                ch.step(d.tensor_copy(gt[:, :, n, 0:CH], pixg[:, n, :].rearrange("p (b c) -> p b c", c=CH)))
            ch.wait()
            for n in range(2):
                f = gt[:, :, n, 0:4]
                q4 = ap(vq[:, :], 0, [[16, B], [4, 4], [1, 4]])
                ch.link(mul(q4, ap(f, 0, [[NT * NF, B], [1, 4], [0, 4]]), ap(f, 0, [[NT * NF, B], [0, 4], [1, 4]])))
                q1 = ap(vq[:, :], 0, [[16, B], [1, 16]])
                ch.link(mul(q1, q1, ap(quad[:, :], 0, [[0, B], [1, 16]])))
                ch.link(d.tensor_reduce(out=var[:, :, n], in_=q1, axis=AX.X, op=ALU.add))

            ch.step(d.tensor_scalar(hi_coef[:, :], lo_rows[:, :], -2.0, 1.0, ALU.mult, ALU.add))
            ch.wait()
            v.wait_ge(s_wcopy, 7)
            d.scalar_tensor_tensor(wa[:, :], wa[:, :].bitcast(F32), hi_coef[0:RA, 0:1], wa_lo[:, :],
                                   ALU.mult, ALU.add).then_inc(s_wready, 1)
            d.scalar_tensor_tensor(wb[RB0:RT, :], wb[RB0:RT, :].bitcast(F32), hi_coef[RB0:RT, 1:2], wb_lo[RB0:RT, :],
                                   ALU.mult, ALU.add).then_inc(s_wready, 1)

            v.wait_ge(s_terms, term_copies())
            ch.link(mul(gp[:, :, :], gp[:, :, :], gd[:, :, :]))
            ch.link(mul(gp[:, :, :], gp[:, :, :], c27[:, :, :]))
            v.wait_ge(s_ex, 1)
            ch.step(d.tensor_reduce(out=ex[:, :, 0:5], in_=gx[:, :, :, :], axis=AX.X, op=ALU.add))
            ch.step(d.tensor_reduce(out=ex[:, :, 5:6], in_=gp[:, :, :], axis=AX.X, op=ALU.add))
            ch.wait()
            ch.step(mul(ex[:, :, :], ex[:, :, :], th(sn, 2)))
            ch.step(mul(ns[:, :, :], ez[:, :, :].rearrange("p q t -> p t q"), th(cs, 2)))
            ch.wait()
            ch.link(d.tensor_tensor(gt[:, :, 2, 4:4 + NQ], ns[:, :, :], ex[:, :, :], ALU.subtract))

            f = gt[:, :, 2, 4:11]
            ch.link(mul(ap(vq[:, :], 0, [[49, B], [7, 7], [1, 7]]),
                        ap(f, 0, [[NT * NF, B], [1, 7], [0, 7]]), ap(f, 0, [[NT * NF, B], [0, 7], [1, 7]])))
            q1 = ap(vq[:, :], 0, [[49, B], [1, 49]])
            ch.link(mul(q1, q1, ap(quad[:, :], 16, [[0, B], [1, 49]])))
            d.tensor_reduce(out=var[:, :, 2], in_=q1, axis=AX.X, op=ALU.add).then_inc(s_var, 1)
            for t in range(NT):
                g_ = gt[:, :, t, :]
                hi = sa[:, :, t, RB0:RB0 + NF]
                ch.link(d.tensor_copy(hi.bitcast(F32R), g_))
                ch.step(d.tensor_tensor(sa[:, :, t, RB0 + NF:RB0 + 2 * NF], g_, hi, ALU.subtract))
                ch.step(d.tensor_copy(sa[:, :, t, RB0 + 2 * NF:RT], hi))
            v.wait_ge(s_sd, 1)
            ch.step(d.tensor_scalar(var[:, :, :], var[:, :, :], LN_EPS, -0.5, ALU.add, ALU.mult))
            ch.link(d.reciprocal(rstd[:, :, :], rstd[:, :, :]))
            ch.link(mul(newt[:, :, :], rstd[:, :, :], rstd[:, :, :]))
            ch.link(mul(newt[:, :, :], newt[:, :, :], var[:, :, :]))
            ch.link(d.tensor_scalar(newt[:, :, :], newt[:, :, :], 1.5, None, ALU.add))
            ch.link(mul(rstd[:, :, :], rstd[:, :, :], newt[:, :, :]))
            ch.link(mul(gs[:, :, :, 0:NF].rearrange("p b t j -> p (b t) j"),
                        gt[:, :, :, :].rearrange("p b t j -> p (b t) j"),
                        ap(rstd[:, :, :], 0, [[1, TILES], [0, NF]])))
            sat = sa[:, :, :, :].rearrange("p b t j -> p (b t) j")
            gst = gs[:, :, :, :].rearrange("p b t j -> p (b t) j")
            ch.link(d.tensor_copy(sat[:, :, 0:NG].bitcast(F32R), gst))
            ch.step(d.tensor_tensor(sat[:, :, NG:2 * NG], gst, sat[:, :, 0:NG], ALU.subtract))
            ch.step(d.tensor_copy(sat[:, :, 2 * NG:RA], sat[:, :, 0:NG]))
            ch.wait()
            v.sem_inc(s_sa, 1)
            v.wait_ge(s_const, 14)

            def queries_keys(b):
                r = b % 2
                for h in range(2):
                    v.wait_ge(s_q, 2 * b + h + 1)
                    d.tensor_scalar(qt[r][0:G2, h, :], (Q0, Q1)[h][0:G2, 0:NT * P], SCALE, None, ALU.max)\
                     .then_inc(s_qt, 1)
                v.wait_ge(s_k, 2 * b + 1)
                if b >= 2:
                    v.wait_ge(s_kg, b - 1)
                d.tensor_scalar(kt[r][:, 0:2, :], K0[:, 0:2 * D].rearrange("p (t d) -> p t d", t=2), SCALE, None,
                                ALU.max).then_inc(s_kt, 1)
                v.wait_ge(s_k, 2 * b + 2)
                d.tensor_scalar(kt[r][:, 2, :], K1[:, 0:D], SCALE, None, ALU.max).then_inc(s_kt, 1)

            def key_features(b):
                r = b % 2
                v.wait_ge(s_kg, b + 1)
                if b >= 2:
                    v.wait_ge(s_kv, b - 1)
                d.tensor_copy(kg[r][:, :], K1[0:NG, 256:256 + D]).then_inc(s_kgc, 1)

            def key_values(b):
                r = b % 2
                v.wait_ge(s_kv, b + 1)
                if b >= 2:
                    v.wait_ge(s_den, b - 1)
                    v.wait_ge(s_m, b - 1)
                mul(kvm[r][:, :, :], MM[0:G2, 0:2 * G2].rearrange("p (k d) -> p k d", k=2),
                    ap(head_mask[:, :], 0, [[0, 2], [1, G2]])).then_inc(s_kvc, 1)
                mul(dm[r][0:G2, :, :], MM[0:G2, 2 * G2:2 * G2 + 2 * NQ].rearrange("p (k d) -> p k d", k=2),
                    ap(head_mask[:, :], 0, [[0, 2], [HD, NQ]])).then_inc(s_kvc, 1)

            def tile_statistics(b, tiles):
                for t in tiles:
                    v.wait_ge(s_hc, NT * b + t + 1)
                    d.bn_stats(st6[:, t, :], row[b % 2][:, t, 0:D]).then_inc(s_bn, 1)

            def statistics(b):
                v.wait_ge(s_bn, NT * (b + 1))
                for t in range(NT):
                    ch.step(d.bn_aggr(mv[:, t, :], st6[:, t, :]))
                ch.wait()
                v.sem_inc(s_v2, 1)

            def inverse_denominators(b):
                r = b % 2
                v.wait_ge(s_den, b + 1)
                if b >= 2:
                    v.wait_ge(s_zt, 2 * (b - 1))
                d.reciprocal(zr[r][:, :, :, :].rearrange("p t g h -> p (t g h)"), HB[:, 0:NT * 2 * NQ])\
                 .then_inc(s_z, 1)

            def scaled_queries(b):
                r = b % 2
                for h in range(2):
                    v.wait_ge(s_zt, 2 * b + h + 1)
                    if b >= 2 and h == 0:
                        v.wait_ge(s_h, NT * (b - 1))
                    mul(zt[r][:, h, :], qt[r][0:G2, h, :], (D0, D1)[h][0:G2, 0:NT * P]).then_inc(s_qz, 1)

            def largest_logits(b):
                lg = row[b % 2][:, :, D:DL]
                ch.link(d.tensor_reduce(out=mx[:, :], in_=lg, axis=AX.X, op=ALU.max))
                mxb = ap(mx[:, :], 0, [[1, NT], [0, E]])
                ch.step(d.tensor_tensor(ge[:, b * NT:(b + 1) * NT, :], lg, mxb, ALU.is_ge))
                ch.link(d.tensor_tensor(dl[:, :, :], lg, mxb, ALU.subtract))

            def finish_rows(b):
                r = b % 2
                rw_ = row[r]
                v.wait_ge(s_sd2, b + 1)
                ch.link(d.reciprocal(rw_[:, :, C_RS], std[r][:, :]))
                ch.step(d.scalar_tensor_tensor(rw_[:, :, C_NM], mv[:, :, 0], -1.0, rw_[:, :, C_RS],
                                               ALU.mult, ALU.mult))
                ch.step(mul(rw_[:, :, D:DL], dl[:, :, :], ap(rw_[:, :, C_RS:C_RS + 1], 0, [[RW, NT], [0, E]])))
                ch.wait()
                v.sem_inc(s_done, 1)

            def choose(k):
                tiles = slice(k * TG, (k + 1) * TG)
                ch.link(mul(ohf[:, :, :], ge[:, tiles, :], expert_key[:, :, :]))
                ch.link(d.tensor_reduce(out=key[:, :], in_=ohf[:, :, :], axis=AX.X, op=ALU.max))
                ch.link(d.tensor_tensor(ohf[:, :, :], expert_key[:, :, :], ap(key[:, :], 0, [[1, TG], [0, E]]),
                                        ALU.is_equal))
                ch.step(d.tensor_copy(oh_all[:, tiles, :], ohf[:, :, :]))

            def count_before(k):
                ch.step(d.tensor_copy(earlier[:, :, 0], carry[:, :]))
                ch.step(d.tensor_copy(earlier[:, :, 1:TG], ohf[:, 0:TG - 1, :].rearrange("p t e -> p e t")))
                ch.wait()
                ch.link(d.tensor_tensor_scan(before[:, :, :].rearrange("p e t -> p (e t)"),
                                             keep[:, :, :].rearrange("p e t -> p (e t)"),
                                             earlier[:, :, :].rearrange("p e t -> p (e t)"), 0.0,
                                             ALU.mult, ALU.add))
                ch.link(d.tensor_tensor(carry[:, :], before[:, :, TG - 1], ohf[:, TG - 1, :], ALU.add))
                ch.link(d.tensor_copy(carry_bf[:, :], carry[:, :]))
                v.sem_inc(s_oh, 1)

            def read_ranks(k):
                tiles = slice(k * TG, (k + 1) * TG)
                v.wait_ge(s_rk, k + 1)
                cum = Q0[:, CUM0:CUM0 + TG * E].rearrange("p (t e) -> p t e", e=E)
                ch.link(mul(ohf[:, :, :], cum, ohf[:, :, :]))
                ch.link(d.tensor_reduce(out=rank[:, :], in_=ohf[:, :, :], axis=AX.X, op=ALU.add))
                ch.link(d.tensor_copy(r_i[:, :], rank[:, :]))
                ch.step(d.tensor_scalar(lo_i[:, :], r_i[:, :], P - 1, None, ALU.bitwise_and))
                ch.step(d.tensor_scalar(hi_i[:, :], r_i[:, :], 7, None, ALU.arith_shift_right))
                ch.wait()
                ch.step(d.tensor_copy(lo_f[:, tiles], lo_i[:, :]))
                ch.step(d.tensor_copy(hi_f[:, tiles], hi_i[:, :]))
                ch.wait()
                v.sem_inc(s_lo, 1)

            def tables():
                for n in range(POOL_TILES, TILES):
                    d.tensor_scalar(oh_lo[:, n, :], iota_lane[:, :], lo_f[:, n:n + 1], None, ALU.is_equal)\
                     .then_inc(s_ohlo_v, 1)
                ch.link(d.tensor_scalar(cnt_i[:, :], Q0[:, CNT0:CNT0 + E], float(BLK - 1), None, ALU.add))
                ch.link(d.tensor_scalar(cnt_j[:, :], cnt_i[:, :], 8, None, ALU.arith_shift_right))
                ch.link(d.tensor_copy(cnt[:, :], cnt_j[:, :]))
                ch.link(d.tensor_tensor_scan(blk_end[:, :], ones_e[:, :], cnt[:, :], 0.0, ALU.mult, ALU.add))
                ch.step(d.tensor_tensor(be[:, :, :], iota_blk[:, :, :], ap(blk_end[0:1, :], 0, [[0, NBLK], [1, E]]),
                                        ALU.is_ge))
                ch.step(d.tensor_scalar(n_last[:, :], blk_end[0:1, E - 1:E], -1.0 - 2 * LAST_MIN, None, ALU.add))
                ch.step(d.tensor_tensor(first_block[:, :], blk_end[:, :], cnt[:, :], ALU.subtract))
                ch.wait()
                ch.step(d.tensor_reduce(out=bef[:, :], in_=be[:, :, :], axis=AX.X, op=ALU.add))
                ch.step(d.tensor_scalar(last_pair[:, :], n_last[:, :], 1, None, ALU.arith_shift_right))
                ch.step(d.tensor_scalar(both[:, :], n_last[:, :], 1, None, ALU.bitwise_and))
                ch.step(d.tensor_scalar(first_tile[:, :], first_block[:, :], float(ST), None, ALU.mult))
                ch.wait()
                ch.step(d.tensor_scalar(blk_expert[:, :], bef[:, :], float(E - 1), None, ALU.min))
                ch.step(d.tensor_tensor(other[:, :], bef[:, 2:], bef[:, :NBLK - 2], ALU.not_equal))
                ch.step(mul(tl[:, :, :], oh_all[:, :, :], ap(first_tile[:, :], 0, [[0, TILES], [1, E]])))
                ch.wait()
                ch.link(d.scalar_tensor_tensor(fresh[:, 2:], bef[:, 2:], float(E), other[:, :], ALU.is_lt, ALU.mult))
                v.sem_inc(s_plan, 1)
                ch.link(d.tensor_reduce(out=tile_f[:, :], in_=tl[:, :, :], axis=AX.X, op=ALU.add))
                ch.link(d.tensor_tensor(tile_f[:, :], tile_f[:, :], hi_f[:, :], ALU.add))
                ch.link(d.tensor_tensor(in_tile[:, :, :], ap(iota_lane[:, :], 0, [[0, TILES], [1, NTILE]]),
                                        ap(tile_f[:, :], 0, [[1, TILES], [0, NTILE]]), ALU.is_equal))
                ch.step(d.tensor_scalar(oh_hi[:, :, 0, :], in_tile[:, :, :], iota_p[:, :], None, ALU.mult))
                ch.step(mul(oh_hi[:, :, 1, :], in_tile[:, :, :], ap(iota_t[:, :], 0, [[1, TILES], [0, NTILE]])))
                ch.wait()
                v.sem_inc(s_ohhi, 1)
                v.wait_ge(s_inv, 1)
                ch.link(d.tensor_copy(lane_f[:, :], Q0[:, 0:NTILE]))
                ch.link(d.scalar_tensor_tensor(gidf[:, :], Q0[:, NTILE:2 * NTILE], float(P), lane_f[:, :],
                                               ALU.mult, ALU.add))
                ch.link(d.tensor_scalar(gid[:, :], gidf[:, :], -1.0, 0.0, ALU.add, ALU.max))
                v.sem_inc(s_tab, 1)
                ch.link(d.tensor_scalar(sidf[:, :], gidf[:, :], 0.0, float(OUT_OF_BOUNDS), ALU.is_equal, ALU.mult))
                ch.link(d.scalar_tensor_tensor(sid[:, :], sidf[:, :], -1.0, gidf[:, :], ALU.add, ALU.add))
                v.sem_inc(s_sid, 1)

            queries_keys(0)
            key_features(0)
            key_values(0)
            for b in range(B):
                if b + 1 < B:
                    queries_keys(b + 1)
                if b:
                    tile_statistics(b - 1, (NT - 1,))
                    statistics(b - 1)
                inverse_denominators(b)
                if b + 1 < B:
                    key_features(b + 1)
                scaled_queries(b)
                if b + 1 < B:
                    key_values(b + 1)
                if b:
                    largest_logits(b - 1)
                    finish_rows(b - 1)
                if b == RANK_BATCH - 2:
                    choose(0)
                elif b == RANK_BATCH - 1:
                    count_before(0)
                elif b == RANK_BATCH:
                    read_ranks(0)
                tile_statistics(b, range(NT - 1))
            tile_statistics(B - 1, (NT - 1,))
            largest_logits(B - 1)
            choose(1)
            count_before(1)
            statistics(B - 1)
            finish_rows(B - 1)
            read_ranks(1)
            tables()

            def mark(r):
                d.memset(mark_dve[:, r:r + 1], 0.0).then_inc(s_wl, 2)

            def prepare(j, r, b, opening=False):
                v.wait_ge(s_hs[r], 16 * ST * (j + 1))
                if not opening:
                    v.wait_ge(s_x, b - 1)
                for s_ in range(ST - 1):
                    h_ = hs[r][:, s_, :]
                    rs, nm = h_[:, C_RS:C_RS + 1], h_[:, C_NM:C_NM + 1]
                    d.tensor_scalar(xn[r][:, s_, 0:P], h_[:, 0:P], rs, nm, ALU.mult, ALU.add).then_inc(s_xn, 1)
                    d.tensor_scalar(xn[r][:, s_, P:256].rearrange("p (a j) -> p a j", a=2),
                                    ap(h_, P, [[0, 2], [1, 64]]), rs, nm, ALU.mult, ALU.add).then_inc(s_xn, 1)

            def split_slots(r, b):
                v.wait_ge(s_xh, b + 1)
                d.tensor_tensor(xl[r][:, :], PP[:, 0:BLK], xh[r][:, 0:BLK].bitcast(F32), ALU.subtract)\
                 .then_inc(s_xl, 1)
                d.tensor_tensor(xh[r][64:P, BLK:2 * BLK], PP[64:P, BLK:2 * BLK],
                                xh[r][64:P, BLK:2 * BLK].bitcast(F32), ALU.subtract).then_inc(s_xl, 1)

            def low_up(r, b):
                for g_ in range(2):
                    cols = slice(g_ * FF, (g_ + 1) * FF)
                    v.wait_ge(s_wh, 3 * b + g_ + 1)
                    d.tensor_tensor(wl[r][:, cols], raw[r][:, cols], wh[r][:, cols].bitcast(F32), ALU.subtract)\
                     .then_inc(s_wl, 1)

            def split_weights(r, b, opening=False):
                def split():
                    if not opening:
                        v.wait_ge(s_u, 3 * b - 3)
                    low_up(r, b)

                where_fresh(v, b, opening, split, lambda: mark(r))

            def block(j, r, first=False, tail=False):
                b = 2 * j + r
                opening = first and r == 0
                nxt = (j, 1) if r == 0 else (j + 1, 0)
                for c in range(FC // 2):
                    v.wait_ge(s_hh, 3 * b + c + 1)
                    d.scalar_tensor_tensor(hl[r][:, 2 * c:2 * c + 2, :],
                                           UU[c][:, :].rearrange("p (c t) -> p c t", c=2), 0.0,
                                           hh[r][:, 2 * c:2 * c + 2, :].bitcast(F32), ALU.max, ALU.subtract)\
                     .then_inc(s_hl, 1)
                    if c == 0 and not (tail and r == 1):
                        prepare(*nxt, b + 1, opening)
                    if c == 2 and not (tail and r == 1):
                        split_weights(1 - r, b + 1, opening)
                if not (tail and r == 1):
                    split_slots(1 - r, b + 1)
                v.wait_ge(s_exp, ST * b + ST)
                d.reciprocal(prob[r][:, :], sume[r][:, :]).then_inc(s_pr, 1)
                v.wait_ge(s_res, b + 1)
                v.wait_ge(s_pr, b + 1)
                if not first:
                    v.wait_ge(s_fin[r], 16 * ST * j)
                for s_ in range(ST):
                    v.wait_ge(s_y[s_], b + 1)
                    for k in (1, 0):
                        if k == 0:
                            v.wait_ge(s_yr, 2 * ST * b + 2 * s_ + 1)
                        d.scalar_tensor_tensor(yr[r][:, s_, :], YY[2 * r + s_][:, k * D:(k + 1) * D],
                                               prob[r][:, s_:s_ + 1], (res if k else yr)[r][:, s_, :],
                                               ALU.mult, ALU.add).then_inc(s_yr, 1)

            low_up(0, 0)
            prepare(0, 0, 0, True)
            split_slots(0, 0)
            last, two = last_blocks(v)
            pairs(v, block, last, two)

        @block_.tensor
        def _(pe):
            t_ = nc.tensor

            def mm(o, l, r_, start=True, stop=True):
                return t_.matmul(o, l, r_, start=start, stop=stop)

            pe.wait_ge(s_const, 1)
            pe.wait_ge(s_wload, 96)
            for gi in range(2):
                last = mm(bank[0][:, 0:NF], ones_mean[:, :], wfs[:, gi, :], gi == 0, gi == 1)
            for gi in range(2):
                last = mm(bank[0][:, NF:NF + E], ones_mean[:, :], ir[:, gi, D:DL], gi == 0, gi == 1)
            last.then_inc(s_wmean, 1)
            pe.wait_ge(s_wcent, 1)
            pe.wait_ge(s_const, 14)
            for gi in range(2):
                mm(bank[1][:, 0:65], ones_mean[:, :], outer[:, gi, :], gi == 0, gi == 1)
            for gi in range(2):
                for k in range(2):
                    mm(bank[1][0:G2, 128 + E * gi:128 + E * gi + E], pw[:, k, gi * G2:(gi + 1) * G2], ir[:, k, D:DL],
                       k == 0, k == 1)
            for o, lo, hi, copies in ((bank[2], 0, 2 * D, 3), (bank[3], 2 * D, 3 * D, 1)):
                rows = copies * NG
                for k in range(2):
                    mm(o[0:rows, 0:hi - lo], wf_c[:, k, 0:copies, :].rearrange("p c j -> p (c j)"),
                       wq_in[:, k, lo:hi], k == 0, False)
                mm(o[0:rows, 0:hi - lo], one_hot_row[:, 0:rows], const_row[:, lo:hi], False, True)
            for k in range(2):
                last = mm(bank[4][RB0:RT, 0:DL], wf_b[:, k, :, :].rearrange("p c j -> p (c j)"), ir[:, k, :],
                          k == 0, k == 1)
            last.then_inc(s_wprod, 1)
            pe.wait_ge(s_wcopy, 7)
            pe.wait_ge(s_wready, 2)
            pe.wait_ge(s_sa, 1)

            def transpose(b):
                for t in range(NT):
                    last = t_.transpose(K0[0:RT, t * P:(t + 1) * P], sa[:, b, t, :], ident[:, :])
                last.then_inc(s_t, 1)

            def queries_keys(b):
                pe.wait_ge(s_gtt, b + 1)
                g_ = gtt[b % 3]
                if b:
                    pe.wait_ge(s_qt, 2 * b)
                for h in range(2):
                    mm((Q0, Q1)[h][0:G2, 0:NT * P], wa[:, h * G2:(h + 1) * G2], g_[0:RA, :]).then_inc(s_q, 1)
                for t in range(2):
                    last = mm(K0[:, t * D:(t + 1) * D], g_[0:RA, t * P:(t + 1) * P], wa[:, D:2 * D])
                last.then_inc(s_k, 1)
                if b:
                    pe.wait_ge(s_kgc, b)
                mm(K1[:, 0:D], g_[0:RA, 2 * P:3 * P], wa[:, D:2 * D]).then_inc(s_k, 1)

            def key_features(b):
                pe.wait_ge(s_kt, 2 * b + 2)
                for t in range(NT):
                    last = mm(K1[0:NG, 256:256 + D], gs[:, b, t, :], kt[b % 2][:, t, :], t == 0, t == NT - 1)
                last.then_inc(s_kg, 1)

            def key_values(b):
                r = b % 2
                pe.wait_ge(s_kgc, b + 1)
                if b:
                    pe.wait_ge(s_mc, b)
                for h in range(2):
                    s_ = slice(h * G2, (h + 1) * G2)
                    mm(MM[0:G2, h * G2:(h + 1) * G2], vw[:, s_], kg[r][:, s_])
                    last = mm(MM[0:G2, 2 * G2 + h * NQ:2 * G2 + (h + 1) * NQ], kg[r][:, s_], ksum_sel[:, 0:NQ])
                last.then_inc(s_kv, 1)

            def products(b):
                r = b % 2
                pe.wait_ge(s_kvc, 2 * b + 2)
                if b >= 2:
                    pe.wait_ge(s_h, NT * (b - 1))
                for h in range(2):
                    last = mm(MM[0:G2, h * DL:(h + 1) * DL], kvm[r][:, h, :], pr[:, h, :])
                last.then_inc(s_m, 1)
                if b:
                    pe.wait_ge(s_hc, NT * b)
                for t in range(NT):
                    for h in range(2):
                        o = (2 * t + h) * NQ
                        last = mm(HB[:, o:o + NQ], qt[r][:, h, t * P:(t + 1) * P], dm[r][:, h, :])
                last.then_inc(s_den, 1)

            def expand(b):
                pe.wait_ge(s_zx, b + 1)
                for h in range(2):
                    for t in range(NT):
                        last = t_.transpose((D0, D1)[h][0:G2, t * P:(t + 1) * P],
                                            zx[:, t, h * G2:(h + 1) * G2], ident[:, :])
                    last.then_inc(s_zt, 1)

            def hidden(b):
                r = b % 2
                pe.wait_ge(s_mc, b + 1)
                pe.wait_ge(s_qz, 2 * (b + 1))
                for t in range(NT):
                    s_ = slice(t * P, (t + 1) * P)
                    o = HT[t][:, 0:DL]
                    mm(o, gtt[b % 3][RB0:RT, s_], wb[RB0:RT, :], True, False)
                    mm(o, zt[r][:, 0, s_], mb[r][:, 0, :], False, False)
                    mm(o, zt[r][:, 1, s_], mb[r][:, 1, :], False, True).then_inc(s_h, 1)

            def ranks(k):
                pe.wait_ge(s_oh, k + 1)
                if k == 1:
                    mm(Q0[:, CNT0:CNT0 + E], ones_bf[:, :], carry_bf[:, :])
                o = Q0[:, CUM0:CUM0 + TG * E]
                mm(o, tri[:, :], oh_all[:, k * TG:(k + 1) * TG, :].rearrange("p t e -> p (t e)"), True, False)
                mm(o.rearrange("p (t e) -> p t e", e=E), ones_bf[:, :], before[:, :, :].rearrange("p e t -> p t e"),
                   False, True).then_inc(s_rk, 1)

            transpose(0)
            queries_keys(0)
            key_features(0)
            transpose(1)
            key_values(0)
            for b in range(B):
                if b + 1 < B:
                    queries_keys(b + 1)
                products(b)
                if b + 1 < B:
                    key_features(b + 1)
                if b + 2 < B:
                    transpose(b + 2)
                expand(b)
                if b + 1 < B:
                    key_values(b + 1)
                if b == RANK_BATCH:
                    ranks(0)
                hidden(b)
            ranks(1)
            pe.wait_ge(s_ohhi, 1)
            pe.wait_ge(s_ohlo, POOL_TILES)
            pe.wait_ge(s_ohlo_v, TILES - POOL_TILES)
            for n in range(TILES):
                last = mm(Q0[:, 0:2 * NTILE], oh_lo[:, n, :], oh_hi[:, n, :, :].rearrange("p k s -> p (k s)"),
                          n == 0, n == TILES - 1)
            last.then_inc(s_inv, 1)

            def transpose_slots(r, b):
                pe.wait_ge(s_xn, 2 * b + 2)
                pe.wait_ge(s_xa, 2 * b + 2)
                for k in range(2):
                    for s_ in range(ST):
                        last = t_.transpose(PP[:, k * BLK + s_ * P:k * BLK + (s_ + 1) * P],
                                            xn[r][:, s_, k * P:(k + 1) * P], ident[:, :])
                last.then_inc(s_x, 1)

            def block(j, r, first=False, tail=False):
                b = 2 * j + r
                pe.wait_ge(s_xl, 2 * b + 2)
                pe.wait_ge(s_wh, 3 * b + 2)
                pe.wait_ge(s_wl, 2 * b + 2)
                for c in range(FC):
                    if c % 2 == 0 and not (first and r == 0):
                        pe.wait_ge(s_hl, 3 * b + c // 2 - 2)
                    o = UU[c // 2][:, (c % 2) * BLK:(c % 2 + 1) * BLK]
                    s1, s2 = slice(c * P, (c + 1) * P), slice(FF + c * P, FF + (c + 1) * P)
                    mm(o, wh[r][:, s1], xh[r][:, 0:BLK], True, False)
                    mm(o, wh[r][:, s1], xl[r][:, :], False, False)
                    mm(o, wl[r][:, s1], xh[r][:, 0:BLK], False, False)
                    mm(o, wh[r][:, s2], xh[r][:, BLK:2 * BLK], False, False)
                    last = mm(o, wl[r][:, s2], xh[r][:, BLK:2 * BLK], False, True)
                    if c % 2:
                        last.then_inc(s_u, 1)
                if not (tail and r == 1):
                    transpose_slots(1 - r, b + 1)
                pe.wait_ge(s_wh, 3 * b + 3)
                pe.wait_ge(s_wd, b + 1)
                if not first:
                    pe.wait_ge(s_yr, 2 * ST * b - 2 * ST)
                for s_ in range(ST):
                    o = YY[2 * r + s_][:, 0:2 * D].rearrange("p (k d) -> p k d", k=2)
                    t0 = slice(s_ * P, (s_ + 1) * P)
                    for c in range(FC):
                        if s_ == 0 and c % 2 == 0:
                            pe.wait_ge(s_hl, 3 * b + c // 2 + 1)
                        w_ = slice(2 * FF + c * D, 2 * FF + (c + 1) * D)
                        mm(o, hh[r][:, c, t0], whl[r][:, :, w_], c == 0, False)
                        last = mm(o[:, 0, :], hl[r][:, c, t0], wh[r][:, w_], False, c == FC - 1)
                    last.then_inc(s_y[s_], 1)

            pe.wait_ge(s_tab, 1)
            transpose_slots(0, 0)
            last_, two = last_blocks(pe)
            pairs(pe, block, last_, two)


_OUT = (B, NT * P, D)


def kernel(x, x_txt, L0_tok_curve, L0_tok_proj_w, L0_tok_proj_b, L0_txt_quantum_params, L0_txt_post_w,
           L0_txt_post_b, L0_attn_qkv_w, L0_attn_proj_w, L0_attn_proj_b, L0_ffn_router_w, L0_ffn_wi, L0_ffn_wo):
    import concourse.bacc as bacc
    from concourse.bass_utils import run_bass_kernel_spmd

    nc = bacc.Bacc("TRN2", target_bir_lowering=False, num_devices=1)
    x = np.asarray(x)
    layout = {
        "pixels": x.transpose(2, 3, 0, 1).reshape(IMG * IMG, B * CH),
        "curve": np.asarray(L0_tok_curve),
        "txt_ids": np.asarray(x_txt).T,
        "qparams": np.asarray(L0_txt_quantum_params).reshape(VOCAB, NPAR),
        "wf": np.concatenate([np.asarray(L0_tok_proj_w), np.asarray(L0_tok_proj_b)[:, None],
                              np.asarray(L0_txt_post_w), np.asarray(L0_txt_post_b)[:, None]], axis=1),
        "qkv_wT": np.asarray(L0_attn_qkv_w).T,
        "proj_w": np.asarray(L0_attn_proj_w),
        "proj_wT": np.asarray(L0_attn_proj_w).T,
        "proj_b": np.asarray(L0_attn_proj_b).reshape(2, G2).T,
        "router_w": np.asarray(L0_ffn_router_w),
        "wi": np.asarray(L0_ffn_wi),
        "wo": np.asarray(L0_ffn_wo),
    }
    arrays, args = {}, []
    for name, a in layout.items():
        a = np.ascontiguousarray(a)
        arrays[f"{name}_dram"] = a
        args.append(nc.dram_tensor(f"{name}_dram", a.shape, mybir.dt.from_np(a.dtype), kind="ExternalInput").ap())
    args.append(nc.dram_tensor("out_dram", _OUT, F32, kind="ExternalOutput").ap())
    fusion_kernel(nc, *args)
    r = run_bass_kernel_spmd(nc, [arrays], core_ids=[0])
    return r.results[0]["out_dram"]
```
